# Optimizing a Trainium2 kernel written in Bass

```python
import numpy as np
import jax
import jax.numpy as jnp

def _softmax(x, axis=-1):
    return jax.nn.softmax(x, axis=axis)

def _gelu(x):
    return jax.nn.gelu(x, approximate=True)

def _silu(x):
    return jax.nn.silu(x)

def _sigmoid(x):
    return jax.nn.sigmoid(x)

def _layernorm(x, axis=-1, eps=1e-05):
    m = jnp.mean(x, axis=axis, keepdims=True)
    v = jnp.var(x, axis=axis, keepdims=True)
    return (x - m) / jnp.sqrt(v + eps)

def _scatter_add(tgt, idx, src, axis=0):
    return tgt.at[idx].add(src)

def _segment_sum(src, seg, n):
    return jax.ops.segment_sum(src, seg, n)
kernel_name = 'mk_perceiver_d1_seqx_r4_68333a'

def setup_inputs(seed: int=0):
    np.random.seed(seed)
    _w = jnp.asarray

    def _rec_inputs():
        import jax
        import jax.numpy as jnp
        _rk = jax.random.key(seed)
        x = -0.0005207 + 1.001 * jax.random.normal(jax.random.fold_in(_rk, 1), (1, 256, 1024), jnp.float32)
        _lenS = 256 - jax.random.randint(jax.random.fold_in(_rk, 7), (1,), 0, max(1, 256 // 4) + 1, jnp.int32)
        _lenS2 = 4096 - jax.random.randint(jax.random.fold_in(_rk, 8), (1,), 0, max(1, 4096 // 4) + 1, jnp.int32)
        _ctx_4096P = jax.random.normal(jax.random.fold_in(_rk, 11), (1, 16, 1024), jnp.float32)
        _ctx_4096c = jax.random.dirichlet(jax.random.fold_in(_rk, 511), 0.3 * jnp.ones((16,), jnp.float32), (1, 4096))
        _ctx_4096t = jnp.einsum('bsk,bkd->bsd', _ctx_4096c, _ctx_4096P)
        _ctx_4096t = _ctx_4096t * jax.lax.rsqrt(jnp.mean(jnp.square(_ctx_4096t)) + 1e-12) * 0.953939
        ctx_4096 = -0.00010331 + 0.999899 * (_ctx_4096t + 0.3 * jax.random.normal(jax.random.fold_in(_rk, 611), (1, 4096, 1024), jnp.float32))
        return (x, ctx_4096)
    x, ctx_4096 = _rec_inputs()

    def _L0_xattn_setup():
        import jax, jax.numpy as jnp
        import numpy as np
        HEADS = 32
        KV_HEADS = 8
        HEAD_DIM = 128
        EPS = 1e-06

        def rms_norm(x, w):
            var = jnp.mean(jnp.square(x.astype(jnp.float32)), axis=-1, keepdims=True)
            return (x.astype(jnp.float32) * jax.lax.rsqrt(var + EPS)).astype(x.dtype) * w
        key = jax.random.key(seed)
        ks = jax.random.split(key, 6)
        bsz, n_lat, seq, hidden = (8, 64, 1024, 1024)
        return {'latents': jax.random.normal(ks[0], (bsz, n_lat, hidden), jnp.float32), 'context': jax.random.normal(ks[1], (bsz, seq, hidden), jnp.float32), 'Wq': jax.random.normal(ks[2], (hidden, HEADS * HEAD_DIM), jnp.float32) * 0.02, 'Wk': jax.random.normal(ks[3], (hidden, KV_HEADS * HEAD_DIM), jnp.float32) * 0.02, 'Wv': jax.random.normal(ks[4], (hidden, KV_HEADS * HEAD_DIM), jnp.float32) * 0.02, 'Wo': jax.random.normal(ks[5], (HEADS * HEAD_DIM, hidden), jnp.float32) * 0.02, 'q_norm_w': jnp.ones((HEAD_DIM,), jnp.float32), 'k_norm_w': jnp.ones((HEAD_DIM,), jnp.float32)}
    _L0_xattn_all = _L0_xattn_setup()
    _L0_xattn_in = {k: v for k, v in _L0_xattn_all.items() if k in ('Wq', 'Wk', 'Wv', 'Wo', 'q_norm_w', 'k_norm_w')}
    del _L0_xattn_all

    def _L0_attn_setup():
        import jax, jax.numpy as jnp
        import numpy as np
        DIM = 1024
        N_HEADS = 32
        N_KV_HEADS = 8
        HEAD_DIM = DIM // N_HEADS
        N_REP = N_HEADS // N_KV_HEADS
        THETA = 10000.0
        B, S = (4, 256)

        def _rope_cos_sin(seq_len):
            freqs = 1.0 / THETA ** (jnp.arange(0, HEAD_DIM, 2, dtype=jnp.float32) / HEAD_DIM)
            t = jnp.arange(seq_len, dtype=jnp.float32)
            ang = jnp.outer(t, freqs)
            return (jnp.cos(ang), jnp.sin(ang))

        def _apply_rope(x, cos, sin):
            xr = x[..., 0::2]
            xi = x[..., 1::2]
            c = cos[None, :, None, :]
            s = sin[None, :, None, :]
            out_r = xr * c - xi * s
            out_i = xr * s + xi * c
            return jnp.stack([out_r, out_i], axis=-1).reshape(x.shape)
        key = jax.random.key(seed)
        ks = jax.random.split(key, 5)
        sc = 1.0 / np.sqrt(DIM).astype(np.float32)
        x = jax.random.normal(ks[0], (B, S, DIM), jnp.float32)
        wq = jax.random.normal(ks[1], (DIM, N_HEADS * HEAD_DIM), jnp.float32) * sc
        wk = jax.random.normal(ks[2], (DIM, N_KV_HEADS * HEAD_DIM), jnp.float32) * sc
        wv = jax.random.normal(ks[3], (DIM, N_KV_HEADS * HEAD_DIM), jnp.float32) * sc
        wo = jax.random.normal(ks[4], (N_HEADS * HEAD_DIM, DIM), jnp.float32) * sc
        return {'x': x, 'wq': wq, 'wk': wk, 'wv': wv, 'wo': wo}
    _L0_attn_all = _L0_attn_setup()
    _L0_attn_in = {k: v for k, v in _L0_attn_all.items() if k in ('wq', 'wk', 'wv', 'wo')}
    del _L0_attn_all

    def _L0_ffn_setup():
        import jax, jax.numpy as jnp
        import numpy as np
        B, T, D_IN, D_OUT = (8, 512, 1024, 1024)
        N_LORAS, RANK = (16, 32)
        SCALING = 1.0
        key = jax.random.key(seed)
        ks = jax.random.split(key, 8)
        std = 1.0 / D_IN ** 0.5
        x = jax.random.normal(ks[0], (B, T, D_IN), dtype=jnp.float32)
        idx = jax.random.randint(ks[1], (B,), 0, N_LORAS)
        gate = jax.nn.one_hot(idx, N_LORAS, dtype=jnp.float32)
        kernel = jax.random.normal(ks[2], (D_IN, D_OUT), dtype=jnp.float32) * std
        bias = jnp.zeros((D_OUT,), dtype=jnp.float32)
        lora_A = jax.random.normal(ks[3], (N_LORAS, RANK, D_IN), dtype=jnp.float32) * std
        lora_B = jax.random.normal(ks[4], (N_LORAS, D_OUT, RANK), dtype=jnp.float32) * 0.01
        lora_A_shared = jax.random.normal(ks[5], (RANK, D_IN), dtype=jnp.float32) * std
        lora_B_shared = jax.random.normal(ks[6], (D_OUT, RANK), dtype=jnp.float32) * 0.01
        return {'x': x, 'gate': gate, 'kernel': kernel, 'bias': bias, 'lora_A': lora_A, 'lora_B': lora_B, 'lora_A_shared': lora_A_shared, 'lora_B_shared': lora_B_shared}
    _L0_ffn_all = _L0_ffn_setup()
    _L0_ffn_in = {k: v for k, v in _L0_ffn_all.items() if k in ('gate', 'kernel', 'bias', 'lora_A', 'lora_B', 'lora_A_shared', 'lora_B_shared')}
    del _L0_ffn_all
    return {'x': x, 'ctx_4096': ctx_4096, 'L0_xattn_Wq': _L0_xattn_in['Wq'], 'L0_xattn_Wk': _L0_xattn_in['Wk'], 'L0_xattn_Wv': _L0_xattn_in['Wv'], 'L0_xattn_Wo': _L0_xattn_in['Wo'], 'L0_xattn_q_norm_w': _L0_xattn_in['q_norm_w'], 'L0_xattn_k_norm_w': _L0_xattn_in['k_norm_w'], 'L0_attn_wq': _L0_attn_in['wq'], 'L0_attn_wk': _L0_attn_in['wk'], 'L0_attn_wv': _L0_attn_in['wv'], 'L0_attn_wo': _L0_attn_in['wo'], 'L0_ffn_gate': _L0_ffn_in['gate'], 'L0_ffn_kernel': _L0_ffn_in['kernel'], 'L0_ffn_bias': _L0_ffn_in['bias'], 'L0_ffn_lora_A': _L0_ffn_in['lora_A'], 'L0_ffn_lora_B': _L0_ffn_in['lora_B'], 'L0_ffn_lora_A_shared': _L0_ffn_in['lora_A_shared'], 'L0_ffn_lora_B_shared': _L0_ffn_in['lora_B_shared']}

def reference(x, ctx_4096, L0_xattn_Wq, L0_xattn_Wk, L0_xattn_Wv, L0_xattn_Wo, L0_xattn_q_norm_w, L0_xattn_k_norm_w, L0_attn_wq, L0_attn_wk, L0_attn_wv, L0_attn_wo, L0_ffn_gate, L0_ffn_kernel, L0_ffn_bias, L0_ffn_lora_A, L0_ffn_lora_B, L0_ffn_lora_A_shared, L0_ffn_lora_B_shared):
    import jax
    import jax.numpy as jnp

    def _L0_xattn_ref(latents, context, Wq, Wk, Wv, Wo, q_norm_w, k_norm_w):
        import jax, jax.numpy as jnp
        import numpy as np
        HEADS = 32
        KV_HEADS = 8
        HEAD_DIM = 128
        EPS = 1e-06

        def rms_norm(x, w):
            var = jnp.mean(jnp.square(x.astype(jnp.float32)), axis=-1, keepdims=True)
            return (x.astype(jnp.float32) * jax.lax.rsqrt(var + EPS)).astype(x.dtype) * w
        bsz, q_len, hidden = latents.shape
        kv = jnp.concatenate([context, latents], axis=1)
        kv_len = kv.shape[1]
        groups = HEADS // KV_HEADS
        q = (latents @ Wq).reshape(bsz, q_len, HEADS, HEAD_DIM).transpose(0, 2, 1, 3)
        k = (kv @ Wk).reshape(bsz, kv_len, KV_HEADS, HEAD_DIM).transpose(0, 2, 1, 3)
        v = (kv @ Wv).reshape(bsz, kv_len, KV_HEADS, HEAD_DIM).transpose(0, 2, 1, 3)
        q = rms_norm(q, q_norm_w)
        k = rms_norm(k, k_norm_w)
        qg = q.reshape(bsz, KV_HEADS, groups, q_len, HEAD_DIM)
        scale = 1.0 / np.sqrt(HEAD_DIM)
        scores = jnp.einsum('bhgqd,bhkd->bhgqk', qg, k) * scale
        probs = jax.nn.softmax(scores.astype(jnp.float32), axis=-1).astype(q.dtype)
        out = jnp.einsum('bhgqk,bhkd->bhgqd', probs, v)
        out = out.reshape(bsz, HEADS, q_len, HEAD_DIM).transpose(0, 2, 1, 3)
        out = out.reshape(bsz, q_len, HEADS * HEAD_DIM)
        return out @ Wo

    def _L0_attn_ref(x, wq, wk, wv, wo):
        import jax, jax.numpy as jnp
        import numpy as np
        DIM = 1024
        N_HEADS = 32
        N_KV_HEADS = 8
        HEAD_DIM = DIM // N_HEADS
        N_REP = N_HEADS // N_KV_HEADS
        THETA = 10000.0
        B, S = (4, 256)

        def _rope_cos_sin(seq_len):
            freqs = 1.0 / THETA ** (jnp.arange(0, HEAD_DIM, 2, dtype=jnp.float32) / HEAD_DIM)
            t = jnp.arange(seq_len, dtype=jnp.float32)
            ang = jnp.outer(t, freqs)
            return (jnp.cos(ang), jnp.sin(ang))

        def _apply_rope(x, cos, sin):
            xr = x[..., 0::2]
            xi = x[..., 1::2]
            c = cos[None, :, None, :]
            s = sin[None, :, None, :]
            out_r = xr * c - xi * s
            out_i = xr * s + xi * c
            return jnp.stack([out_r, out_i], axis=-1).reshape(x.shape)
        bsz, seq_len, _ = x.shape
        q = (x @ wq).reshape(bsz, seq_len, N_HEADS, HEAD_DIM)
        k = (x @ wk).reshape(bsz, seq_len, N_KV_HEADS, HEAD_DIM)
        v = (x @ wv).reshape(bsz, seq_len, N_KV_HEADS, HEAD_DIM)
        cos, sin = _rope_cos_sin(seq_len)
        q = _apply_rope(q, cos, sin)
        k = _apply_rope(k, cos, sin)
        k = jnp.repeat(k, N_REP, axis=2)
        v = jnp.repeat(v, N_REP, axis=2)
        scores = jnp.einsum('bqhd,bkhd->bhqk', q, k) / np.float32(np.sqrt(HEAD_DIM))
        mask = jnp.triu(jnp.full((seq_len, seq_len), -jnp.inf, dtype=scores.dtype), k=1)
        scores = scores + mask
        attn = jax.nn.softmax(scores.astype(jnp.float32), axis=-1).astype(q.dtype)
        out = jnp.einsum('bhqk,bkhd->bqhd', attn, v).reshape(bsz, seq_len, N_HEADS * HEAD_DIM)
        return out @ wo

    def _L0_ffn_ref(x, gate, kernel, bias, lora_A, lora_B, lora_A_shared, lora_B_shared):
        import jax, jax.numpy as jnp
        import numpy as np
        B, T, D_IN, D_OUT = (8, 512, 1024, 1024)
        N_LORAS, RANK = (16, 32)
        SCALING = 1.0
        base_out = jnp.matmul(x, kernel) + bias
        b = gate.shape[0]
        x_flat = x.reshape(b, -1, x.shape[-1])
        A_eff = jnp.einsum('bn,nri->bri', gate, lora_A)
        B_eff = jnp.einsum('bn,nor->bor', gate, lora_B)
        Ax = jnp.einsum('bri,bti->btr', A_eff, x_flat)
        delta_flat = jnp.einsum('bor,btr->bto', B_eff, Ax)
        Ax_s = jnp.einsum('ri,bti->btr', lora_A_shared, x_flat)
        delta_flat = delta_flat + jnp.einsum('or,btr->bto', lora_B_shared, Ax_s)
        delta = delta_flat.reshape(x.shape[:-1] + (kernel.shape[-1],))
        return base_out + (SCALING * delta).astype(base_out.dtype)
    x = x + _L0_xattn_ref(_layernorm(x, axis=-1), ctx_4096, L0_xattn_Wq, L0_xattn_Wk, L0_xattn_Wv, L0_xattn_Wo, L0_xattn_q_norm_w, L0_xattn_k_norm_w)
    x = x + _L0_attn_ref(_layernorm(x, axis=-1), L0_attn_wq, L0_attn_wk, L0_attn_wv, L0_attn_wo)
    x = x + _L0_ffn_ref(_layernorm(x, axis=-1), L0_ffn_gate, L0_ffn_kernel, L0_ffn_bias, L0_ffn_lora_A, L0_ffn_lora_B, L0_ffn_lora_A_shared, L0_ffn_lora_B_shared)
    return x

_drawn_inputs = setup_inputs


def setup_inputs(seed=0):
    import zlib

    import numpy as np

    out = dict(_drawn_inputs(seed))
    spreads = {'L0_xattn_q_norm_w': (1.0, 0.6),
     'L0_xattn_k_norm_w': (1.0, 0.6),
     'L0_ffn_bias': (0.0, 0.1)}
    factors = {}
    for name, (base, spread) in spreads.items():
        noise = np.random.default_rng([zlib.crc32(name.encode()), seed]).standard_normal(out[name].shape)
        drawn = base * np.exp(spread * noise) if base else spread * noise
        out[name] = jnp.asarray(drawn.astype(out[name].dtype))
    for name, factor in factors.items():
        out[name] = (out[name] * factor).astype(out[name].dtype)
    return out
```

```python
from contextlib import ExitStack

import numpy as np

import concourse.bass as bass
from concourse import mybir

F32 = mybir.dt.float32
F32R = mybir.dt.float32r
ALU = mybir.AluOpType
ACT = mybir.ActivationFunctionType
AX = mybir.AxisListType

P = 128
BANK = 512
ROWS = 256
ROW_TILES = ROWS // P
HID = 1024
HID_TILES = HID // P
CTX = 4096
CTX_TILES = CTX // P
KEYS = CTX + ROWS
KEY_TILES = KEYS // P
HEADS = 32
KV_HEADS = 8
GROUP = HEADS // KV_HEADS
DIM = 128
LN_EPS = 1e-5
RMS_EPS = 1e-6
SELF_DIM = HID // HEADS
LORAS = 16
RANK = 32
LORA_BATCH = 8
ROWS_PER_GATE = ROWS // LORA_BATCH
NEGATIVE = -1e30

PASSES = ((0, 0), (0, 1), (1, 0))


def wait(engine, semaphore, value):
    if not isinstance(value, int) or value > 0:
        engine.wait_ge(semaphore, value)


def over_last(ap, shape):
    return ap.unsqueeze(len(shape) - 1).broadcast_to(list(shape))


class Core:

    def __init__(self, nc, stack):
        self.nc, self.stack = nc, stack
        self.psum = stack.enter_context(nc.psum_tensor("psum", [P, 8, BANK], F32))
        self.ident = self.sbuf("ident", [P, P])
        self.ones = self.sbuf("ones", [P, P])
        self.minus_half = self.sbuf("minus_half", [P, KV_HEADS])
        self.x = self.sbuf("x_rows", [P, ROW_TILES, HID])

    def sbuf(self, name, shape, dtype=F32, stack=None):
        return (stack or self.stack).enter_context(self.nc.sbuf_tensor(name, shape, dtype))

    def sem(self, name):
        return self.stack.enter_context(self.nc.semaphore(name))


def layer_norm_vector(eng, core, rows, normed, stats, mv, done, to_pool, from_pool):
    for t in range(ROW_TILES):
        for half in range(2):
            eng.bn_stats(stats[:, t, half, :], rows[:, t, half * BANK:(half + 1) * BANK]).then_inc(done, 1)
    eng.wait_ge(done, 4)
    for t in range(ROW_TILES):
        eng.bn_aggr(mv[:, t, 0:2], stats[:, t, :, :]).then_inc(done, 1)
    eng.wait_ge(done, 6)
    eng.tensor_scalar(mv[:, :, 2], mv[:, :, 1], LN_EPS, None, ALU.add).then_inc(to_pool, 1)
    eng.wait_ge(from_pool, 1)
    for t in range(ROW_TILES):
        eng.tensor_scalar(normed[:, t, :], rows[:, t, :], mv[:, t, 0:1], mv[:, t, 3:4],
                          ALU.subtract, ALU.mult).then_inc(done, 1)


def layer_norm_pool(eng, core, mv, to_pool, from_pool):
    eng.wait_ge(to_pool, 1)
    eng.tensor_tensor(mv[:, :, 3], mv[:, :, 2], core.minus_half[:, 0:ROW_TILES], ALU.pow).then_inc(from_pool, 1)


def project_queries(core, a, xnT, q_scratch):
    nc, ps = core.nc, core.psum
    CHUNK = BANK
    with ExitStack() as own:
        normed = core.sbuf("xn_rows", [P, ROW_TILES, HID], stack=own)
        stats = core.sbuf("q_ln_stats", [P, ROW_TILES, 2, 6], stack=own)
        mv = core.sbuf("q_ln_mv", [P, ROW_TILES, 4], stack=own)
        w_raw = core.sbuf("wq_raw", [P, 2, HID_TILES, CHUNK], stack=own)
        w_part = [core.sbuf(f"wq_part{n}", [P, 2, HID_TILES, CHUNK], F32R, stack=own) for n in range(2)]
        square = core.sbuf("q_square", [P, ROW_TILES, CHUNK], stack=own)
        sums = core.sbuf("q_sums", [P, ROW_TILES, GROUP], stack=own)
        scale_in = core.sbuf("q_mean_square", [P, ROW_TILES, GROUP], stack=own)
        scale = core.sbuf("q_rms_scale", [P, ROW_TILES, GROUP], stack=own)
        q_rows = core.sbuf("q_rows", [P, ROW_TILES, CHUNK], stack=own)
        q_part = [core.sbuf(f"q_part{n}", [P, 2, GROUP, ROWS], F32R, stack=own) for n in range(2)]
        weights = core.sbuf("norm_weights", [P, 4], stack=own)

        s_const = core.sem("q_const_loaded")
        s_x = core.sem("q_x_loaded")
        s_fill = core.sem("q_constants_set")
        s_ln = core.sem("q_ln_steps")
        s_var = core.sem("q_var_ready")
        s_rstd = core.sem("q_rstd_ready")
        s_xt = core.sem("q_xn_transposed")
        s_xhi = core.sem("q_xn_hi")
        s_xlo = core.sem("q_xn_lo")
        s_nw = core.sem("q_norm_weights")
        s_w = [core.sem(f"q_w_loaded{n}") for n in range(2)]
        s_whi = core.sem("q_w_hi")
        s_wlo = core.sem("q_w_lo")
        s_mm = core.sem("q_products")
        s_sq = core.sem("q_squared")
        s_sum = core.sem("q_summed")
        s_ms = core.sem("q_mean_square_ready")
        s_rms = core.sem("q_rms_ready")
        s_rows = core.sem("q_rows_ready")
        s_t = core.sem("q_transposed")
        s_qhi = core.sem("q_hi")
        s_qlo = core.sem("q_lo")
        s_st = [core.sem(f"q_stored{n}") for n in range(2)]

        wq = a["Wq"].rearrange("(k p) n -> p k n", p=P)

        def pairs(eng, step):
            step(0, 0)
            step(0, 1)
            with eng.Fori(1, KV_HEADS // 2) as i:
                step(i, 0)
                step(i, 1)

        with nc.Block() as block:
            @block.sync
            def _(eng):
                eng.dma_start(core.x[:, :, :], a["x"].rearrange("b (t p) n -> p (b t) n", p=P)).then_inc(s_x, 16)
                eng.dma_start(core.ident[:, :], a["ident"]).then_inc(s_const, 16)
                eng.dma_start(weights[:, 0:1], a["q_norm_w"].rearrange("(p o) -> p o", o=1)).then_inc(s_const, 16)
                eng.dma_start(weights[:, 1:2], a["k_norm_w"].rearrange("(p o) -> p o", o=1)).then_inc(s_const, 16)

                def load(i, par):
                    c = 2 * i + par
                    wait(eng, s_whi, c - 1)
                    wait(eng, s_wlo, c - 1)
                    eng.dma_start(w_raw[:, par, :, :], wq[:, :, bass.ds(c * CHUNK, CHUNK)]).then_inc(s_w[par], 16)

                def store(i, par):
                    wait(eng, s_qlo, 2 * i + par + 1)
                    for n in range(2):
                        eng.dma_start(q_scratch[bass.ds(2 * i + par, 1), :, n, :, :].rearrange("o p g r -> (o p) g r"),
                                      q_part[n][:, par, :, :].bitcast(F32)).then_inc(s_st[par], 16)

                load(0, 0)
                load(0, 1)
                load(1, 0)
                load(1, 1)
                with eng.Fori(2, KV_HEADS // 2) as i:
                    store(i - 2, 0)
                    load(i, 0)
                    store(i - 2, 1)
                    load(i, 1)
                for i in (KV_HEADS // 2 - 2, KV_HEADS // 2 - 1):
                    store(i, 0)
                    store(i, 1)

            @block.gpsimd
            def _(eng):
                eng.memset(core.ones[:, :], 1.0).then_inc(s_fill, 1)
                eng.memset(core.minus_half[:, :], -0.5).then_inc(s_fill, 1)
                eng.wait_ge(s_fill, 2)
                layer_norm_pool(eng, core, mv, s_var, s_rstd)

                def step(i, par):
                    c = 2 * i + par
                    wait(eng, s_ms, c + 1)
                    eng.tensor_tensor(scale[:, :, :], scale_in[:, :, :],
                                      core.minus_half[:, :].rearrange("p (t g) -> p t g", g=GROUP),
                                      ALU.pow).then_inc(s_rms, 1)
                pairs(eng, step)
                eng.wait_ge(s_st[0], 16 * KV_HEADS)
                eng.wait_ge(s_st[1], 16 * KV_HEADS)

            @block.tensor
            def _(eng):
                eng.wait_ge(s_const, 48)
                eng.wait_ge(s_ln, 8)
                for t in range(ROW_TILES):
                    for k in range(HID_TILES):
                        mm = eng.transpose(ps[:, 2 * t + k // 4, (k % 4) * P:(k % 4 + 1) * P],
                                           normed[:, t, k * P:(k + 1) * P], core.ident[:, :])
                    mm.then_inc(s_xt, 1)

                def transposes(i, par):
                    c = 2 * i + par
                    wait(eng, s_rows, c + 1)
                    wait(eng, s_qlo, c)
                    for t in range(ROW_TILES):
                        for g in range(GROUP):
                            mm = eng.transpose(ps[:, 4 + t, g * P:(g + 1) * P],
                                               q_rows[:, t, g * P:(g + 1) * P], core.ident[:, :])
                    mm.then_inc(s_t, 1)

                def products(i, par):
                    c = 2 * i + par
                    wait(eng, s_wlo, c + 1)
                    wait(eng, s_rows, c - 1)
                    for t in range(ROW_TILES):
                        for k in range(HID_TILES):
                            for n, (s, m) in enumerate(PASSES):
                                mm = eng.matmul(ps[:, 2 * par + t, :], xnT[s][:, k, t * P:(t + 1) * P],
                                                w_part[m][:, par, k, :],
                                                start=(k == 0 and n == 0), stop=(k == HID_TILES - 1 and n == 2))
                    mm.then_inc(s_mm, 1)

                eng.wait_ge(s_xlo, ROW_TILES)
                products(0, 0)
                products(0, 1)
                transposes(0, 0)
                with eng.Fori(1, KV_HEADS // 2) as i:
                    products(i, 0)
                    transposes(i - 1, 1)
                    products(i, 1)
                    transposes(i, 0)
                transposes(KV_HEADS // 2 - 1, 1)

            @block.scalar
            def _(eng):
                for t in range(ROW_TILES):
                    eng.wait_ge(s_xt, t + 1)
                    eng.activation(xnT[0][:, :, t * P:(t + 1) * P],
                                   ps[:, 2 * t:2 * t + 2, :].rearrange("p b (k n) -> p (b k) n", n=P),
                                   ACT.Copy).then_inc(s_xhi, 1)

                def split(i, par):
                    c = 2 * i + par
                    wait(eng, s_w[par], 16 * (i + 1))
                    wait(eng, s_mm, c - 1)
                    eng.activation(w_part[0][:, par, :, :], w_raw[:, par, :, :], ACT.Copy).then_inc(s_whi, 1)

                def squares(i, par):
                    c = 2 * i + par
                    wait(eng, s_mm, c + 1)
                    wait(eng, s_sum, c)
                    eng.activation(square[:, :, :], ps[:, 2 * par:2 * par + 2, :], ACT.Square).then_inc(s_sq, 1)

                def part(i, par):
                    c = 2 * i + par
                    wait(eng, s_t, c + 1)
                    wait(eng, s_st[par], 32 * i)
                    eng.activation(q_part[0][:, par, :, :].rearrange("p g (t n) -> p t g n", n=P),
                                   ps[:, 4:6, :].rearrange("p t (g n) -> p t g n", n=P),
                                   ACT.Identity, scale=weights[:, 3:4]).then_inc(s_qhi, 1)

                eng.wait_ge(s_nw, 2)
                split(0, 0)
                split(0, 1)
                squares(0, 0)
                with eng.Fori(1, KV_HEADS // 2) as i:
                    split(i, 0)
                    squares(i - 1, 1)
                    part(i - 1, 0)
                    split(i, 1)
                    squares(i, 0)
                    part(i - 1, 1)
                squares(KV_HEADS // 2 - 1, 1)
                part(KV_HEADS // 2 - 1, 0)
                part(KV_HEADS // 2 - 1, 1)

            @block.vector
            def _(eng):
                eng.wait_ge(s_const, 48)
                eng.tensor_tensor(weights[:, 2:3], weights[:, 0:1], weights[:, 1:2], ALU.mult).then_inc(s_nw, 1)
                eng.wait_ge(s_nw, 1)
                eng.tensor_scalar(weights[:, 3:4], weights[:, 2:3], float(1.0 / np.sqrt(DIM)), None,
                                  ALU.mult).then_inc(s_nw, 1)
                eng.wait_ge(s_x, 16)
                layer_norm_vector(eng, core, core.x, normed, stats, mv, s_ln, s_var, s_rstd)
                for t in range(ROW_TILES):
                    eng.wait_ge(s_xhi, t + 1)
                    eng.tensor_tensor(xnT[1][:, :, t * P:(t + 1) * P],
                                      ps[:, 2 * t:2 * t + 2, :].rearrange("p b (k n) -> p (b k) n", n=P),
                                      xnT[0][:, :, t * P:(t + 1) * P].bitcast(F32), ALU.subtract).then_inc(s_xlo, 1)

                def split(i, par):
                    c = 2 * i + par
                    wait(eng, s_whi, c + 1)
                    eng.tensor_tensor(w_part[1][:, par, :, :], w_raw[:, par, :, :],
                                      w_part[0][:, par, :, :].bitcast(F32), ALU.subtract).then_inc(s_wlo, 1)

                def norm(i, par):
                    c = 2 * i + par
                    wait(eng, s_sq, c + 1)
                    eng.tensor_reduce(sums[:, :, :], square[:, :, :].rearrange("p t (g n) -> p t g n", n=DIM),
                                      AX.X, ALU.add).then_inc(s_sum, 1)
                    wait(eng, s_sum, c + 1)
                    wait(eng, s_rms, c)
                    eng.tensor_scalar(scale_in[:, :, :], sums[:, :, :], 1.0 / DIM, RMS_EPS,
                                      ALU.mult, ALU.add).then_inc(s_ms, 1)
                    wait(eng, s_rms, c + 1)
                    wait(eng, s_t, c)
                    for t in range(ROW_TILES):
                        ins = eng.tensor_tensor(q_rows[:, t, :].rearrange("p (g n) -> p g n", n=DIM),
                                                ps[:, 2 * par + t, :].rearrange("p (g n) -> p g n", n=DIM),
                                                over_last(scale[:, t, :], (P, GROUP, DIM)), ALU.mult)
                    ins.then_inc(s_rows, 1)

                def part(i, par):
                    c = 2 * i + par
                    wait(eng, s_qhi, c + 1)
                    for t in range(ROW_TILES):
                        ins = eng.scalar_tensor_tensor(
                            out=q_part[1][:, par, :, t * P:(t + 1) * P],
                            in0=ps[:, 4 + t, :].rearrange("p (g n) -> p g n", n=P), scalar=weights[:, 3:4],
                            in1=q_part[0][:, par, :, t * P:(t + 1) * P].bitcast(F32),
                            op0=ALU.mult, op1=ALU.subtract)
                    ins.then_inc(s_qlo, 1)

                eng.wait_ge(s_nw, 2)
                split(0, 0)
                split(0, 1)
                norm(0, 0)
                with eng.Fori(1, KV_HEADS // 2) as i:
                    split(i, 0)
                    norm(i - 1, 1)
                    part(i - 1, 0)
                    split(i, 1)
                    norm(i, 0)
                    part(i - 1, 1)
                norm(KV_HEADS // 2 - 1, 1)
                part(KV_HEADS // 2 - 1, 0)
                part(KV_HEADS // 2 - 1, 1)


def project_keys_values(core, a, xnT, k_scratch, v_scratch):
    nc, ps = core.nc, core.psum
    KV = KV_HEADS * DIM
    T_BANK, K_BANK, V_BANK = 0, 2, 4
    with ExitStack() as own:
        w_part = [core.sbuf(f"wkv_part{n}", [P, HID_TILES, 2 * KV], F32R, stack=own) for n in range(2)]
        w_raw = core.sbuf("wkv_raw", [P, 2, KV], stack=own)
        rows = core.sbuf("ctx_rows", [P, 2, HID], stack=own)
        rowsT = [core.sbuf(f"ctxT_part{n}", [P, 2, HID_TILES, P], F32R, stack=own) for n in range(2)]
        square = core.sbuf("k_square", [P, KV], stack=own)
        small = core.sbuf("k_small", [P, 3, KV_HEADS], stack=own)
        k_out = core.sbuf("k_out", [P, 2, KV], stack=own)
        v_out = core.sbuf("v_out", [P, 2, KV], stack=own)

        s_w = [core.sem(f"kv_w_loaded{n}") for n in range(2)]
        s_whi = core.sem("kv_w_hi")
        s_wlo = core.sem("kv_w_lo")
        s_rows = [core.sem(f"kv_rows_loaded{n}") for n in range(2)]
        s_t = core.sem("kv_transposed")
        s_hi = core.sem("kv_hi")
        s_lo = core.sem("kv_lo")
        s_k = core.sem("kv_k_product")
        s_v = core.sem("kv_v_product")
        s_sq = core.sem("kv_squared")
        s_sum = core.sem("kv_summed")
        s_ms = core.sem("kv_mean_square")
        s_rms = core.sem("kv_rms_scale")
        s_krow = core.sem("kv_k_rows")
        s_vrow = core.sem("kv_v_rows")
        s_kst = [core.sem(f"kv_k_stored{n}") for n in range(2)]
        s_vst = [core.sem(f"kv_v_stored{n}") for n in range(2)]

        LAST = CTX_TILES // 2 - 1
        LATENT = KEY_TILES // 2 - 1

        with nc.Block() as block:
            @block.sync
            def _(eng):
                ctx = a["ctx"].rearrange("b (t p) n -> p (b t) n", p=P)

                def load(i, par):
                    wait(eng, s_t, 2 * i + par - 1)
                    eng.dma_start(rows[:, par, :], ctx[:, bass.ds(2 * i + par, 1), :].rearrange("p o n -> p (o n)")).then_inc(s_rows[par], 16)

                def load_weights(n):
                    wait(eng, s_wlo, n - 1)
                    w = a["Wk"] if n < HID_TILES else a["Wv"]
                    k = n % HID_TILES
                    eng.dma_start(w_raw[:, n % 2, :], w[k * P:(k + 1) * P, :]).then_inc(s_w[n % 2], 16)

                def store(i, par):
                    t = 2 * i + par
                    for done, out, scratch, stored in ((s_krow, k_out, k_scratch, s_kst), (s_vrow, v_out, v_scratch, s_vst)):
                        wait(eng, done, t + 1)
                        eng.dma_start(scratch[:, :, bass.ds(t, 1), :].rearrange("h p o d -> p (h o) d"),
                                      out[:, par, :].rearrange("p (h d) -> p h d", d=DIM)).then_inc(stored[par], 16)

                load(0, 0)
                for n in range(HID_TILES):
                    load_weights(n)
                load(0, 1)
                for n in range(HID_TILES, 2 * HID_TILES):
                    load_weights(n)
                with eng.Fori(0, LAST) as i:
                    load(i + 1, 0)
                    store(i, 0)
                    load(i + 1, 1)
                    store(i, 1)
                for i in (LAST, LATENT):
                    store(i, 0)
                    store(i, 1)
                for par in range(2):
                    eng.wait_ge(s_kst[par], 16 * KEY_TILES // 2)
                    eng.wait_ge(s_vst[par], 16 * KEY_TILES // 2)

            @block.gpsimd
            def _(eng):
                with eng.Fori(0, KEY_TILES) as t:
                    eng.wait_ge(s_ms, t + 1)
                    eng.tensor_tensor(small[:, 2, :], small[:, 1, :], core.minus_half[:, :], ALU.pow).then_inc(s_rms, 1)

            @block.tensor
            def _(eng):
                def transposes(i, par):
                    t = 2 * i + par
                    wait(eng, s_rows[par], 16 * (i + 1))
                    wait(eng, s_lo, t)
                    for k in range(HID_TILES):
                        mm = eng.transpose(ps[:, T_BANK + k // 4, (k % 4) * P:(k % 4 + 1) * P],
                                           rows[:, par, k * P:(k + 1) * P], core.ident[:, :])
                    mm.then_inc(s_t, 1)

                def product(bank, at, left, ready):
                    for k in range(HID_TILES):
                        if ready is not None:
                            eng.wait_ge(s_wlo, ready + k + 1)
                        for n, (s, m) in enumerate(PASSES):
                            for half in range(2):
                                col = at + half * BANK
                                mm = eng.matmul(ps[:, bank + half, :], left(s, k), w_part[m][:, k, col:col + BANK],
                                                start=(k == 0 and n == 0), stop=(k == HID_TILES - 1 and n == 2))
                    return mm

                def products(i, par, latent=False, first=False):
                    t = 2 * i + par
                    if latent:
                        def left(s, k):
                            return xnT[s][:, k, par * P:(par + 1) * P]
                    else:
                        wait(eng, s_lo, t + 1)
                        def left(s, k):
                            return rowsT[s][:, par, k, :]
                    wait(eng, s_krow, t)
                    product(K_BANK, 0, left, 0 if first else None).then_inc(s_k, 1)
                    wait(eng, s_vrow, t)
                    product(V_BANK, KV, left, HID_TILES if first else None).then_inc(s_v, 1)

                transposes(0, 0)
                transposes(0, 1)
                products(0, 0, first=True)
                transposes(1, 0)
                products(0, 1)
                with eng.Fori(1, LAST) as i:
                    transposes(i, 1)
                    products(i, 0)
                    transposes(i + 1, 0)
                    products(i, 1)
                transposes(LAST, 1)
                products(LAST, 0)
                products(LAST, 1)
                products(LATENT, 0, latent=True)
                products(LATENT, 1, latent=True)

            @block.scalar
            def _(eng):
                def split_weights(n):
                    eng.wait_ge(s_w[n % 2], 16 * (n // 2 + 1))
                    eng.activation(w_part[0][:, n % HID_TILES, (n // HID_TILES) * KV:(n // HID_TILES + 1) * KV],
                                   w_raw[:, n % 2, :], ACT.Copy).then_inc(s_whi, 1)

                def high(i, par):
                    t = 2 * i + par
                    wait(eng, s_t, t + 1)
                    wait(eng, s_v, t - 1)
                    eng.activation(rowsT[0][:, par, :, :],
                                   ps[:, T_BANK:T_BANK + 2, :].rearrange("p b (k n) -> p (b k) n", n=P),
                                   ACT.Copy).then_inc(s_hi, 1)

                def drain(i, par):
                    t = 2 * i + par
                    wait(eng, s_k, t + 1)
                    wait(eng, s_sum, t)
                    eng.activation(square[:, :].rearrange("p (b n) -> p b n", n=BANK), ps[:, K_BANK:K_BANK + 2, :],
                                   ACT.Square).then_inc(s_sq, 1)
                    wait(eng, s_v, t + 1)
                    wait(eng, s_vst[par], 16 * i)
                    eng.activation(v_out[:, par, :].rearrange("p (b n) -> p b n", n=BANK), ps[:, V_BANK:V_BANK + 2, :],
                                   ACT.Copy).then_inc(s_vrow, 1)

                high(0, 0)
                for n in range(HID_TILES):
                    split_weights(n)
                high(0, 1)
                for n in range(HID_TILES, 2 * HID_TILES):
                    split_weights(n)
                with eng.Fori(0, LAST) as i:
                    drain(i, 0)
                    high(i + 1, 0)
                    drain(i, 1)
                    high(i + 1, 1)
                for i in (LAST, LATENT):
                    drain(i, 0)
                    drain(i, 1)

            @block.vector
            def _(eng):
                def split_weights(n):
                    eng.wait_ge(s_whi, n + 1)
                    at = w_part[0][:, n % HID_TILES, (n // HID_TILES) * KV:(n // HID_TILES + 1) * KV]
                    eng.tensor_tensor(w_part[1][:, n % HID_TILES, (n // HID_TILES) * KV:(n // HID_TILES + 1) * KV],
                                      w_raw[:, n % 2, :], at.bitcast(F32), ALU.subtract).then_inc(s_wlo, 1)

                def low(i, par):
                    wait(eng, s_hi, 2 * i + par + 1)
                    eng.tensor_tensor(rowsT[1][:, par, :, :],
                                      ps[:, T_BANK:T_BANK + 2, :].rearrange("p b (k n) -> p (b k) n", n=P),
                                      rowsT[0][:, par, :, :].bitcast(F32), ALU.subtract).then_inc(s_lo, 1)

                def norm(i, par):
                    t = 2 * i + par
                    wait(eng, s_sq, t + 1)
                    eng.tensor_reduce(small[:, 0, :], square[:, :].rearrange("p (h d) -> p h d", d=DIM),
                                      AX.X, ALU.add).then_inc(s_sum, 1)
                    wait(eng, s_sum, t + 1)
                    eng.tensor_scalar(small[:, 1, :], small[:, 0, :], 1.0 / DIM, RMS_EPS,
                                      ALU.mult, ALU.add).then_inc(s_ms, 1)
                    wait(eng, s_rms, t + 1)
                    wait(eng, s_kst[par], 16 * i)
                    eng.tensor_tensor(k_out[:, par, :].rearrange("p (h d) -> p h d", d=DIM),
                                      ps[:, K_BANK:K_BANK + 2, :].rearrange("p b (h d) -> p (b h) d", d=DIM),
                                      over_last(small[:, 2, :], (P, KV_HEADS, DIM)), ALU.mult).then_inc(s_krow, 1)

                low(0, 0)
                for n in range(HID_TILES):
                    split_weights(n)
                low(0, 1)
                for n in range(HID_TILES, 2 * HID_TILES):
                    split_weights(n)
                with eng.Fori(0, LAST) as i:
                    norm(i, 0)
                    low(i + 1, 0)
                    norm(i, 1)
                    low(i + 1, 1)
                for i in (LAST, LATENT):
                    norm(i, 0)
                    norm(i, 1)


def cross_attention(core, q_scratch, k_scratch, v_scratch, o_scratch):
    nc, ps = core.nc, core.psum
    STEPS = KEY_TILES // 2
    CHUNKS = -(-KEYS // BANK)
    UNITS = 2 * CHUNKS
    S_BANK, T_BANK, O_BANK, AUX = 0, 3, 5, 7
    QK_AT = [(2 * s, 2 * s + 1) if s < 4 else (s + 4,) if s < 12 else (16, 17) if s == 12 else () for s in range(STEPS)]
    TURN_AT = {1: 0, 2: 1, 3: 2, 4: 3, 6: 4, 8: 5, 10: 6, 12: 7, 13: 8}
    EARLY_EXP = {13: (0, 1), 14: (2,), 15: (3,), 16: (4,)}
    LATE_EXP = {s: (s + 5,) for s in range(UNITS - 5)}
    SUM_AT, SPREAD_AT = 13, 15

    def cols(n):
        at = n // 2 * BANK
        return at, min(BANK, KEYS - at)

    with ExitStack() as own:
        scores = core.sbuf("scores", [P, 2, ROW_TILES, KEYS], stack=own)
        keysT = [core.sbuf(f"keysT_part{n}", [P, KEYS], F32R, stack=own) for n in range(2)]
        values = [core.sbuf(f"values_part{n}", [P, KEY_TILES, DIM], F32R, stack=own) for n in range(2)]
        k_raw = core.sbuf("k_raw", [P, KEY_TILES, DIM], stack=own)
        v_raw = core.sbuf("v_raw", [P, KEY_TILES, DIM], stack=own)
        queries = core.sbuf("queries", [P, GROUP, 2, ROWS], F32R, stack=own)
        probsT = [core.sbuf(f"probsT_part{n}", [P, 2, 2, ROWS], F32R, stack=own) for n in range(2)]
        o_full = core.sbuf("o_full", [P, 2, ROWS], stack=own)
        o_part = core.sbuf("o_part", [P, 2, 2, ROWS], F32R, stack=own)
        spread = core.sbuf("inverse_sums_spread", [P, ROWS], stack=own)
        diag = core.sbuf("inverse_sums_diagonal", [P, ROW_TILES, P], stack=own)
        unit_max = core.sbuf("unit_max", [P, 2, ROW_TILES, CHUNKS], stack=own)
        minus_max = core.sbuf("minus_max", [P, 2, ROW_TILES], stack=own)
        unit_sum = core.sbuf("unit_sum", [P, 2, ROW_TILES, CHUNKS], stack=own)
        row_sum = core.sbuf("row_sum", [P, 2, ROW_TILES], stack=own)

        s_kraw = core.sem("x_k_loaded")
        s_vraw = core.sem("x_v_loaded")
        s_q = [core.sem(f"x_q_loaded{m}") for m in range(GROUP)]
        s_turn = core.sem("x_keys_turned")
        s_khi = core.sem("x_keys_hi")
        s_klo = core.sem("x_keys_lo")
        s_vhi = core.sem("x_values_hi")
        s_vlo = core.sem("x_values_lo")
        s_qk = core.sem("x_unit_products")
        s_se = core.sem("x_unit_drained")
        s_max = core.sem("x_max")
        s_exp = core.sem("x_exp")
        s_pt = core.sem("x_probs_turned")
        s_phi = core.sem("x_probs_hi")
        s_plo = core.sem("x_probs_lo")
        s_pv = core.sem("x_pv")
        s_sum = core.sem("x_row_sums")
        s_inv = core.sem("x_inverse_sums")
        s_diag = core.sem("x_diagonal")
        s_bc = core.sem("x_spread_product")
        s_spread = core.sem("x_spread")
        s_on = core.sem("x_o_normed")
        s_ohi = core.sem("x_o_hi")
        s_olo = core.sem("x_o_lo")
        s_ost = [core.sem(f"x_o_stored{n}") for n in range(2)]

        def heads(eng, body):
            body(0)
            with eng.Fori(1, KV_HEADS - 1) as j:
                body(j)
            body(KV_HEADS - 1)

        def final(j):
            return isinstance(j, int) and j == KV_HEADS - 1

        with nc.Block() as block:
            @block.sync
            def _(eng):
                def load_k(j):
                    wait(eng, s_turn, CHUNKS * j)
                    eng.dma_start(k_raw[:, :, :], k_scratch[bass.ds(j, 1), :, :, :].rearrange("o p t d -> (o p) t d")).then_inc(s_kraw, 16)

                def load_v(j):
                    wait(eng, s_vlo, STEPS * j)
                    eng.dma_start(v_raw[:, :, :], v_scratch[bass.ds(j, 1), :, :, :].rearrange("o p t d -> (o p) t d")).then_inc(s_vraw, 16)

                def load_q(j, m):
                    wait(eng, s_qk, UNITS * (4 * j + m - 3))
                    eng.dma_start(queries[:, m, :, :].bitcast(F32),
                                  q_scratch[bass.ds(j, 1), :, :, m, :].rearrange("o p n r -> (o p) n r")).then_inc(s_q[m], 16)

                def store(j, m):
                    eng.wait_ge(s_olo, 4 * j + m + 1)
                    eng.dma_start(o_scratch[:, bass.ds(4 * j + m, 1), :, :].rearrange("p o n r -> p (o n) r"),
                                  o_part[:, m % 2, :, :].bitcast(F32)).then_inc(s_ost[m % 2], 16)

                load_k(0)
                for m in range(GROUP):
                    load_q(0, m)
                load_v(0)

                def body(j):
                    if not final(j):
                        load_k(j + 1)
                        load_q(j + 1, 0)
                        load_v(j + 1)
                    for m in range(GROUP):
                        if m > 0:
                            if not final(j):
                                load_q(j + 1, m)
                            store(j, m - 1)
                    store(j, GROUP - 1)
                heads(eng, body)
                for par in range(2):
                    eng.wait_ge(s_ost[par], 16 * HEADS // 2)

            @block.gpsimd
            def _(eng):
                ones = core.ones[:, :].unsqueeze(1).broadcast_to([P, 2, P])

                def split_values(j, p):
                    at = slice(2 * p, 2 * p + 2)
                    wait(eng, s_pv, STEPS * (4 * j - 1) + p + 1)
                    if p == 0:
                        wait(eng, s_vraw, 16 * (j + 1))
                    eng.tensor_tensor(values[0][:, at, :], v_raw[:, at, :], ones, ALU.mult).then_inc(s_vhi, 1)
                    eng.wait_ge(s_vhi, STEPS * j + p + 1)
                    eng.tensor_tensor(values[1][:, at, :], v_raw[:, at, :], values[0][:, at, :].bitcast(F32),
                                      ALU.subtract).then_inc(s_vlo, 1)

                def split_output(j, m):
                    G = 4 * j + m
                    eng.wait_ge(s_on, G + 1)
                    wait(eng, s_ost[m % 2], 16 * (2 * j + m // 2))
                    eng.tensor_tensor(o_part[:, m % 2, 0, :].rearrange("p (t n) -> p t n", n=P),
                                      o_full[:, m % 2, :].rearrange("p (t n) -> p t n", n=P), ones, ALU.mult).then_inc(s_ohi, 1)
                    eng.wait_ge(s_ohi, G + 1)
                    eng.tensor_tensor(o_part[:, m % 2, 1, :], o_full[:, m % 2, :],
                                      o_part[:, m % 2, 0, :].bitcast(F32), ALU.subtract).then_inc(s_olo, 1)

                for p in range(STEPS):
                    split_values(0, p)

                def body(j):
                    for m in range(GROUP - 1):
                        split_output(j, m)
                    if not final(j):
                        for p in range(STEPS):
                            split_values(j + 1, p)
                    split_output(j, GROUP - 1)
                heads(eng, body)

            @block.tensor
            def _(eng):
                def turn_keys(j, c):
                    at, width = cols(2 * c)
                    if c == 0:
                        eng.wait_ge(s_kraw, 16 * (j + 1))
                        wait(eng, s_spread, 4 * j - 2)
                    else:
                        eng.wait_ge(s_klo, CHUNKS * j + c)
                    for k in range(width // P):
                        mm = eng.transpose(ps[:, AUX, k * P:(k + 1) * P], k_raw[:, at // P + k, :], core.ident[:, :])
                    mm.then_inc(s_turn, 1)

                def unit(j, m, n):
                    at, width = cols(n)
                    if n == 0:
                        eng.wait_ge(s_q[m], 16 * (j + 1))
                    if m == 0 and n % 2 == 0:
                        eng.wait_ge(s_klo, CHUNKS * j + n // 2 + 1)
                    wait(eng, s_se, UNITS * (4 * j + m) + n - 2)
                    for i, (s, k) in enumerate(PASSES):
                        mm = eng.matmul(ps[:, S_BANK + n % 3, 0:width], queries[:, m, s, (n % 2) * P:(n % 2 + 1) * P],
                                        keysT[k][:, at:at + width], start=(i == 0), stop=(i == 2))
                    mm.then_inc(s_qk, 1)

                def turn_probs(j, m, p):
                    index = STEPS * (4 * j + m) + p
                    bank = T_BANK + (m + p) % 2
                    if p % 2 == 0:
                        eng.wait_ge(s_exp, UNITS * (4 * j + m) + p + 2)
                    wait(eng, s_plo, index - 1)
                    for k in range(2):
                        for r in range(ROW_TILES):
                            mm = eng.transpose(ps[:, bank, k * ROWS + r * P:k * ROWS + (r + 1) * P],
                                               scores[:, m % 2, r, (2 * p + k) * P:(2 * p + k + 1) * P], core.ident[:, :])
                    mm.then_inc(s_pt, 1)

                def weigh_values(j, m, p):
                    index = STEPS * (4 * j + m) + p
                    eng.wait_ge(s_plo, index + 1)
                    if m == 0:
                        eng.wait_ge(s_vlo, STEPS * j + p + 1)
                    if p == 0:
                        wait(eng, s_on, 4 * j + m - 1)
                    for k in range(2):
                        for i, (s, v) in enumerate(PASSES):
                            mm = eng.matmul(ps[:, O_BANK + m % 2, 0:ROWS], values[s][:, 2 * p + k, :],
                                            probsT[v][:, (m + p) % 2, k, :],
                                            start=(p == 0 and k == 0 and i == 0),
                                            stop=(p == STEPS - 1 and k == 1 and i == 2))
                    mm.then_inc(s_pv, 1)

                def spread_sums(j, m):
                    G = 4 * j + m
                    eng.wait_ge(s_diag, G + 1)
                    wait(eng, s_spread, G)
                    if m == 2 and not final(j):
                        eng.wait_ge(s_klo, CHUNKS * (j + 2))
                    eng.matmul(ps[:, AUX, 0:ROWS], core.ones[:, :], diag[:, :, :].rearrange("p t n -> p (t n)"),
                               start=True, stop=True).then_inc(s_bc, 1)

                for c in range(CHUNKS):
                    turn_keys(0, c)
                for n in range(UNITS):
                    unit(0, 0, n)
                turn_probs(0, 0, 0)

                def body(j):
                    for m in range(GROUP):
                        more = not (final(j) and m == GROUP - 1)
                        j1, m1 = (j, m + 1) if m < GROUP - 1 else (j + 1, 0)
                        for p in range(STEPS):
                            if p < STEPS - 1:
                                turn_probs(j, m, p + 1)
                            elif more:
                                turn_probs(j1, m1, 0)
                            if more:
                                for n in QK_AT[p]:
                                    unit(j1, m1, n)
                            if m == 2 and not final(j) and p in TURN_AT:
                                turn_keys(j + 1, TURN_AT[p])
                            if p == SPREAD_AT:
                                spread_sums(j, m)
                            weigh_values(j, m, p)
                heads(eng, body)

            @block.scalar
            def _(eng):
                def high_keys(j, c):
                    at, width = cols(2 * c)
                    eng.wait_ge(s_turn, CHUNKS * j + c + 1)
                    eng.activation(keysT[0][:, at:at + width], ps[:, AUX, 0:width], ACT.Copy).then_inc(s_khi, 1)

                def exponential(j, m, n):
                    at, width = cols(n)
                    r, c = n % 2, n // 2
                    if n == 0:
                        eng.wait_ge(s_max, 4 * j + m + 1)
                        wait(eng, s_sum, 4 * j + m - 1)
                    eng.activation(scores[:, m % 2, r, at:at + width], scores[:, m % 2, r, at:at + width], ACT.Exp,
                                   bias=minus_max[:, m % 2, r:r + 1],
                                   accum_out=unit_sum[:, m % 2, r, c:c + 1]).then_inc(s_exp, 1)

                def high_probs(j, m, p):
                    index = STEPS * (4 * j + m) + p
                    eng.wait_ge(s_pt, index + 1)
                    wait(eng, s_pv, index - 1)
                    eng.activation(probsT[0][:, (m + p) % 2, :, :],
                                   ps[:, T_BANK + (m + p) % 2, :].rearrange("p (k r) -> p k r", r=ROWS),
                                   ACT.Copy).then_inc(s_phi, 1)

                def copy_spread(j, m):
                    eng.wait_ge(s_bc, 4 * j + m + 1)
                    wait(eng, s_on, 4 * j + m)
                    eng.activation(spread[:, :], ps[:, AUX, 0:ROWS], ACT.Copy).then_inc(s_spread, 1)

                for c in range(CHUNKS):
                    high_keys(0, c)
                for n in range(5):
                    exponential(0, 0, n)
                high_probs(0, 0, 0)

                def body(j):
                    for m in range(GROUP):
                        more = not (final(j) and m == GROUP - 1)
                        j1, m1 = (j, m + 1) if m < GROUP - 1 else (j + 1, 0)
                        for p in range(STEPS):
                            if p < STEPS - 1:
                                high_probs(j, m, p + 1)
                            elif more:
                                high_probs(j1, m1, 0)
                            for n in LATE_EXP.get(p, ()):
                                exponential(j, m, n)
                            if more:
                                for n in EARLY_EXP.get(p, ()):
                                    exponential(j1, m1, n)
                            if m == 2 and not final(j) and p in TURN_AT:
                                high_keys(j + 1, TURN_AT[p])
                            if p == SPREAD_AT:
                                copy_spread(j, m)
                heads(eng, body)

            @block.vector
            def _(eng):
                def low_keys(j, c):
                    at, width = cols(2 * c)
                    eng.wait_ge(s_khi, CHUNKS * j + c + 1)
                    eng.tensor_tensor(keysT[1][:, at:at + width], ps[:, AUX, 0:width],
                                      keysT[0][:, at:at + width].bitcast(F32), ALU.subtract).then_inc(s_klo, 1)

                def drain_unit(j, m, n):
                    at, width = cols(n)
                    r, c = n % 2, n // 2
                    G = 4 * j + m
                    eng.wait_ge(s_qk, UNITS * G + n + 1)
                    if n == 0:
                        wait(eng, s_pt, STEPS * (G - 1))
                    eng.tensor_scalar(scores[:, m % 2, r, at:at + width], ps[:, S_BANK + n % 3, 0:width], 1.0, None,
                                      ALU.mult, ALU.max, accum_out=unit_max[:, m % 2, r, c:c + 1]).then_inc(s_se, 1)

                def maximum(j, m):
                    G = 4 * j + m
                    eng.wait_ge(s_se, UNITS * (G + 1))
                    wait(eng, s_exp, UNITS * (G - 1))
                    eng.tensor_reduce(minus_max[:, m % 2, :], unit_max[:, m % 2, :, :], AX.X, ALU.max,
                                      negate=True).then_inc(s_max, 1)

                def low_probs(j, m, p):
                    index = STEPS * (4 * j + m) + p
                    eng.wait_ge(s_phi, index + 1)
                    eng.tensor_tensor(probsT[1][:, (m + p) % 2, :, :],
                                      ps[:, T_BANK + (m + p) % 2, :].rearrange("p (k r) -> p k r", r=ROWS),
                                      probsT[0][:, (m + p) % 2, :, :].bitcast(F32), ALU.subtract).then_inc(s_plo, 1)

                def invert_sums(j, m):
                    G = 4 * j + m
                    eng.wait_ge(s_exp, UNITS * (G + 1))
                    eng.tensor_reduce(row_sum[:, 0, :], unit_sum[:, m % 2, :, :], AX.X, ALU.add).then_inc(s_sum, 1)
                    eng.wait_ge(s_sum, G + 1)
                    eng.reciprocal(row_sum[:, 1, :], row_sum[:, 0, :]).then_inc(s_inv, 1)
                    eng.wait_ge(s_inv, G + 1)
                    wait(eng, s_bc, G)
                    for r in range(ROW_TILES):
                        ins = eng.tensor_scalar(diag[:, r, :], core.ident[:, :], row_sum[:, 1, r:r + 1], None, ALU.mult)
                    ins.then_inc(s_diag, 1)

                def norm_output(j, m):
                    G = 4 * j + m
                    eng.wait_ge(s_pv, STEPS * (G + 1))
                    eng.wait_ge(s_spread, G + 1)
                    wait(eng, s_olo, G - 1)
                    eng.tensor_tensor(o_full[:, m % 2, :], ps[:, O_BANK + m % 2, 0:ROWS], spread[:, :],
                                      ALU.mult).then_inc(s_on, 1)

                for c in range(CHUNKS):
                    low_keys(0, c)
                for n in range(UNITS):
                    drain_unit(0, 0, n)
                maximum(0, 0)
                low_probs(0, 0, 0)

                def body(j):
                    for m in range(GROUP):
                        more = not (final(j) and m == GROUP - 1)
                        j1, m1 = (j, m + 1) if m < GROUP - 1 else (j + 1, 0)
                        for p in range(STEPS):
                            if p < STEPS - 1:
                                low_probs(j, m, p + 1)
                            elif more:
                                low_probs(j1, m1, 0)
                            if p == 0 and m > 0:
                                norm_output(j, m - 1)
                            if more:
                                for n in QK_AT[p]:
                                    drain_unit(j1, m1, n)
                                if p == 12:
                                    maximum(j1, m1)
                            if m == 2 and not final(j) and p in TURN_AT:
                                low_keys(j + 1, TURN_AT[p])
                            if p == SUM_AT:
                                invert_sums(j, m)
                    norm_output(j, GROUP - 1)
                heads(eng, body)


def project_attention(core, a, o_scratch):
    nc, ps = core.nc, core.psum
    PAIRS = HEADS // GROUP // 2
    with ExitStack() as own:
        w_raw = core.sbuf("wo_raw", [P, 2, GROUP, HID], stack=own)
        w_part = [core.sbuf(f"wo_part{n}", [P, 2, GROUP, HID], F32R, stack=own) for n in range(2)]
        outT = core.sbuf("oT_parts", [P, 2, GROUP, 2, ROWS], F32R, stack=own)
        s_w = [core.sem(f"p_w_loaded{n}") for n in range(2)]
        s_o = [core.sem(f"p_o_loaded{n}") for n in range(2)]
        s_whi = core.sem("p_w_hi")
        s_wlo = core.sem("p_w_lo")
        s_mm = core.sem("p_products")

        wo = a["Wo"].rearrange("(h p) n -> p h n", p=P)

        def pairs(eng, step):
            step(0, 0)
            step(0, 1)
            with eng.Fori(1, PAIRS - 1) as i:
                step(i, 0)
                step(i, 1)
            step(PAIRS - 1, 0)
            step(PAIRS - 1, 1)

        with nc.Block() as block:
            @block.sync
            def _(eng):
                def load(i, par):
                    c = 2 * i + par
                    wait(eng, s_wlo, c - 1)
                    eng.dma_start(w_raw[:, par, :, :], wo[:, bass.ds(c * GROUP, GROUP), :]).then_inc(s_w[par], 16)
                    wait(eng, s_mm, c - 1)
                    eng.dma_start(outT[:, par, :, :, :].bitcast(F32),
                                  o_scratch[:, bass.ds(c * GROUP, GROUP), :, :]).then_inc(s_o[par], 16)
                pairs(eng, load)

            @block.tensor
            def _(eng):
                def products(i, par):
                    c = 2 * i + par
                    eng.wait_ge(s_o[par], 16 * (i + 1))
                    eng.wait_ge(s_wlo, c + 1)
                    first = isinstance(i, int) and c == 0
                    last = isinstance(i, int) and c == 2 * PAIRS - 1
                    for g in range(GROUP):
                        for t in range(ROW_TILES):
                            for n, (s, m) in enumerate(PASSES):
                                for half in range(2):
                                    mm = eng.matmul(ps[:, 2 * t + half, :], outT[:, par, g, s, t * P:(t + 1) * P],
                                                    w_part[m][:, par, g, half * BANK:(half + 1) * BANK],
                                                    start=(first and g == 0 and n == 0),
                                                    stop=(last and g == GROUP - 1 and n == 2))
                    mm.then_inc(s_mm, 1)
                pairs(eng, products)

            @block.scalar
            def _(eng):
                def split(i, par):
                    eng.wait_ge(s_w[par], 16 * (i + 1))
                    wait(eng, s_mm, 2 * i + par - 1)
                    eng.activation(w_part[0][:, par, :, :], w_raw[:, par, :, :], ACT.Copy).then_inc(s_whi, 1)
                pairs(eng, split)

            @block.vector
            def _(eng):
                def split(i, par):
                    eng.wait_ge(s_whi, 2 * i + par + 1)
                    eng.tensor_tensor(w_part[1][:, par, :, :], w_raw[:, par, :, :],
                                      w_part[0][:, par, :, :].bitcast(F32), ALU.subtract).then_inc(s_wlo, 1)
                pairs(eng, split)
                eng.wait_ge(s_mm, 2 * PAIRS)
                for t in range(ROW_TILES):
                    eng.tensor_tensor(core.x[:, t, :].rearrange("p (b n) -> p b n", n=BANK),
                                      ps[:, 2 * t:2 * t + 2, :],
                                      core.x[:, t, :].rearrange("p (b n) -> p b n", n=BANK), ALU.add)


def self_attention(core, a):
    nc, ps = core.nc, core.psum
    QKV = HID + 2 * KV_HEADS * SELF_DIM
    QK = HID + KV_HEADS * SELF_DIM
    TURNED = HID // (GROUP * SELF_DIM)
    STEPS = 2 * KV_HEADS
    SCALE = float(1.0 / np.sqrt(SELF_DIM))
    HALF = SELF_DIM // 2
    with ExitStack() as own:
        normed = core.sbuf("a_xn", [P, ROW_TILES, HID], stack=own)
        stats = core.sbuf("a_ln_stats", [P, ROW_TILES, 2, 6], stack=own)
        mv = core.sbuf("a_ln_mv", [P, ROW_TILES, 4], stack=own)
        xT = [core.sbuf(f"a_xnT_part{n}", [P, HID_TILES, ROWS], F32R, stack=own) for n in range(2)]
        w_raw = core.sbuf("a_w_raw", [P, 2, QKV], stack=own)
        w_part = [core.sbuf(f"a_w_part{n}", [P, HID_TILES, QKV], F32R, stack=own) for n in range(2)]
        tables = core.sbuf("a_rope_tables", [P, ROW_TILES, 2, HALF], stack=own)
        mask = core.sbuf("a_mask", [P, P], stack=own)
        turned = core.sbuf("a_rope_products", [P, 4, QK // 2], stack=own)
        qk = core.sbuf("a_qk_rows", [P, ROW_TILES, QK], stack=own)
        v = core.sbuf("a_v_rows", [P, ROW_TILES, KV_HEADS * SELF_DIM], stack=own)
        k_copies = core.sbuf("a_k_copies", [P, ROW_TILES, KV_HEADS, GROUP, SELF_DIM], stack=own)
        qT = core.sbuf("a_qT", [P, TURNED, ROWS], stack=own)
        kT = core.sbuf("a_kT", [P, TURNED, ROWS], stack=own)
        scores = core.sbuf("a_scores", [P, 2, GROUP, ROWS], stack=own)
        probsT = core.sbuf("a_probsT", [P, 2, 2, BANK], stack=own)
        small = core.sbuf("a_small", [P, STEPS, 4, GROUP], stack=own)

        s_x = core.sem("a_tables_loaded")
        s_w = [core.sem(f"a_w_loaded{n}") for n in range(2)]
        s_whi = core.sem("a_w_hi")
        s_wlo = core.sem("a_w_lo")
        s_ln = core.sem("a_ln_steps")
        s_var = core.sem("a_var_ready")
        s_rstd = core.sem("a_rstd_ready")
        s_t = core.sem("a_transposed")
        s_hi = core.sem("a_hi")
        s_lo = core.sem("a_lo")
        s_mm = core.sem("a_products")
        s_v = core.sem("a_v_rows_ready")
        s_rp = core.sem("a_rope_products_ready")
        s_rope = core.sem("a_rope_ready")
        s_kc = core.sem("a_k_copied")
        s_qt = core.sem("a_qk_turned")
        s_qta = core.sem("a_qT_ready")
        s_kta = core.sem("a_kT_ready")
        s_s = core.sem("a_scores_product")
        s_masked = core.sem("a_masked")
        s_mx = core.sem("a_max")
        s_nm = core.sem("a_minus_max")
        s_exp = core.sem("a_exp")
        s_pt = core.sem("a_probs_turned")
        s_pa = core.sem("a_probsT_first")
        s_pb = core.sem("a_probsT_second")
        s_pv = core.sem("a_pv")
        s_inv = core.sem("a_inverse")
        s_out = core.sem("a_out_rows")

        def width(x):
            return P * (x % 2 + 1)

        with nc.Block() as block:
            @block.sync
            def _(eng):
                eng.dma_start(tables[:, :, :, :], a["rope"].rearrange("(t p) c n -> p t c n", p=P)).then_inc(s_x, 16)
                eng.dma_start(mask[:, :], a["mask"]).then_inc(s_x, 16)
                KV = KV_HEADS * SELF_DIM
                for k in range(HID_TILES):
                    wait(eng, s_wlo, k - 1)
                    for w, at, n in (("wq", 0, HID), ("wk", HID, KV), ("wv", HID + KV, KV)):
                        eng.dma_start(w_raw[:, k % 2, at:at + n], a[w][k * P:(k + 1) * P, :]).then_inc(s_w[k % 2], 16)
                for k in range(HID_TILES):
                    eng.wait_ge(s_wlo, HID_TILES + k - 1)
                    eng.dma_start(w_raw[:, k % 2, 0:HID], a["wo"][k * P:(k + 1) * P, :]).then_inc(s_w[k % 2], 16)

            @block.gpsimd
            def _(eng):
                layer_norm_pool(eng, core, mv, s_var, s_rstd)
                for t in range(ROW_TILES):
                    pair = qk[:, t, :].rearrange("p (n two) -> p n two", two=2)
                    eng.wait_ge(s_rp, 4 * t + 4)
                    eng.tensor_tensor(pair[:, :, 0], turned[:, 0, :], turned[:, 1, :], ALU.subtract)
                    eng.tensor_tensor(pair[:, :, 1], turned[:, 2, :], turned[:, 3, :], ALU.add).then_inc(s_rope, 1)
                    eng.wait_ge(s_rope, t + 1)
                    for j in range(KV_HEADS):
                        ins = eng.tensor_copy(k_copies[:, t, j, :, :],
                                              qk[:, t, HID + j * SELF_DIM:HID + (j + 1) * SELF_DIM].unsqueeze(1)
                                              .broadcast_to([P, GROUP, SELF_DIM]))
                    ins.then_inc(s_kc, 1)

            @block.tensor
            def _(eng):
                def turn_rows(src, t, bank):
                    for k in range(HID_TILES):
                        mm = eng.transpose(ps[:, bank + k // 4, (k % 4) * P:(k % 4 + 1) * P],
                                           src[:, t, k * P:(k + 1) * P], core.ident[:, :])
                    return mm

                eng.wait_ge(s_ln, 8)
                for t in range(ROW_TILES):
                    turn_rows(normed, t, 2 * t).then_inc(s_t, 1)
                eng.wait_ge(s_lo, ROW_TILES)
                for k in range(HID_TILES):
                    eng.wait_ge(s_wlo, k + 1)
                    for t in range(ROW_TILES):
                        for n, (s, m) in enumerate(PASSES):
                            for b in range(QKV // BANK):
                                mm = eng.matmul(ps[:, 3 * t + b, :], xT[s][:, k, t * P:(t + 1) * P],
                                                w_part[m][:, k, b * BANK:(b + 1) * BANK],
                                                start=(k == 0 and n == 0), stop=(k == HID_TILES - 1 and n == 2))
                mm.then_inc(s_mm, 1)
                eng.wait_ge(s_rope, 1)
                turn_rows(qk, 0, 6).then_inc(s_qt, 1)
                eng.wait_ge(s_kc, 1)
                eng.wait_ge(s_rp, 8)
                eng.wait_ge(s_v, ROW_TILES)
                copies = k_copies[:, :, :, :, :].rearrange("p t j g d -> p t (j g d)")
                turn_rows(copies, 0, 0).then_inc(s_qt, 1)
                eng.wait_ge(s_rope, 2)
                turn_rows(qk, 1, 2).then_inc(s_qt, 1)
                eng.wait_ge(s_kc, 2)
                turn_rows(copies, 1, 4).then_inc(s_qt, 1)

                def score(x):
                    j, t = x // 2, x % 2
                    wait(eng, s_masked, x)
                    for r in range(GROUP):
                        at = slice(r * SELF_DIM, (r + 1) * SELF_DIM)
                        mm = eng.matmul(ps[:, r, 0:width(x)],
                                        qT[at, j, t * P:(t + 1) * P], kT[at, j, 0:width(x)], start=True, stop=True)
                    mm.then_inc(s_s, 1)

                def turn_probs(x):
                    eng.wait_ge(s_exp, x + 1)
                    wait(eng, s_pa, x)
                    wait(eng, s_pb, x // 2)
                    for k in range(x % 2 + 1):
                        for r in range(GROUP):
                            mm = eng.transpose(ps[:, 4 + k, r * P:(r + 1) * P],
                                               scores[:, x % 2, r, k * P:(k + 1) * P], core.ident[:, :])
                    mm.then_inc(s_pt, 1)

                def weigh(x):
                    j, t = x // 2, x % 2
                    eng.wait_ge(s_pa, x + 1)
                    wait(eng, s_pb, (x + 1) // 2)
                    wait(eng, s_out, x - 1)
                    for r in range(GROUP):
                        for k in range(t + 1):
                            mm = eng.matmul(ps[:, 6 + x % 2, r * SELF_DIM:(r + 1) * SELF_DIM],
                                            probsT[:, x % 2, k, r * P:(r + 1) * P],
                                            v[:, k, j * SELF_DIM:(j + 1) * SELF_DIM], start=(k == 0), stop=(k == t))
                    mm.then_inc(s_pv, 1)

                eng.wait_ge(s_qta, 2)
                eng.wait_ge(s_kta, 2)
                score(0)
                for x in range(STEPS):
                    if x + 1 < STEPS:
                        score(x + 1)
                    turn_probs(x)
                    if x > 0:
                        weigh(x - 1)
                weigh(STEPS - 1)
                eng.wait_ge(s_out, STEPS)
                for t in range(ROW_TILES):
                    turn_rows(normed, t, 2 * t).then_inc(s_t, 1)
                eng.wait_ge(s_lo, 2 * ROW_TILES)
                for k in range(HID_TILES):
                    eng.wait_ge(s_wlo, HID_TILES + k + 1)
                    for t in range(ROW_TILES):
                        for n, (s, m) in enumerate(PASSES):
                            for half in range(2):
                                mm = eng.matmul(ps[:, 4 + 2 * t + half, :], xT[s][:, k, t * P:(t + 1) * P],
                                                w_part[m][:, k, half * BANK:(half + 1) * BANK],
                                                start=(k == 0 and n == 0), stop=(k == HID_TILES - 1 and n == 2))
                mm.then_inc(s_mm, 1)

            @block.scalar
            def _(eng):
                def split(n, cols):
                    k = n % HID_TILES
                    count = 3 * (k // 2 + 1) if n < HID_TILES else 3 * HID_TILES // 2 + k // 2 + 1
                    eng.wait_ge(s_w[k % 2], 16 * count)
                    eng.activation(w_part[0][:, k, 0:cols], w_raw[:, k % 2, 0:cols], ACT.Copy).then_inc(s_whi, 1)

                def high(t, count):
                    eng.wait_ge(s_t, count)
                    eng.activation(xT[0][:, :, t * P:(t + 1) * P],
                                   ps[:, 2 * t:2 * t + 2, :].rearrange("p b (k n) -> p (b k) n", n=P),
                                   ACT.Copy).then_inc(s_hi, 1)

                for k in range(2):
                    split(k, QKV)
                for t in range(ROW_TILES):
                    high(t, t + 1)
                for k in range(2, HID_TILES):
                    split(k, QKV)
                eng.wait_ge(s_mm, 1)
                for t in range(ROW_TILES):
                    eng.activation(v[:, t, :], ps[:, 3 * t + 2, QK - 2 * BANK:BANK], ACT.Copy).then_inc(s_v, 1)
                for n in range(2):
                    eng.wait_ge(s_qt, 2 * n + 1)
                    b = (6, 2)[n]
                    eng.activation(qT[:, :, n * P:(n + 1) * P], ps[:, b:b + 2, :].rearrange("p b (k n) -> p (b k) n", n=P),
                                   ACT.Copy).then_inc(s_qta, 1)
                for x in range(STEPS):
                    eng.wait_ge(s_nm, x + 1)
                    for r in range(GROUP):
                        ins = eng.activation(scores[:, x % 2, r, 0:width(x)], scores[:, x % 2, r, 0:width(x)], ACT.Exp,
                                             scale=SCALE, bias=small[:, x, 1, r:r + 1],
                                             accum_out=small[:, x, 2, r:r + 1])
                    ins.then_inc(s_exp, 1)
                    eng.wait_ge(s_pt, x + 1)
                    wait(eng, s_pv, x - 1)
                    eng.activation(probsT[:, x % 2, 0, :], ps[:, 4, :], ACT.Copy).then_inc(s_pa, 1)
                    if x % 2:
                        split(HID_TILES + x // 2, HID)
                for t in range(ROW_TILES):
                    high(t, ROW_TILES + t + 1)

            @block.vector
            def _(eng):
                def split(n, cols):
                    k = n % HID_TILES
                    eng.wait_ge(s_whi, n + 1)
                    eng.tensor_tensor(w_part[1][:, k, 0:cols], w_raw[:, k % 2, 0:cols],
                                      w_part[0][:, k, 0:cols].bitcast(F32), ALU.subtract).then_inc(s_wlo, 1)

                def low(t, count):
                    eng.wait_ge(s_hi, count)
                    eng.tensor_tensor(xT[1][:, :, t * P:(t + 1) * P],
                                      ps[:, 2 * t:2 * t + 2, :].rearrange("p b (k n) -> p (b k) n", n=P),
                                      xT[0][:, :, t * P:(t + 1) * P].bitcast(F32), ALU.subtract).then_inc(s_lo, 1)

                layer_norm_vector(eng, core, core.x, normed, stats, mv, s_ln, s_var, s_rstd)
                for k in range(2):
                    split(k, QKV)
                for t in range(ROW_TILES):
                    low(t, t + 1)
                for k in range(2, HID_TILES):
                    split(k, QKV)
                eng.wait_ge(s_mm, 1)
                eng.wait_ge(s_x, 32)
                for t in range(ROW_TILES):
                    rows = ps[:, 3 * t:3 * t + 3, :].rearrange("p b n -> p (b n)")[:, 0:QK]
                    pair = rows.rearrange("p (h n two) -> p h n two", n=HALF, two=2)
                    wait(eng, s_rope, t)
                    eng.wait_ge(s_v, t + 1)
                    for n, (odd, sine) in enumerate(((0, 0), (1, 1), (0, 1), (1, 0))):
                        table = tables[:, t, sine, :].unsqueeze(1).broadcast_to([P, QK // SELF_DIM, HALF])
                        eng.tensor_tensor(turned[:, n, :].rearrange("p (h n) -> p h n", n=HALF), pair[:, :, :, odd],
                                          table, ALU.mult).then_inc(s_rp, 1)
                for n in range(2):
                    eng.wait_ge(s_qt, 2 * n + 2)
                    b = (0, 4)[n]
                    eng.tensor_copy(kT[:, :, n * P:(n + 1) * P],
                                    ps[:, b:b + 2, :].rearrange("p b (k n) -> p (b k) n", n=P)).then_inc(s_kta, 1)

                def maximum(x):
                    w = width(x)
                    eng.wait_ge(s_s, x + 1)
                    wait(eng, s_pt, x - 1)
                    if x % 2:
                        eng.tensor_copy(scores[:, 1, :, 0:P], ps[:, 0:GROUP, 0:P])
                    eng.tensor_tensor(scores[:, x % 2, :, w - P:w], ps[:, 0:GROUP, w - P:w],
                                      mask[:, :].unsqueeze(1).broadcast_to([P, GROUP, P]), ALU.add).then_inc(s_masked, 1)
                    eng.wait_ge(s_masked, x + 1)
                    eng.tensor_reduce(small[:, x, 0, :], scores[:, x % 2, :, 0:w], AX.X, ALU.max).then_inc(s_mx, 1)
                    eng.wait_ge(s_mx, x + 1)
                    eng.tensor_scalar(small[:, x, 1, :], small[:, x, 0, :], -SCALE, None, ALU.mult).then_inc(s_nm, 1)

                def norm(x):
                    j, t = x // 2, x % 2
                    eng.wait_ge(s_exp, x + 1)
                    eng.reciprocal(small[:, x, 3, :], small[:, x, 2, :]).then_inc(s_inv, 1)
                    eng.wait_ge(s_inv, x + 1)
                    eng.wait_ge(s_pv, x + 1)
                    eng.tensor_tensor(normed[:, t, j * P:(j + 1) * P].rearrange("p (g d) -> p g d", d=SELF_DIM),
                                      ps[:, 6 + x % 2, 0:P].rearrange("p (g d) -> p g d", d=SELF_DIM),
                                      over_last(small[:, x, 3, :], (P, GROUP, SELF_DIM)), ALU.mult).then_inc(s_out, 1)

                maximum(0)
                for x in range(STEPS):
                    if x + 1 < STEPS:
                        maximum(x + 1)
                    if x % 2:
                        eng.wait_ge(s_pt, x + 1)
                        wait(eng, s_pv, x - 1)
                        eng.tensor_copy(probsT[:, 1, 1, :], ps[:, 5, :]).then_inc(s_pb, 1)
                    if x > 0:
                        norm(x - 1)
                    if x % 2:
                        split(HID_TILES + x // 2, HID)
                norm(STEPS - 1)
                for t in range(ROW_TILES):
                    low(t, ROW_TILES + t + 1)
                eng.wait_ge(s_mm, 2)
                for t in range(ROW_TILES):
                    eng.tensor_tensor(core.x[:, t, :].rearrange("p (b n) -> p b n", n=BANK),
                                      ps[:, 4 + 2 * t:6 + 2 * t, :],
                                      core.x[:, t, :].rearrange("p (b n) -> p b n", n=BANK), ALU.add)


def feed_forward(core, a, out):
    nc, ps = core.nc, core.psum
    NR = LORAS * RANK
    A_TILES = NR // P
    with ExitStack() as own:
        raw = [core.sbuf(f"f_raw{n}", [P, HID_TILES, BANK], stack=own) for n in range(2)]
        a_shared = core.sbuf("f_a_shared", [RANK, HID], stack=own)
        b_shared = core.sbuf("f_b_shared", [P, HID_TILES, RANK], stack=own)
        aT = [core.sbuf(f"f_aT_part{n}", [P, HID_TILES, NR], F32R, stack=own) for n in range(2)]
        asT = [core.sbuf(f"f_asT_part{n}", [P, HID_TILES, RANK], F32R, stack=own) for n in range(2)]
        bT = [core.sbuf(f"f_bT_part{n}", [P, A_TILES, HID], F32R, stack=own) for n in range(2)]
        bsT = [core.sbuf(f"f_bsT_part{n}", [RANK, HID], F32R, stack=own) for n in range(2)]
        w_part = [core.sbuf(f"f_w_part{n}", [P, HID_TILES, BANK], F32R, stack=own) for n in range(2)]
        normed = core.sbuf("f_xn", [P, ROW_TILES, HID], stack=own)
        stats = core.sbuf("f_ln_stats", [P, ROW_TILES, 2, 6], stack=own)
        mv = core.sbuf("f_ln_mv", [P, ROW_TILES, 4], stack=own)
        xT = [core.sbuf(f"f_xnT_part{n}", [P, HID_TILES, ROWS], F32R, stack=own) for n in range(2)]
        gates = core.sbuf("f_gates", [P, ROW_TILES, LORAS], stack=own)
        bias = core.sbuf("f_bias", [P, HID], stack=own)
        z = core.sbuf("f_z", [P, ROW_TILES, NR + RANK], stack=own)
        zT = [core.sbuf(f"f_zT_part{n}", [P, ROW_TILES, NR], F32R, stack=own) for n in range(2)]
        zsT = [core.sbuf(f"f_zsT_part{n}", [RANK, ROWS], F32R, stack=own) for n in range(2)]

        s_a = core.sem("f_a_loaded")
        s_b = core.sem("f_b_loaded")
        s_small = core.sem("f_gates_bias_loaded")
        s_w = [core.sem(f"f_w_loaded{n}") for n in range(2)]
        s_t = core.sem("f_adapters_turned")
        s_hi = core.sem("f_adapters_hi")
        s_lo = core.sem("f_adapters_lo")
        s_whi = core.sem("f_w_hi")
        s_wlo = core.sem("f_w_lo")
        s_ln = core.sem("f_ln_steps")
        s_var = core.sem("f_var_ready")
        s_rstd = core.sem("f_rstd_ready")
        s_xt = core.sem("f_xn_turned")
        s_xhi = core.sem("f_xn_hi")
        s_xlo = core.sem("f_xn_lo")
        s_ax = core.sem("f_ax_product")
        s_z = core.sem("f_z_rows")
        s_zt = core.sem("f_z_turned")
        s_zhi = core.sem("f_z_hi")
        s_zlo = core.sem("f_z_lo")
        s_xb = core.sem("f_x_plus_bias")
        s_mm = core.sem("f_products")
        s_sum = core.sem("f_sums")
        s_out = core.sem("f_stored")

        fills = []
        for k in range(HID_TILES):
            fills.append(("a", [(raw[0][:, :, :].rearrange("p k n -> p (k n)")[:, t * HID + k * P:t * HID + (k + 1) * P], t * P, P)
                                for t in range(A_TILES)], P, NR, [part[:, k, :] for part in aT]))
        fills.append(("a", [(a_shared[:, k * P:(k + 1) * P], k * RANK, RANK) for k in range(HID_TILES)],
                      P, HID_TILES * RANK, [part[:, :, :].rearrange("p k n -> p (k n)") for part in asT]))
        for q in range(A_TILES):
            for h in range(2):
                fills.append(("b", [(raw[1][:, 4 * h + t, q * P:(q + 1) * P], t * P, P) for t in range(4)],
                              P, BANK, [part[:, q, h * BANK:(h + 1) * BANK] for part in bT]))
        for h in range(2):
            fills.append(("b", [(b_shared[:, 4 * h + t, :], t * P, P) for t in range(4)],
                          RANK, BANK, [part[:, h * BANK:(h + 1) * BANK] for part in bsT]))
        A_FILLS = HID_TILES + 1

        def halves(t):
            return slice(t * P, (t + 1) * P)

        with nc.Block() as block:
            @block.sync
            def _(eng):
                eng.dma_start(raw[0][:, :, :].rearrange("p k n -> p (k n)").rearrange("p (t i) -> p t i", i=HID),
                              a["lora_A"].rearrange("n r i -> (n r) i").rearrange("(t p) i -> p t i", p=P)).then_inc(s_a, 16)
                eng.dma_start(a_shared[:, :], a["lora_A_shared"]).then_inc(s_a, 16)
                for t in range(HID_TILES):
                    eng.dma_start(raw[1][:, t, :].rearrange("p (n r) -> p n r", r=RANK),
                                  a["lora_B"][:, t * P:(t + 1) * P, :].rearrange("n p r -> p n r")).then_inc(s_b, 16)
                eng.dma_start(b_shared[:, :, :], a["lora_B_shared"].rearrange("(t p) r -> p t r", p=P)).then_inc(s_b, 16)
                for b in range(LORA_BATCH):
                    t, at = b * ROWS_PER_GATE // P, b * ROWS_PER_GATE % P
                    eng.dma_start(gates[at:at + ROWS_PER_GATE, t, :],
                                  a["gate"][b:b + 1, :].broadcast_to([ROWS_PER_GATE, LORAS])).then_inc(s_small, 16)
                eng.dma_start(bias[:, :], a["bias"].rearrange("(o n) -> o n", o=1).broadcast_to([P, HID])).then_inc(s_small, 16)
                for h in range(2):
                    eng.wait_ge(s_t, (A_FILLS, len(fills))[h])
                    eng.dma_start(raw[h][:, :, :], a["kernel"].rearrange("(k p) n -> p k n", p=P)[:, :, h * BANK:(h + 1) * BANK]).then_inc(s_w[h], 16)
                for h in range(2):
                    eng.wait_ge(s_sum, h + 1)
                    eng.dma_start(out.rearrange("b (t p) n -> p (b t) n", p=P)[:, :, h * BANK:(h + 1) * BANK],
                                  normed[:, :, h * BANK:(h + 1) * BANK]).then_inc(s_out, 16)
                eng.wait_ge(s_out, 32)

            @block.gpsimd
            def _(eng):
                layer_norm_pool(eng, core, mv, s_var, s_rstd)
                eng.wait_ge(s_small, 16 * (LORA_BATCH + 1))
                eng.wait_ge(s_ln, 8)
                for t in range(ROW_TILES):
                    eng.tensor_tensor(core.x[:, t, :], core.x[:, t, :], bias[:, :], ALU.add).then_inc(s_xb, 1)

            @block.tensor
            def _(eng):
                for n, (which, moves, parts, width, dest) in enumerate(fills):
                    if n == 0:
                        eng.wait_ge(s_a, 32)
                    if n == A_FILLS:
                        eng.wait_ge(s_b, 16 * (HID_TILES + 1))
                    wait(eng, s_lo, n - 1)
                    for src, at, cols in moves:
                        rows = RANK if src.shape[0] == RANK else P
                        mm = eng.transpose(ps[0:parts, n % 2, at:at + (cols if parts == P else P)], src,
                                           core.ident[0:rows, 0:rows])
                    mm.then_inc(s_t, 1)
                eng.wait_ge(s_ln, 8)
                for t in range(ROW_TILES):
                    for k in range(HID_TILES):
                        mm = eng.transpose(ps[:, 2 + 2 * t + k // 4, (k % 4) * P:(k % 4 + 1) * P],
                                           normed[:, t, halves(k)], core.ident[:, :])
                    mm.then_inc(s_xt, 1)
                eng.wait_ge(s_lo, len(fills))
                eng.wait_ge(s_xlo, ROW_TILES)
                for t in range(ROW_TILES):
                    for bank, w, cols, at in ((6 + t, aT, NR, 0), (t, asT, RANK, 0)):
                        for k in range(HID_TILES):
                            for n, (s, m) in enumerate(PASSES):
                                mm = eng.matmul(ps[:, bank, at:at + cols], xT[s][:, k, halves(t)], w[m][:, k, :],
                                                start=(k == 0 and n == 0), stop=(k == HID_TILES - 1 and n == 2))
                mm.then_inc(s_ax, 1)

                def base(h):
                    eng.wait_ge(s_wlo, h + 1)
                    for t in range(ROW_TILES):
                        for k in range(HID_TILES):
                            for n, (s, m) in enumerate(PASSES):
                                mm = eng.matmul(ps[:, 2 + 2 * t + h, :], xT[s][:, k, halves(t)], w_part[m][:, k, :],
                                                start=(k == 0 and n == 0), stop=False)
                    return mm

                def delta(h):
                    for t in range(ROW_TILES):
                        for k in range(A_TILES):
                            for s, m in PASSES:
                                eng.matmul(ps[:, 2 + 2 * t + h, :], zT[s][:, t, halves(k)],
                                           bT[m][:, k, h * BANK:(h + 1) * BANK], start=False, stop=False)
                        for n, (s, m) in enumerate(PASSES):
                            mm = eng.matmul(ps[:, 2 + 2 * t + h, :], zsT[s][:, halves(t)],
                                            bsT[m][:, h * BANK:(h + 1) * BANK], start=False, stop=(n == 2))
                    mm.then_inc(s_mm, 1)

                base(0).then_inc(s_mm, 1)
                eng.wait_ge(s_z, 4)
                for t in range(ROW_TILES):
                    for k in range(A_TILES):
                        eng.transpose(ps[:, 6 + t, halves(k)], z[:, t, halves(k)], core.ident[:, :])
                for t in range(ROW_TILES):
                    mm = eng.transpose(ps[0:RANK, 0, halves(t)], z[:, t, NR:NR + RANK], core.ident[:, :])
                mm.then_inc(s_zt, 1)
                eng.wait_ge(s_zlo, 2)
                delta(0)
                base(1)
                delta(1)

            @block.scalar
            def _(eng):
                for n, (which, moves, parts, width, dest) in enumerate(fills):
                    eng.wait_ge(s_t, n + 1)
                    eng.activation(dest[0], ps[0:parts, n % 2, 0:width], ACT.Copy).then_inc(s_hi, 1)
                for t in range(ROW_TILES):
                    eng.wait_ge(s_xt, t + 1)
                    eng.activation(xT[0][:, :, halves(t)],
                                   ps[:, 2 + 2 * t:4 + 2 * t, :].rearrange("p b (k n) -> p (b k) n", n=P),
                                   ACT.Copy).then_inc(s_xhi, 1)
                eng.wait_ge(s_w[0], 16)
                eng.activation(w_part[0][:, :, :], raw[0][:, :, :], ACT.Copy).then_inc(s_whi, 1)
                eng.wait_ge(s_zt, 1)
                eng.activation(zT[0][:, :, :], ps[:, 6:8, :], ACT.Copy).then_inc(s_zhi, 1)
                eng.activation(zsT[0][:, :], ps[0:RANK, 0, 0:ROWS], ACT.Copy).then_inc(s_zhi, 1)
                eng.wait_ge(s_w[1], 16)
                eng.wait_ge(s_mm, 1)
                eng.activation(w_part[0][:, :, :], raw[1][:, :, :], ACT.Copy).then_inc(s_whi, 1)

            @block.vector
            def _(eng):
                for n, (which, moves, parts, width, dest) in enumerate(fills):
                    eng.wait_ge(s_hi, n + 1)
                    eng.tensor_tensor(dest[1], ps[0:parts, n % 2, 0:width], dest[0].bitcast(F32),
                                      ALU.subtract).then_inc(s_lo, 1)
                layer_norm_vector(eng, core, core.x, normed, stats, mv, s_ln, s_var, s_rstd)
                for t in range(ROW_TILES):
                    eng.wait_ge(s_xhi, t + 1)
                    eng.tensor_tensor(xT[1][:, :, halves(t)],
                                      ps[:, 2 + 2 * t:4 + 2 * t, :].rearrange("p b (k n) -> p (b k) n", n=P),
                                      xT[0][:, :, halves(t)].bitcast(F32), ALU.subtract).then_inc(s_xlo, 1)
                eng.wait_ge(s_whi, 1)
                eng.tensor_tensor(w_part[1][:, :, :], raw[0][:, :, :], w_part[0][:, :, :].bitcast(F32),
                                  ALU.subtract).then_inc(s_wlo, 1)
                eng.wait_ge(s_ax, 1)
                eng.wait_ge(s_small, 16 * (LORA_BATCH + 1))
                for t in range(ROW_TILES):
                    eng.tensor_tensor(z[:, t, 0:NR].rearrange("p (n r) -> p n r", r=RANK),
                                      ps[:, 6 + t, :].rearrange("p (n r) -> p n r", r=RANK),
                                      over_last(gates[:, t, :], (P, LORAS, RANK)), ALU.mult).then_inc(s_z, 1)
                    eng.tensor_copy(z[:, t, NR:NR + RANK], ps[:, t, 0:RANK]).then_inc(s_z, 1)
                eng.wait_ge(s_zhi, 2)
                eng.tensor_tensor(zT[1][:, :, :], ps[:, 6:8, :], zT[0][:, :, :].bitcast(F32), ALU.subtract).then_inc(s_zlo, 1)
                eng.tensor_tensor(zsT[1][:, :], ps[0:RANK, 0, 0:ROWS], zsT[0][:, :].bitcast(F32),
                                  ALU.subtract).then_inc(s_zlo, 1)
                eng.wait_ge(s_whi, 2)
                eng.tensor_tensor(w_part[1][:, :, :], raw[1][:, :, :], w_part[0][:, :, :].bitcast(F32),
                                  ALU.subtract).then_inc(s_wlo, 1)
                eng.wait_ge(s_xb, ROW_TILES)
                for h in range(2):
                    eng.wait_ge(s_mm, h + 2)
                    for t in range(ROW_TILES):
                        ins = eng.tensor_tensor(normed[:, t, h * BANK:(h + 1) * BANK], ps[:, 2 + 2 * t + h, :],
                                                core.x[:, t, h * BANK:(h + 1) * BANK], ALU.add)
                    ins.then_inc(s_sum, 1)


def perceiver_layer(nc, a, out):
    with ExitStack() as stack:
        core = Core(nc, stack)

        def scratch(name, shape):
            return nc.dram_tensor(name, shape, F32, kind="Internal").ap()

        q_scratch = scratch("q_scratch", (KV_HEADS, P, 2, GROUP, ROWS))
        k_scratch = scratch("k_scratch", (KV_HEADS, P, KEY_TILES, DIM))
        v_scratch = scratch("v_scratch", (KV_HEADS, P, KEY_TILES, DIM))
        o_scratch = scratch("o_scratch", (P, HEADS, 2, ROWS))
        with ExitStack() as early:
            xnT = [core.sbuf(f"xnT_part{n}", [P, HID_TILES, ROWS], F32R, stack=early) for n in range(2)]
            project_queries(core, a, xnT, q_scratch)
            project_keys_values(core, a, xnT, k_scratch, v_scratch)
        cross_attention(core, q_scratch, k_scratch, v_scratch, o_scratch)
        project_attention(core, a, o_scratch)
        self_attention(core, a)
        feed_forward(core, a, out)


_NAMES = {
    "x": "x", "ctx": "ctx_4096", "Wq": "L0_xattn_Wq", "Wk": "L0_xattn_Wk", "Wv": "L0_xattn_Wv",
    "Wo": "L0_xattn_Wo", "q_norm_w": "L0_xattn_q_norm_w", "k_norm_w": "L0_xattn_k_norm_w",
    "wq": "L0_attn_wq", "wk": "L0_attn_wk", "wv": "L0_attn_wv", "wo": "L0_attn_wo",
    "gate": "L0_ffn_gate", "kernel": "L0_ffn_kernel", "bias": "L0_ffn_bias", "lora_A": "L0_ffn_lora_A",
    "lora_B": "L0_ffn_lora_B", "lora_A_shared": "L0_ffn_lora_A_shared", "lora_B_shared": "L0_ffn_lora_B_shared",
}


def shape_constants():
    half = SELF_DIM // 2
    freqs = (1.0 / np.float32(10000.0) ** (np.arange(0, SELF_DIM, 2, dtype=np.float32) / np.float32(SELF_DIM))).astype(np.float32)
    angle = np.outer(np.arange(ROWS, dtype=np.float32), freqs).astype(np.float32)
    rope = np.stack([np.cos(angle), np.sin(angle)], axis=1).astype(np.float32)
    assert rope.shape == (ROWS, 2, half)
    return {
        "ident": np.eye(P, dtype=np.float32),
        "rope": rope,
        "mask": np.triu(np.full((P, P), NEGATIVE, np.float32), 1),
    }


def kernel(**inputs):
    import concourse.bacc as bacc
    from concourse.bass_utils import run_bass_kernel_spmd

    nc = bacc.Bacc("TRN2", target_bir_lowering=False, num_devices=1)
    given = {short: np.ascontiguousarray(inputs[name]) for short, name in _NAMES.items()} | shape_constants()
    arrays, aps = {}, {}
    for short, array in given.items():
        arrays[f"in_{short}"] = array
        aps[short] = nc.dram_tensor(f"in_{short}", array.shape, mybir.dt.from_np(array.dtype), kind="ExternalInput").ap()
    out = nc.dram_tensor("out_x", (1, ROWS, HID), F32, kind="ExternalOutput").ap()
    perceiver_layer(nc, aps, out)
    result = run_bass_kernel_spmd(nc, [arrays], core_ids=[0])
    return result.results[0]["out_x"]
```

```python
from contextlib import ExitStack

import numpy as np

import concourse.bass as bass
from concourse import mybir

F32 = mybir.dt.float32
F32R = mybir.dt.float32r
ALU = mybir.AluOpType
ACT = mybir.ActivationFunctionType
AX = mybir.AxisListType

P = 128
BANK = 512
ROWS = 256
ROW_TILES = ROWS // P
HID = 1024
HID_TILES = HID // P
CTX = 4096
CTX_TILES = CTX // P
KEYS = CTX + ROWS
KEY_TILES = KEYS // P
HEADS = 32
KV_HEADS = 8
GROUP = HEADS // KV_HEADS
DIM = 128
LN_EPS = 1e-5
RMS_EPS = 1e-6
SELF_DIM = HID // HEADS
LORAS = 16
RANK = 32
LORA_BATCH = 8
ROWS_PER_GATE = ROWS // LORA_BATCH
NEGATIVE = -1e30

PASSES = ((0, 0), (0, 1), (1, 0))


def wait(engine, semaphore, value):
    if not isinstance(value, int) or value > 0:
        engine.wait_ge(semaphore, value)


def over_last(ap, shape):
    return ap.unsqueeze(len(shape) - 1).broadcast_to(list(shape))


class Core:

    def __init__(self, nc, stack):
        self.nc, self.stack = nc, stack
        self.psum = stack.enter_context(nc.psum_tensor("psum", [P, 8, BANK], F32))
        self.ident = self.sbuf("ident", [P, P])
        self.ones = self.sbuf("ones", [P, P])
        self.minus_half = self.sbuf("minus_half", [P, KV_HEADS])
        self.x = self.sbuf("x_rows", [P, ROW_TILES, HID])

    def sbuf(self, name, shape, dtype=F32, stack=None):
        return (stack or self.stack).enter_context(self.nc.sbuf_tensor(name, shape, dtype))

    def sem(self, name):
        return self.stack.enter_context(self.nc.semaphore(name))


def layer_norm_statistics(eng, rows, stats, mv, done, to_pool):
    for t in range(ROW_TILES):
        for half in range(2):
            eng.bn_stats(stats[:, t, half, :], rows[:, t, half * BANK:(half + 1) * BANK]).then_inc(done, 1)
        eng.wait_ge(done, 3 * t + 2)
        eng.bn_aggr(mv[:, t, 0:2], stats[:, t, :, :]).then_inc(done, 1)
        eng.wait_ge(done, 3 * t + 3)
        eng.tensor_scalar(mv[:, t, 2:3], mv[:, t, 1:2], LN_EPS, None, ALU.add).then_inc(to_pool, 1)


def layer_norm_vector(eng, core, rows, normed, stats, mv, done, to_pool, from_pool):
    layer_norm_statistics(eng, rows, stats, mv, done, to_pool)
    for t in range(ROW_TILES):
        eng.wait_ge(from_pool, t + 1)
        eng.tensor_scalar(normed[:, t, :], rows[:, t, :], mv[:, t, 0:1], mv[:, t, 3:4],
                          ALU.subtract, ALU.mult).then_inc(done, 1)


def layer_norm_pool(eng, core, mv, to_pool, from_pool):
    for t in range(ROW_TILES):
        eng.wait_ge(to_pool, t + 1)
        eng.tensor_tensor(mv[:, t, 3:4], mv[:, t, 2:3], core.minus_half[:, 0:1], ALU.pow).then_inc(from_pool, 1)


SHARED_WORDS = 2 * KEYS + KEY_TILES * DIM + GROUP * 2 * ROWS


class Shared:

    def __init__(self, core, stack):
        self.keysT = [core.sbuf(f"keysT_part{n}", [P, KEYS], F32R, stack=stack) for n in range(2)]
        self.k_raw = core.sbuf("k_raw", [P, KEY_TILES, DIM], stack=stack)
        self.queries = core.sbuf("queries", [P, GROUP, 2, ROWS], F32R, stack=stack)
        self.s_kraw = core.sem("x_k_loaded")
        self.s_q = [core.sem(f"x_q_loaded{m}") for m in range(GROUP)]
        self.s_turn = core.sem("x_keys_turned")
        self.s_khi = core.sem("x_keys_hi")
        self.s_klo = core.sem("x_keys_lo")
        self.s_ost = [core.sem(f"x_o_stored{n}") for n in range(2)]


class Projection:
    HEADS = 2

    def __init__(self, core, wo, o_scratch, stack):
        self.wo, self.o_scratch = wo.rearrange("(h p) n -> p h n", p=P), o_scratch
        self.w_raw = core.sbuf("wo_raw", [P, 2, self.HEADS, HID], stack=stack)
        self.w_part = [core.sbuf(f"wo_part{n}", [P, 2, self.HEADS, HID], F32R, stack=stack) for n in range(2)]
        self.outT = core.sbuf("oT_parts", [P, 2, self.HEADS, 2, ROWS], F32R, stack=stack)
        self.s_w = [core.sem(f"p_w_loaded{n}") for n in range(2)]
        self.s_o = [core.sem(f"p_o_loaded{n}") for n in range(2)]
        self.s_whi = core.sem("p_w_hi")
        self.s_wlo = core.sem("p_w_lo")

    def load_weights(self, eng, i, par):
        eng.dma_start(self.w_raw[:, par, :, :],
                      self.wo[:, bass.ds((2 * i + par) * self.HEADS, self.HEADS), :]).then_inc(self.s_w[par], 16)

    def load_outputs(self, eng, i, par):
        eng.dma_start(self.outT[:, par, :, :, :].bitcast(F32),
                      self.o_scratch[:, bass.ds((2 * i + par) * self.HEADS, self.HEADS), :, :]).then_inc(self.s_o[par], 16)

    def high(self, eng, i, par, g):
        eng.wait_ge(self.s_w[par], 16 * (i + 1))
        eng.activation(self.w_part[0][:, par, g, :], self.w_raw[:, par, g, :], ACT.Copy).then_inc(self.s_whi, 1)

    def low(self, eng, i, par, g):
        eng.wait_ge(self.s_whi, (2 * i + par) * self.HEADS + g + 1)
        eng.tensor_tensor(self.w_part[1][:, par, g, :], self.w_raw[:, par, g, :],
                          self.w_part[0][:, par, g, :].bitcast(F32), ALU.subtract).then_inc(self.s_wlo, 1)


CHUNKS = -(-KEYS // BANK)


def chunk_columns(c):
    return c * BANK, min(BANK, KEYS - c * BANK)


def project_inputs(core, a, own, shared, q_scratch, k_scratch, v_scratch):
    nc, ps = core.nc, core.psum
    KV = KV_HEADS * DIM
    T_BANK, K_BANK, V_BANK, KEYS_BANK = 0, 2, 4, 6
    LAST = CTX_TILES // 2 - 1
    LATENT = KEY_TILES // 2 - 1
    PIECES = 2 * HID_TILES
    Q_PAIRS = KV_HEADS // 2

    wv_part = [core.sbuf(f"wv_part{n}", [P, HID_TILES, KV], F32R, stack=own) for n in range(2)]
    wk_part = [core.sbuf(f"wk_part{n}", [P, HID_TILES, KV], F32R, stack=own) for n in range(2)]
    w_raw = core.sbuf("w_raw", [P, 2, KV], stack=own)
    rows = core.sbuf("key_rows", [P, 2, HID], stack=own)
    rowsT = [core.sbuf(f"key_rowsT_part{n}", [P, 2, HID_TILES, P], F32R, stack=own) for n in range(2)]
    square = core.sbuf("squares", [P, KV], stack=own)
    small = core.sbuf("rms_small", [P, 3, KV_HEADS], stack=own)
    k_out = core.sbuf("k_out", [P, 2, KV], stack=own)
    v_out = core.sbuf("v_out", [P, 2, KV], stack=own)
    q_part = [core.sbuf(f"q_part{n}", [P, 2, GROUP, ROWS], F32R, stack=own) for n in range(2)]
    stats = core.sbuf("ln_stats", [P, ROW_TILES, 2, 6], stack=own)
    mv = core.sbuf("ln_mv", [P, ROW_TILES, 4], stack=own)
    weights = core.sbuf("norm_weights", [P, 4], stack=own)

    s_const = core.sem("i_ident_loaded")
    s_small = core.sem("i_x_weights_loaded")
    s_fill = core.sem("i_constants_set")
    s_nw = core.sem("i_norm_weights")
    s_ln = core.sem("i_ln_steps")
    s_var = core.sem("i_var_ready")
    s_rstd = core.sem("i_rstd_ready")
    s_w = [core.sem(f"i_w_loaded{n}") for n in range(2)]
    s_whi = core.sem("i_w_hi")
    s_wlo = core.sem("i_w_lo")
    s_rows = [core.sem(f"i_rows_loaded{n}") for n in range(2)]
    s_t = core.sem("i_rows_transposed")
    s_hi = core.sem("i_rows_hi")
    s_lo = core.sem("i_rows_lo")
    s_k = core.sem("i_k_product")
    s_v = core.sem("i_v_product")
    s_q = core.sem("i_q_product")
    s_sq = core.sem("i_squared")
    s_sum = core.sem("i_summed")
    s_ms = core.sem("i_mean_square")
    s_rms = core.sem("i_rms_scale")
    s_krow = core.sem("i_k_rows")
    s_vrow = core.sem("i_v_rows")
    s_qrow = core.sem("i_q_rows")
    s_qt = core.sem("i_q_transposed")
    s_qhi = core.sem("i_q_hi")
    s_qlo = core.sem("i_q_lo")
    s_kst = [core.sem(f"i_k_stored{n}") for n in range(2)]
    s_vst = [core.sem(f"i_v_stored{n}") for n in range(2)]
    s_qst = [core.sem(f"i_q_stored{n}") for n in range(2)]

    def q_piece(part, par, h):
        return part[:, 2 * h:2 * h + 2, par * BANK:(par + 1) * BANK]

    with nc.Block() as block:
        @block.sync
        def _(eng):
            ctx = a["ctx"].rearrange("b (t p) n -> p (b t) n", p=P)
            wq = a["Wq"].rearrange("(k p) n -> p k n", p=P)

            def load(i, par):
                wait(eng, s_t, 2 * i + par - 1)
                eng.dma_start(rows[:, par, :], ctx[:, bass.ds(2 * i + par, 1), :].rearrange("p o n -> p (o n)")).then_inc(s_rows[par], 16)

            def load_weights(n):
                wait(eng, s_wlo, n - 1)
                w = a["Wk"] if n < HID_TILES else a["Wv"]
                k = n % HID_TILES
                eng.dma_start(w_raw[:, n % 2, :], w[k * P:(k + 1) * P, :]).then_inc(s_w[n % 2], 16)

            def load_q_weights(i, par):
                c = 2 * i + par
                for h in range(4):
                    eng.wait_ge(s_wlo, PIECES + 4 * c + h - 1)
                    eng.dma_start(w_raw[:, h % 2, :].rearrange("p (k n) -> p k n", n=BANK),
                                  wq[:, 2 * h:2 * h + 2, bass.ds(c * BANK, BANK)]).then_inc(s_w[h % 2], 16)

            def store(i, par):
                t = 2 * i + par
                for done, out, scratch, stored in ((s_krow, k_out, k_scratch, s_kst), (s_vrow, v_out, v_scratch, s_vst)):
                    wait(eng, done, t + 1)
                    eng.dma_start(scratch[:, :, bass.ds(t, 1), :].rearrange("h p o d -> p (h o) d"),
                                  out[:, par, :].rearrange("p (h d) -> p h d", d=DIM)).then_inc(stored[par], 16)

            def store_q(i, par):
                c = 2 * i + par
                eng.wait_ge(s_qlo, c + 1)
                for n in range(2):
                    eng.dma_start(q_scratch[bass.ds(c, 1), :, n, :, :].rearrange("o p g r -> (o p) g r"),
                                  q_part[n][:, par, :, :].bitcast(F32)).then_inc(s_qst[par], 16)

            load(0, 0)
            eng.dma_start(core.ident[:, :], a["ident"]).then_inc(s_const, 16)
            load_weights(0)
            load_weights(1)
            load(0, 1)
            for n in range(2, PIECES):
                load_weights(n)
            eng.dma_start(core.x[:, :, :], a["x"].rearrange("b (t p) n -> p (b t) n", p=P)).then_inc(s_small, 16)
            eng.dma_start(weights[:, 0:1], a["q_norm_w"].rearrange("(p o) -> p o", o=1)).then_inc(s_small, 16)
            eng.dma_start(weights[:, 1:2], a["k_norm_w"].rearrange("(p o) -> p o", o=1)).then_inc(s_small, 16)
            with eng.Fori(0, LAST) as i:
                load(i + 1, 0)
                store(i, 0)
                load(i + 1, 1)
                store(i, 1)
            store(LAST, 0)
            store(LAST, 1)
            store(LATENT, 0)
            load_q_weights(0, 0)
            store(LATENT, 1)
            load_q_weights(0, 1)
            for par in range(2):
                eng.wait_ge(s_kst[par], 16 * KEY_TILES // 2)
                eng.wait_ge(s_vst[par], 16 * KEY_TILES // 2)
            eng.dma_start(shared.k_raw[:, :, :], k_scratch[0, :, :, :]).then_inc(shared.s_kraw, 16)
            load_q_weights(1, 0)
            load_q_weights(1, 1)
            with eng.Fori(2, Q_PAIRS) as i:
                store_q(i - 2, 0)
                load_q_weights(i, 0)
                store_q(i - 2, 1)
                load_q_weights(i, 1)
            eng.wait_ge(s_qst[0], 32)
            for m in range(GROUP):
                eng.dma_start(shared.queries[:, m, :, :].bitcast(F32), q_scratch[0, :, :, m, :]).then_inc(shared.s_q[m], 16)
            for i in (Q_PAIRS - 2, Q_PAIRS - 1):
                store_q(i, 0)
                store_q(i, 1)
            for par in range(2):
                eng.wait_ge(s_qst[par], 32 * Q_PAIRS)

        @block.gpsimd
        def _(eng):
            eng.memset(core.minus_half[:, :], -0.5).then_inc(s_fill, 1)
            eng.memset(core.ones[:, :], 1.0).then_inc(s_fill, 1)
            eng.wait_ge(s_fill, 2)
            layer_norm_pool(eng, core, mv, s_var, s_rstd)
            with eng.Fori(0, KEY_TILES + KV_HEADS) as n:
                eng.wait_ge(s_ms, n + 1)
                eng.tensor_tensor(small[:, 2, :], small[:, 1, :], core.minus_half[:, :], ALU.pow).then_inc(s_rms, 1)

        @block.tensor
        def _(eng):
            def transposes(i, par, latent=False):
                t = 2 * i + par
                if latent:
                    eng.wait_ge(s_ln, 7 + par)
                else:
                    wait(eng, s_rows[par], 16 * (i + 1))
                wait(eng, s_lo, t)
                for k in range(HID_TILES):
                    mm = eng.transpose(ps[:, T_BANK + k // 4, (k % 4) * P:(k % 4 + 1) * P],
                                       rows[:, par, k * P:(k + 1) * P], core.ident[:, :])
                mm.then_inc(s_t, 1)

            def product(bank, par, w_part, ready):
                for k in range(HID_TILES):
                    if ready is not None:
                        eng.wait_ge(s_wlo, ready + k + 1)
                    for n, (s, m) in enumerate(PASSES):
                        for half in range(2):
                            mm = eng.matmul(ps[:, bank + half, :], rowsT[s][:, par, k, :],
                                            w_part[m][:, k, half * BANK:(half + 1) * BANK],
                                            start=(k == 0 and n == 0), stop=(k == HID_TILES - 1 and n == 2))
                return mm

            def products(i, par, first=False):
                t = 2 * i + par
                wait(eng, s_lo, t + 1)
                wait(eng, s_krow, t)
                product(K_BANK, par, wk_part, 0 if first else None).then_inc(s_k, 1)
                wait(eng, s_vrow, t)
                product(V_BANK, par, wv_part, HID_TILES if first else None).then_inc(s_v, 1)

            eng.wait_ge(s_const, 16)
            transposes(0, 0)
            transposes(0, 1)
            products(0, 0, first=True)
            transposes(1, 0)
            products(0, 1)
            with eng.Fori(1, LAST) as i:
                transposes(i, 1)
                products(i, 0)
                transposes(i + 1, 0)
                products(i, 1)
            transposes(LAST, 1)
            products(LAST, 0)
            transposes(LATENT, 0, latent=True)
            products(LAST, 1)
            transposes(LATENT, 1, latent=True)
            products(LATENT, 0)
            products(LATENT, 1)

            def q_products(i, par):
                c = 2 * i + par
                bank = (K_BANK, T_BANK)[par]
                if isinstance(i, int) and i == 0:
                    eng.wait_ge((s_krow, s_lo)[par], KEY_TILES)
                else:
                    eng.wait_ge(s_qrow, c - 1)
                for h in range(4):
                    eng.wait_ge(s_wlo, PIECES + 4 * c + h + 1)
                    for k in (2 * h, 2 * h + 1):
                        for t in range(ROW_TILES):
                            for n, (s, m) in enumerate(PASSES):
                                mm = eng.matmul(ps[:, bank + t, :], rowsT[s][:, t, k, :],
                                                wk_part[m][:, k, par * BANK:(par + 1) * BANK],
                                                start=(k == 0 and n == 0), stop=(k == HID_TILES - 1 and n == 2))
                mm.then_inc(s_q, 1)

            def q_transposes(i, par):
                c = 2 * i + par
                if isinstance(i, int) and c == 0:
                    eng.wait_ge(s_vrow, KEY_TILES)
                wait(eng, s_qrow, c + 1)
                wait(eng, s_qlo, c)
                for t in range(ROW_TILES):
                    for g in range(GROUP):
                        mm = eng.transpose(ps[:, V_BANK + t, g * P:(g + 1) * P],
                                           rows[:, par, t * BANK + g * P:t * BANK + (g + 1) * P], core.ident[:, :])
                mm.then_inc(s_qt, 1)

            def turn_keys(c):
                at, width = chunk_columns(c)
                eng.wait_ge(shared.s_kraw, 16)
                wait(eng, shared.s_klo, c - 1)
                for k in range(width // P):
                    mm = eng.transpose(ps[:, KEYS_BANK + c % 2, k * P:(k + 1) * P],
                                       shared.k_raw[:, at // P + k, :], core.ident[:, :])
                mm.then_inc(shared.s_turn, 1)

            q_products(0, 0)
            q_products(0, 1)
            q_transposes(0, 0)
            with eng.Fori(1, Q_PAIRS - 1) as i:
                q_products(i, 0)
                q_transposes(i - 1, 1)
                q_products(i, 1)
                q_transposes(i, 0)
            i = Q_PAIRS - 1
            for c in range(3):
                turn_keys(c)
            q_products(i, 0)
            q_transposes(i - 1, 1)
            for c in range(3, 6):
                turn_keys(c)
            q_products(i, 1)
            q_transposes(i, 0)
            for c in range(6, CHUNKS):
                turn_keys(c)
            q_transposes(i, 1)

        @block.scalar
        def _(eng):
            def split_weights(n):
                eng.wait_ge(s_w[n % 2], 16 * (n // 2 + 1))
                part = (wk_part, wv_part)[n // HID_TILES][0]
                eng.activation(part[:, n % HID_TILES, :], w_raw[:, n % 2, :], ACT.Copy).then_inc(s_whi, 1)

            def high(i, par):
                t = 2 * i + par
                wait(eng, s_t, t + 1)
                wait(eng, s_v, t - 1)
                eng.activation(rowsT[0][:, par, :, :],
                               ps[:, T_BANK:T_BANK + 2, :].rearrange("p b (k n) -> p (b k) n", n=P),
                               ACT.Copy).then_inc(s_hi, 1)

            def squares(product, count, bank, number):
                eng.wait_ge(product, count)
                wait(eng, s_sum, number)
                eng.activation(square[:, :].rearrange("p (b n) -> p b n", n=BANK), ps[:, bank:bank + 2, :],
                               ACT.Square).then_inc(s_sq, 1)

            def copy_v(i, par):
                wait(eng, s_v, 2 * i + par + 1)
                wait(eng, s_vst[par], 16 * i)
                eng.activation(v_out[:, par, :].rearrange("p (b n) -> p b n", n=BANK), ps[:, V_BANK:V_BANK + 2, :],
                               ACT.Copy).then_inc(s_vrow, 1)

            def drain(i, par):
                squares(s_k, 2 * i + par + 1, K_BANK, 2 * i + par)
                copy_v(i, par)

            high(0, 0)
            split_weights(0)
            split_weights(1)
            high(0, 1)
            for n in range(2, PIECES):
                split_weights(n)
            with eng.Fori(0, LAST) as i:
                drain(i, 0)
                high(i + 1, 0)
                drain(i, 1)
                high(i + 1, 1)
            drain(LAST, 0)
            high(LATENT, 0)
            drain(LAST, 1)
            high(LATENT, 1)
            drain(LATENT, 0)
            squares(s_k, KEY_TILES, K_BANK, KEY_TILES - 1)

            def q_split(i, par):
                c = 2 * i + par
                wait(eng, s_q, c - 1)
                for h in range(4):
                    eng.wait_ge(s_w[h % 2], 8 * PIECES + 16 * (2 * c + h // 2 + 1))
                    eng.activation(q_piece(wk_part[0], par, h), w_raw[:, h % 2, :].rearrange("p (k n) -> p k n", n=BANK),
                                   ACT.Copy).then_inc(s_whi, 1)

            def q_squares(i, par):
                c = 2 * i + par
                squares(s_q, c + 1, (K_BANK, T_BANK)[par], KEY_TILES + c)

            def q_high(i, par):
                eng.wait_ge(s_qt, 2 * i + par + 1)
                wait(eng, s_qst[par], 32 * i)
                eng.activation(q_part[0][:, par, :, :].rearrange("p g (t n) -> p t g n", n=P),
                               ps[:, V_BANK:V_BANK + 2, :].rearrange("p t (g n) -> p t g n", n=P),
                               ACT.Identity, scale=weights[:, 3:4]).then_inc(s_qhi, 1)

            def high_keys(c):
                at, width = chunk_columns(c)
                eng.wait_ge(shared.s_turn, c + 1)
                eng.activation(shared.keysT[0][:, at:at + width], ps[:, KEYS_BANK + c % 2, 0:width],
                               ACT.Copy).then_inc(shared.s_khi, 1)

            eng.wait_ge(s_k, KEY_TILES)
            q_split(0, 0)
            copy_v(LATENT, 1)
            eng.wait_ge(s_nw, 2)
            q_split(0, 1)
            q_squares(0, 0)
            with eng.Fori(1, Q_PAIRS - 1) as i:
                q_split(i, 0)
                q_squares(i - 1, 1)
                q_high(i - 1, 0)
                q_split(i, 1)
                q_squares(i, 0)
                q_high(i - 1, 1)
            i = Q_PAIRS - 1
            q_split(i, 0)
            for c in range(3):
                high_keys(c)
            q_squares(i - 1, 1)
            q_high(i - 1, 0)
            q_split(i, 1)
            q_squares(i, 0)
            q_high(i - 1, 1)
            for c in range(3, 6):
                high_keys(c)
            q_squares(i, 1)
            q_high(i, 0)
            for c in range(6, CHUNKS):
                high_keys(c)
            q_high(i, 1)

        @block.vector
        def _(eng):
            def split_weights(n):
                eng.wait_ge(s_whi, n + 1)
                part = (wk_part, wv_part)[n // HID_TILES]
                eng.tensor_tensor(part[1][:, n % HID_TILES, :], w_raw[:, n % 2, :],
                                  part[0][:, n % HID_TILES, :].bitcast(F32), ALU.subtract).then_inc(s_wlo, 1)

            def low(i, par):
                wait(eng, s_hi, 2 * i + par + 1)
                eng.tensor_tensor(rowsT[1][:, par, :, :],
                                  ps[:, T_BANK:T_BANK + 2, :].rearrange("p b (k n) -> p (b k) n", n=P),
                                  rowsT[0][:, par, :, :].bitcast(F32), ALU.subtract).then_inc(s_lo, 1)

            def scales(number):
                wait(eng, s_sq, number + 1)
                eng.tensor_reduce(small[:, 0, :], square[:, :].rearrange("p (h d) -> p h d", d=DIM),
                                  AX.X, ALU.add).then_inc(s_sum, 1)
                wait(eng, s_sum, number + 1)
                eng.tensor_scalar(small[:, 1, :], small[:, 0, :], 1.0 / DIM, RMS_EPS,
                                  ALU.mult, ALU.add).then_inc(s_ms, 1)
                wait(eng, s_rms, number + 1)

            def norm(i, par):
                scales(2 * i + par)
                wait(eng, s_kst[par], 16 * i)
                eng.tensor_tensor(k_out[:, par, :].rearrange("p (h d) -> p h d", d=DIM),
                                  ps[:, K_BANK:K_BANK + 2, :].rearrange("p b (h d) -> p (b h) d", d=DIM),
                                  over_last(small[:, 2, :], (P, KV_HEADS, DIM)), ALU.mult).then_inc(s_krow, 1)

            low(0, 0)
            split_weights(0)
            split_weights(1)
            low(0, 1)
            for n in range(2, PIECES):
                split_weights(n)
            eng.wait_ge(s_small, 48)
            eng.tensor_tensor(weights[:, 2:3], weights[:, 0:1], weights[:, 1:2], ALU.mult).then_inc(s_nw, 1)
            eng.wait_ge(s_nw, 1)
            eng.tensor_scalar(weights[:, 3:4], weights[:, 2:3], float(1.0 / np.sqrt(DIM)), None,
                              ALU.mult).then_inc(s_nw, 1)
            layer_norm_statistics(eng, core.x, stats, mv, s_ln, s_var)
            with eng.Fori(0, LAST) as i:
                norm(i, 0)
                low(i + 1, 0)
                norm(i, 1)
                low(i + 1, 1)
            norm(LAST, 0)
            eng.wait_ge(s_rstd, ROW_TILES)
            eng.wait_ge(s_t, CTX_TILES)
            for t in range(ROW_TILES):
                eng.tensor_scalar(rows[:, t, :], core.x[:, t, :], mv[:, t, 0:1], mv[:, t, 3:4],
                                  ALU.subtract, ALU.mult).then_inc(s_ln, 1)
            low(LATENT, 0)
            norm(LAST, 1)
            low(LATENT, 1)
            norm(LATENT, 0)
            norm(LATENT, 1)

            def q_split(i, par):
                for h in range(4):
                    eng.wait_ge(s_whi, PIECES + 4 * (2 * i + par) + h + 1)
                    eng.tensor_tensor(q_piece(wk_part[1], par, h),
                                      w_raw[:, h % 2, :].rearrange("p (k n) -> p k n", n=BANK),
                                      q_piece(wk_part[0], par, h).bitcast(F32), ALU.subtract).then_inc(s_wlo, 1)

            def q_norm(i, par):
                c = 2 * i + par
                bank = (K_BANK, T_BANK)[par]
                scales(KEY_TILES + c)
                wait(eng, s_qt, c - 1)
                eng.tensor_tensor(rows[:, par, :].rearrange("p (h d) -> p h d", d=DIM),
                                  ps[:, bank:bank + 2, :].rearrange("p b (h d) -> p (b h) d", d=DIM),
                                  over_last(small[:, 2, :], (P, KV_HEADS, DIM)), ALU.mult).then_inc(s_qrow, 1)

            def q_low(i, par):
                eng.wait_ge(s_qhi, 2 * i + par + 1)
                for t in range(ROW_TILES):
                    ins = eng.scalar_tensor_tensor(
                        out=q_part[1][:, par, :, t * P:(t + 1) * P],
                        in0=ps[:, V_BANK + t, :].rearrange("p (g n) -> p g n", n=P), scalar=weights[:, 3:4],
                        in1=q_part[0][:, par, :, t * P:(t + 1) * P].bitcast(F32),
                        op0=ALU.mult, op1=ALU.subtract)
                ins.then_inc(s_qlo, 1)

            def low_keys(c):
                at, width = chunk_columns(c)
                eng.wait_ge(shared.s_khi, c + 1)
                eng.tensor_tensor(shared.keysT[1][:, at:at + width], ps[:, KEYS_BANK + c % 2, 0:width],
                                  shared.keysT[0][:, at:at + width].bitcast(F32), ALU.subtract).then_inc(shared.s_klo, 1)

            q_split(0, 0)
            q_split(0, 1)
            q_norm(0, 0)
            with eng.Fori(1, Q_PAIRS - 1) as i:
                q_split(i, 0)
                q_norm(i - 1, 1)
                q_low(i - 1, 0)
                q_split(i, 1)
                q_norm(i, 0)
                q_low(i - 1, 1)
            i = Q_PAIRS - 1
            q_split(i, 0)
            for c in range(3):
                low_keys(c)
            q_norm(i - 1, 1)
            q_low(i - 1, 0)
            q_split(i, 1)
            q_norm(i, 0)
            q_low(i - 1, 1)
            for c in range(3, 6):
                low_keys(c)
            q_norm(i, 1)
            q_low(i, 0)
            for c in range(6, CHUNKS):
                low_keys(c)
            q_low(i, 1)


def cross_attention(core, shared, out, own, q_scratch, k_scratch, v_scratch, o_scratch):
    nc, ps = core.nc, core.psum
    STEPS = KEY_TILES // 2
    UNITS = 2 * CHUNKS
    S_BANK, T_BANK, O_BANK, AUX = 0, 3, 5, 7
    QK_AT = [(2 * s, 2 * s + 1) if s < 4 else (s + 4,) if s < 12 else (16, 17) if s == 12 else () for s in range(STEPS)]
    TURN_AT = {1: 0, 2: 1, 3: 2, 4: 3, 6: 4, 8: 5, 10: 6, 12: 7, 13: 8}
    PROJECT_AT = {3: 0, 6: 1, 9: 2, 12: 3}
    EARLY_EXP = {13: (0, 1), 14: (2,), 15: (3,), 16: (4,)}
    LATE_EXP = {s: (s + 5,) for s in range(UNITS - 5)}
    SUM_AT, SPREAD_AT = 13, 15

    keysT, k_raw, queries = shared.keysT, shared.k_raw, shared.queries
    scores = core.sbuf("scores", [P, 2, ROW_TILES, KEYS], stack=own)
    values = [core.sbuf(f"values_part{n}", [P, KEY_TILES, DIM], F32R, stack=own) for n in range(2)]
    v_raw = core.sbuf("v_raw", [P, KEY_TILES, DIM], stack=own)
    probsT = [core.sbuf(f"probsT_part{n}", [P, 2, 2, ROWS], F32R, stack=own) for n in range(2)]
    o_full = core.sbuf("o_full", [P, 2, ROWS], stack=own)
    o_part = core.sbuf("o_part", [P, 2, 2, ROWS], F32R, stack=own)
    spread = core.sbuf("inverse_sums_spread", [P, ROWS], stack=own)
    diag = core.sbuf("inverse_sums_diagonal", [P, ROW_TILES, P], stack=own)
    unit_max = core.sbuf("unit_max", [P, 2, ROW_TILES, CHUNKS], stack=own)
    minus_max = core.sbuf("minus_max", [P, 2, ROW_TILES], stack=own)
    unit_sum = core.sbuf("unit_sum", [P, 2, ROW_TILES, CHUNKS], stack=own)
    row_sum = core.sbuf("row_sum", [P, 2, ROW_TILES], stack=own)

    s_kraw, s_q, s_turn, s_khi, s_klo = shared.s_kraw, shared.s_q, shared.s_turn, shared.s_khi, shared.s_klo
    s_vraw = core.sem("x_v_loaded")
    s_vhi = core.sem("x_values_hi")
    s_vlo = core.sem("x_values_lo")
    s_qk = core.sem("x_unit_products")
    s_se = core.sem("x_unit_drained")
    s_max = core.sem("x_max")
    s_exp = core.sem("x_exp")
    s_pt = core.sem("x_probs_turned")
    s_phi = core.sem("x_probs_hi")
    s_plo = core.sem("x_probs_lo")
    s_pv = core.sem("x_pv")
    s_sum = core.sem("x_row_sums")
    s_inv = core.sem("x_inverse_sums")
    s_diag = core.sem("x_diagonal")
    s_bc = core.sem("x_spread_product")
    s_spread = core.sem("x_spread")
    s_on = core.sem("x_o_normed")
    s_ohi = core.sem("x_o_hi")
    s_olo = core.sem("x_o_lo")
    s_ost = shared.s_ost

    def heads(eng, body):
        body(0)
        with eng.Fori(1, KV_HEADS - 1) as j:
            body(j)
        body(KV_HEADS - 1)

    def final(j):
        return isinstance(j, int) and j == KV_HEADS - 1

    with nc.Block() as block:
        @block.sync
        def _(eng):
            def load_k(j):
                wait(eng, s_turn, CHUNKS * j)
                eng.dma_start(k_raw[:, :, :], k_scratch[bass.ds(j, 1), :, :, :].rearrange("o p t d -> (o p) t d")).then_inc(s_kraw, 16)

            def load_v(j):
                wait(eng, s_vlo, STEPS * j)
                eng.dma_start(v_raw[:, :, :], v_scratch[bass.ds(j, 1), :, :, :].rearrange("o p t d -> (o p) t d")).then_inc(s_vraw, 16)

            def load_q(j, m):
                wait(eng, s_qk, UNITS * (4 * j + m - 3))
                eng.dma_start(queries[:, m, :, :].bitcast(F32),
                              q_scratch[bass.ds(j, 1), :, :, m, :].rearrange("o p n r -> (o p) n r")).then_inc(s_q[m], 16)

            def store(j, m):
                eng.wait_ge(s_olo, 4 * j + m + 1)
                eng.dma_start(o_scratch[:, bass.ds(4 * j + m, 1), :, :].rearrange("p o n r -> p (o n) r"),
                              o_part[:, m % 2, :, :].bitcast(F32)).then_inc(s_ost[m % 2], 16)

            load_v(0)

            def body(j):
                if not final(j):
                    load_k(j + 1)
                    load_q(j + 1, 0)
                    load_v(j + 1)
                for m in range(GROUP):
                    if m > 0:
                        if not final(j):
                            load_q(j + 1, m)
                        store(j, m - 1)
                    if m == GROUP - 1 and final(j):
                        start_projection()
                store(j, GROUP - 1)
            def start_projection():
                eng.wait_ge(s_qk, UNITS * HEADS)
                for par in range(2):
                    out.load_weights(eng, 0, par)
                for n in range(2):
                    eng.wait_ge(s_ost[n], 32)
                for par in range(2):
                    out.load_outputs(eng, 0, par)

            heads(eng, body)

        @block.gpsimd
        def _(eng):
            ones = core.ones[:, :].unsqueeze(1).broadcast_to([P, 2, P])

            def split_values(j, p):
                at = slice(2 * p, 2 * p + 2)
                wait(eng, s_pv, STEPS * (4 * j - 1) + p + 1)
                if p == 0:
                    wait(eng, s_vraw, 16 * (j + 1))
                eng.tensor_tensor(values[0][:, at, :], v_raw[:, at, :], ones, ALU.mult).then_inc(s_vhi, 1)
                low_values(j, p)

            def low_values(j, p):
                at = slice(2 * p, 2 * p + 2)
                eng.wait_ge(s_vhi, STEPS * j + p + 1)
                eng.tensor_tensor(values[1][:, at, :], v_raw[:, at, :], values[0][:, at, :].bitcast(F32),
                                  ALU.subtract).then_inc(s_vlo, 1)

            def split_output(j, m):
                G = 4 * j + m
                eng.wait_ge(s_on, G + 1)
                wait(eng, s_ost[m % 2], 16 * (2 * j + m // 2))
                eng.tensor_tensor(o_part[:, m % 2, 0, :].rearrange("p (t n) -> p t n", n=P),
                                  o_full[:, m % 2, :].rearrange("p (t n) -> p t n", n=P), ones, ALU.mult).then_inc(s_ohi, 1)
                eng.wait_ge(s_ohi, G + 1)
                eng.tensor_tensor(o_part[:, m % 2, 1, :], o_full[:, m % 2, :],
                                  o_part[:, m % 2, 0, :].bitcast(F32), ALU.subtract).then_inc(s_olo, 1)

            for p in range(STEPS):
                low_values(0, p)

            def body(j):
                for m in range(GROUP - 1):
                    split_output(j, m)
                if not final(j):
                    for p in range(STEPS):
                        split_values(j + 1, p)
                split_output(j, GROUP - 1)
            heads(eng, body)

        @block.tensor
        def _(eng):
            def turn_keys(j, c):
                at, width = chunk_columns(c)
                if c == 0:
                    eng.wait_ge(s_kraw, 16 * (j + 1))
                    wait(eng, s_spread, 4 * j - 2)
                else:
                    eng.wait_ge(s_klo, CHUNKS * j + c)
                for k in range(width // P):
                    mm = eng.transpose(ps[:, AUX, k * P:(k + 1) * P], k_raw[:, at // P + k, :], core.ident[:, :])
                mm.then_inc(s_turn, 1)

            def unit(j, m, n):
                at, width = chunk_columns(n // 2)
                if n == 0:
                    eng.wait_ge(s_q[m], 16 * (j + 1))
                if m == 0 and n % 2 == 0:
                    eng.wait_ge(s_klo, CHUNKS * j + n // 2 + 1)
                wait(eng, s_se, UNITS * (4 * j + m) + n - 2)
                for i, (s, k) in enumerate(PASSES):
                    mm = eng.matmul(ps[:, S_BANK + n % 3, 0:width], queries[:, m, s, (n % 2) * P:(n % 2 + 1) * P],
                                    keysT[k][:, at:at + width], start=(i == 0), stop=(i == 2))
                mm.then_inc(s_qk, 1)

            def turn_probs(j, m, p):
                index = STEPS * (4 * j + m) + p
                bank = T_BANK + (m + p) % 2
                if p % 2 == 0:
                    eng.wait_ge(s_exp, UNITS * (4 * j + m) + p + 2)
                wait(eng, s_plo, index - 1)
                for k in range(2):
                    for r in range(ROW_TILES):
                        mm = eng.transpose(ps[:, bank, k * ROWS + r * P:k * ROWS + (r + 1) * P],
                                           scores[:, m % 2, r, (2 * p + k) * P:(2 * p + k + 1) * P], core.ident[:, :])
                mm.then_inc(s_pt, 1)

            def weigh_values(j, m, p):
                index = STEPS * (4 * j + m) + p
                eng.wait_ge(s_plo, index + 1)
                if m == 0:
                    eng.wait_ge(s_vlo, STEPS * j + p + 1)
                if p == 0:
                    wait(eng, s_on, 4 * j + m - 1)
                for k in range(2):
                    for i, (s, v) in enumerate(PASSES):
                        mm = eng.matmul(ps[:, O_BANK + m % 2, 0:ROWS], values[s][:, 2 * p + k, :],
                                        probsT[v][:, (m + p) % 2, k, :],
                                        start=(p == 0 and k == 0 and i == 0),
                                        stop=(p == STEPS - 1 and k == 1 and i == 2))
                mm.then_inc(s_pv, 1)

            def spread_sums(j, m):
                G = 4 * j + m
                eng.wait_ge(s_diag, G + 1)
                wait(eng, s_spread, G)
                if m == 2 and not final(j):
                    eng.wait_ge(s_klo, CHUNKS * (j + 2))
                eng.matmul(ps[:, AUX, 0:ROWS], core.ones[:, :], diag[:, :, :].rearrange("p t n -> p (t n)"),
                           start=True, stop=True).then_inc(s_bc, 1)

            for n in range(UNITS):
                unit(0, 0, n)
            turn_probs(0, 0, 0)

            def body(j):
                for m in range(GROUP):
                    more = not (final(j) and m == GROUP - 1)
                    j1, m1 = (j, m + 1) if m < GROUP - 1 else (j + 1, 0)
                    for p in range(STEPS):
                        if p < STEPS - 1:
                            turn_probs(j, m, p + 1)
                        elif more:
                            turn_probs(j1, m1, 0)
                        if more:
                            for n in QK_AT[p]:
                                unit(j1, m1, n)
                        if m == 2 and not final(j) and p in TURN_AT:
                            turn_keys(j + 1, TURN_AT[p])
                        if p == SPREAD_AT:
                            spread_sums(j, m)
                        weigh_values(j, m, p)
            heads(eng, body)

        @block.scalar
        def _(eng):
            def high_keys(j, c):
                at, width = chunk_columns(c)
                eng.wait_ge(s_turn, CHUNKS * j + c + 1)
                eng.activation(keysT[0][:, at:at + width], ps[:, AUX, 0:width], ACT.Copy).then_inc(s_khi, 1)

            def exponential(j, m, n):
                at, width = chunk_columns(n // 2)
                r, c = n % 2, n // 2
                if n == 0:
                    eng.wait_ge(s_max, 4 * j + m + 1)
                    wait(eng, s_sum, 4 * j + m - 1)
                eng.activation(scores[:, m % 2, r, at:at + width], scores[:, m % 2, r, at:at + width], ACT.Exp,
                               bias=minus_max[:, m % 2, r:r + 1],
                               accum_out=unit_sum[:, m % 2, r, c:c + 1]).then_inc(s_exp, 1)

            def high_probs(j, m, p):
                index = STEPS * (4 * j + m) + p
                eng.wait_ge(s_pt, index + 1)
                wait(eng, s_pv, index - 1)
                eng.activation(probsT[0][:, (m + p) % 2, :, :],
                               ps[:, T_BANK + (m + p) % 2, :].rearrange("p (k r) -> p k r", r=ROWS),
                               ACT.Copy).then_inc(s_phi, 1)

            def copy_spread(j, m):
                eng.wait_ge(s_bc, 4 * j + m + 1)
                wait(eng, s_on, 4 * j + m)
                eng.activation(spread[:, :], ps[:, AUX, 0:ROWS], ACT.Copy).then_inc(s_spread, 1)

            eng.wait_ge(s_vraw, 16)
            for p in range(STEPS):
                eng.activation(values[0][:, 2 * p:2 * p + 2, :], v_raw[:, 2 * p:2 * p + 2, :], ACT.Copy).then_inc(s_vhi, 1)
            for n in range(5):
                exponential(0, 0, n)
            high_probs(0, 0, 0)

            def body(j):
                for m in range(GROUP):
                    more = not (final(j) and m == GROUP - 1)
                    j1, m1 = (j, m + 1) if m < GROUP - 1 else (j + 1, 0)
                    for p in range(STEPS):
                        if p < STEPS - 1:
                            high_probs(j, m, p + 1)
                        elif more:
                            high_probs(j1, m1, 0)
                        for n in LATE_EXP.get(p, ()):
                            exponential(j, m, n)
                        if more:
                            for n in EARLY_EXP.get(p, ()):
                                exponential(j1, m1, n)
                        if m == 2 and not final(j) and p in TURN_AT:
                            high_keys(j + 1, TURN_AT[p])
                        if m == GROUP - 1 and final(j) and p in PROJECT_AT:
                            out.high(eng, 0, PROJECT_AT[p] // 2, PROJECT_AT[p] % 2)
                        if p == SPREAD_AT:
                            copy_spread(j, m)
            heads(eng, body)

        @block.vector
        def _(eng):
            def low_keys(j, c):
                at, width = chunk_columns(c)
                eng.wait_ge(s_khi, CHUNKS * j + c + 1)
                eng.tensor_tensor(keysT[1][:, at:at + width], ps[:, AUX, 0:width],
                                  keysT[0][:, at:at + width].bitcast(F32), ALU.subtract).then_inc(s_klo, 1)

            def drain_unit(j, m, n):
                at, width = chunk_columns(n // 2)
                r, c = n % 2, n // 2
                G = 4 * j + m
                eng.wait_ge(s_qk, UNITS * G + n + 1)
                if n == 0:
                    wait(eng, s_pt, STEPS * (G - 1))
                eng.tensor_scalar(scores[:, m % 2, r, at:at + width], ps[:, S_BANK + n % 3, 0:width], 1.0, None,
                                  ALU.mult, ALU.max, accum_out=unit_max[:, m % 2, r, c:c + 1]).then_inc(s_se, 1)

            def maximum(j, m):
                G = 4 * j + m
                eng.wait_ge(s_se, UNITS * (G + 1))
                wait(eng, s_exp, UNITS * (G - 1))
                eng.tensor_reduce(minus_max[:, m % 2, :], unit_max[:, m % 2, :, :], AX.X, ALU.max,
                                  negate=True).then_inc(s_max, 1)

            def low_probs(j, m, p):
                index = STEPS * (4 * j + m) + p
                eng.wait_ge(s_phi, index + 1)
                eng.tensor_tensor(probsT[1][:, (m + p) % 2, :, :],
                                  ps[:, T_BANK + (m + p) % 2, :].rearrange("p (k r) -> p k r", r=ROWS),
                                  probsT[0][:, (m + p) % 2, :, :].bitcast(F32), ALU.subtract).then_inc(s_plo, 1)

            def invert_sums(j, m):
                G = 4 * j + m
                eng.wait_ge(s_exp, UNITS * (G + 1))
                eng.tensor_reduce(row_sum[:, 0, :], unit_sum[:, m % 2, :, :], AX.X, ALU.add).then_inc(s_sum, 1)
                eng.wait_ge(s_sum, G + 1)
                eng.reciprocal(row_sum[:, 1, :], row_sum[:, 0, :]).then_inc(s_inv, 1)
                eng.wait_ge(s_inv, G + 1)
                wait(eng, s_bc, G)
                for r in range(ROW_TILES):
                    ins = eng.tensor_scalar(diag[:, r, :], core.ident[:, :], row_sum[:, 1, r:r + 1], None, ALU.mult)
                ins.then_inc(s_diag, 1)

            def norm_output(j, m):
                G = 4 * j + m
                eng.wait_ge(s_pv, STEPS * (G + 1))
                eng.wait_ge(s_spread, G + 1)
                wait(eng, s_olo, G - 1)
                eng.tensor_tensor(o_full[:, m % 2, :], ps[:, O_BANK + m % 2, 0:ROWS], spread[:, :],
                                  ALU.mult).then_inc(s_on, 1)

            for n in range(UNITS):
                drain_unit(0, 0, n)
            maximum(0, 0)
            low_probs(0, 0, 0)

            def body(j):
                for m in range(GROUP):
                    more = not (final(j) and m == GROUP - 1)
                    j1, m1 = (j, m + 1) if m < GROUP - 1 else (j + 1, 0)
                    for p in range(STEPS):
                        if p < STEPS - 1:
                            low_probs(j, m, p + 1)
                        elif more:
                            low_probs(j1, m1, 0)
                        if p == 0 and m > 0:
                            norm_output(j, m - 1)
                        if more:
                            for n in QK_AT[p]:
                                drain_unit(j1, m1, n)
                            if p == 12:
                                maximum(j1, m1)
                        if m == 2 and not final(j) and p in TURN_AT:
                            low_keys(j + 1, TURN_AT[p])
                        if m == GROUP - 1 and final(j) and p in PROJECT_AT:
                            out.low(eng, 0, PROJECT_AT[p] // 2, PROJECT_AT[p] % 2)
                        if p == SUM_AT:
                            invert_sums(j, m)
                norm_output(j, GROUP - 1)
            heads(eng, body)


class SelfBuffers:
    QKV = HID + 2 * KV_HEADS * SELF_DIM
    QK = HID + KV_HEADS * SELF_DIM
    TURNED = HID // (GROUP * SELF_DIM)

    def __init__(self, core, stack):
        QK, QKV, TURNED = self.QK, self.QKV, self.TURNED
        self.turned = core.sbuf("a_rope_products", [P, 4, QK // 2], stack=stack)
        self.qk = core.sbuf("a_qk_rows", [P, ROW_TILES, QK], stack=stack)
        self.k_copies = core.sbuf("a_k_copies", [P, ROW_TILES, KV_HEADS, GROUP, SELF_DIM], stack=stack)
        self.qT = core.sbuf("a_qT", [P, TURNED, ROWS], stack=stack)
        self.kT = core.sbuf("a_kT", [P, TURNED, ROWS], stack=stack)
        self.normed = core.sbuf("a_xn", [P, ROW_TILES, HID], stack=stack)
        self.xT = [core.sbuf(f"a_xnT_part{n}", [P, HID_TILES, ROWS], F32R, stack=stack) for n in range(2)]
        self.w_raw = core.sbuf("a_w_raw", [P, 2, HID], stack=stack)
        self.w_part = [core.sbuf(f"a_w_part{n}", [P, HID_TILES, QKV], F32R, stack=stack) for n in range(2)]
        self.tables = core.sbuf("a_rope_tables", [P, ROW_TILES, 2, SELF_DIM // 2], stack=stack)
        self.mask = core.sbuf("a_mask", [P, P], stack=stack)
        self.stats = core.sbuf("a_ln_stats", [P, ROW_TILES, 2, 6], stack=stack)
        self.mv = core.sbuf("a_ln_mv", [P, ROW_TILES, 4], stack=stack)
        self.v = core.sbuf("a_v_rows", [P, ROW_TILES, KV_HEADS * SELF_DIM], stack=stack)
        self.scores = core.sbuf("a_scores", [P, 3, GROUP, ROWS], stack=stack)
        self.probsT = core.sbuf("a_probsT", [P, 2, 2, BANK], stack=stack)
        self.stepT = core.sbuf("a_step_outT", [P, 2, P], stack=stack)
        self.small = core.sbuf("a_small", [P, ROW_TILES * KV_HEADS, 4, GROUP], stack=stack)
        self.s_w = core.sem("a_qkv_weights_loaded")
        self.s_whi = core.sem("a_qkv_weights_hi")
        self.s_wlo = core.sem("a_qkv_weights_lo")
        self.s_x = core.sem("a_tables_loaded")


def project_attention(core, a, shared, out, own):
    nc, ps = core.nc, core.psum
    PAIRS = HEADS // out.HEADS // 2
    KV = KV_HEADS * SELF_DIM
    s_mm = core.sem("p_products")
    piece = own.w_raw[:, :, :].rearrange("p two n -> p (two n)")[:, 0:own.QKV].unsqueeze(1)

    with nc.Block() as block:
        @block.sync
        def _(eng):
            def load(i, par):
                c = 2 * i + par
                eng.wait_ge(out.s_wlo, out.HEADS * (c - 1))
                out.load_weights(eng, i, par)
                eng.wait_ge(s_mm, c - 1)
                for n in range(2):
                    eng.wait_ge(shared.s_ost[n], 16 * (c + 1))
                out.load_outputs(eng, i, par)

            def load_piece(k):
                wait(eng, own.s_wlo, k)
                for w, at, n in (("wq", 0, HID), ("wk", HID, KV), ("wv", HID + KV, KV)):
                    eng.dma_start(piece[:, 0, at:at + n],
                                  a[w].rearrange("(k p) n -> p k n", p=P)[:, bass.ds(k, 1), :]
                                  .rearrange("p o n -> p (o n)")).then_inc(own.s_w, 16)

            for n in range(2):
                eng.wait_ge(shared.s_ost[n], 16 * HEADS // 2)
            eng.dma_start(own.tables[:, :, :, :], a["rope"].rearrange("(t p) c n -> p t c n", p=P)).then_inc(own.s_x, 16)
            eng.dma_start(own.mask[:, :], a["mask"]).then_inc(own.s_x, 16)
            load_piece(0)
            with eng.Fori(1, PAIRS) as i:
                load(i, 0)
                load(i, 1)
                load_piece(i)

        @block.tensor
        def _(eng):
            def products(i, par):
                c = 2 * i + par
                eng.wait_ge(out.s_o[par], 16 * (i + 1))
                first = isinstance(i, int) and c == 0
                last = isinstance(i, int) and c == 2 * PAIRS - 1
                for g in range(out.HEADS):
                    eng.wait_ge(out.s_wlo, out.HEADS * c + g + 1)
                    for t in range(ROW_TILES):
                        for n, (s, m) in enumerate(PASSES):
                            for half in range(2):
                                mm = eng.matmul(ps[:, 2 * t + half, :], out.outT[:, par, g, s, t * P:(t + 1) * P],
                                                out.w_part[m][:, par, g, half * BANK:(half + 1) * BANK],
                                                start=(first and g == 0 and n == 0),
                                                stop=(last and g == out.HEADS - 1 and n == 2))
                mm.then_inc(s_mm, 1)
            products(0, 0)
            products(0, 1)
            with eng.Fori(1, PAIRS - 1) as i:
                products(i, 0)
                products(i, 1)
            products(PAIRS - 1, 0)
            products(PAIRS - 1, 1)

        @block.scalar
        def _(eng):
            def split(i, par):
                eng.wait_ge(s_mm, 2 * i + par - 1)
                for g in range(out.HEADS):
                    out.high(eng, i, par, g)

            def split_piece(k):
                eng.wait_ge(own.s_w, 48 * (k + 1))
                eng.activation(own.w_part[0][:, bass.ds(k, 1), :], piece, ACT.Copy).then_inc(own.s_whi, 1)

            split_piece(0)
            with eng.Fori(1, PAIRS) as i:
                split(i, 0)
                split(i, 1)
                split_piece(i)

        @block.vector
        def _(eng):
            def split(i, par):
                for g in range(out.HEADS):
                    out.low(eng, i, par, g)

            def split_piece(k):
                eng.wait_ge(own.s_whi, k + 1)
                eng.tensor_tensor(own.w_part[1][:, bass.ds(k, 1), :], piece,
                                  own.w_part[0][:, bass.ds(k, 1), :].bitcast(F32), ALU.subtract).then_inc(own.s_wlo, 1)

            split_piece(0)
            with eng.Fori(1, PAIRS) as i:
                split(i, 0)
                split(i, 1)
                split_piece(i)
            eng.wait_ge(s_mm, 2 * PAIRS)
            for t in range(ROW_TILES):
                eng.tensor_tensor(core.x[:, t, :].rearrange("p (b n) -> p b n", n=BANK),
                                  ps[:, 2 * t:2 * t + 2, :],
                                  core.x[:, t, :].rearrange("p (b n) -> p b n", n=BANK), ALU.add)


def self_attention(core, a, own):
    nc, ps = core.nc, core.psum
    QKV, QK = own.QKV, own.QK
    STEPS = ROW_TILES * KV_HEADS
    SCALE = float(1.0 / np.sqrt(SELF_DIM))
    HALF = SELF_DIM // 2
    normed, xT, w_raw, w_part, turned, qk, v = own.normed, own.xT, own.w_raw, own.w_part, own.turned, own.qk, own.v
    k_copies, qT, kT, scores, probsT, small = own.k_copies, own.qT, own.kT, own.scores, own.probsT, own.small
    tables, mask, stats, mv = own.tables, own.mask, own.stats, own.mv

    s_w = [core.sem(f"a_w_loaded{n}") for n in range(2)]
    s_whi = core.sem("a_w_hi")
    s_wlo = core.sem("a_w_lo")
    s_ln = core.sem("a_ln_steps")
    s_var = core.sem("a_var_ready")
    s_rstd = core.sem("a_rstd_ready")
    s_t = core.sem("a_transposed")
    s_hi = core.sem("a_hi")
    s_lo = core.sem("a_lo")
    s_mm = core.sem("a_products")
    s_v = core.sem("a_v_rows_ready")
    s_rp = core.sem("a_rope_products_ready")
    s_rope = core.sem("a_rope_ready")
    s_kc = core.sem("a_k_copied")
    s_qt = core.sem("a_qk_turned")
    s_qta = core.sem("a_qT_ready")
    s_kta = core.sem("a_kT_ready")
    s_s = core.sem("a_scores_product")
    s_masked = core.sem("a_masked")
    s_mx = core.sem("a_max")
    s_nm = core.sem("a_minus_max")
    s_exp = core.sem("a_exp")
    s_pt = core.sem("a_probs_turned")
    s_pa = core.sem("a_probsT")
    s_pv = core.sem("a_pv")
    s_oc = core.sem("a_out_copied")
    s_ot = core.sem("a_out_turned")
    s_inv = core.sem("a_inverse")
    s_out = core.sem("a_out_rows")

    def width(x):
        return P * (x // KV_HEADS + 1)

    SECOND_AT = (2, 3, 4, 5)

    with nc.Block() as block:
        @block.sync
        def _(eng):
            for k in range(HID_TILES):
                wait(eng, s_wlo, k - 1)
                eng.dma_start(w_raw[:, k % 2, 0:HID], a["wo"][k * P:(k + 1) * P, :]).then_inc(s_w[k % 2], 16)

        @block.gpsimd
        def _(eng):
            layer_norm_pool(eng, core, mv, s_var, s_rstd)
            for t in range(ROW_TILES):
                pair = qk[:, t, :].rearrange("p (n two) -> p n two", two=2)
                eng.wait_ge(s_rp, 4 * t + 4)
                eng.tensor_tensor(pair[:, :, 0], turned[:, 0, :], turned[:, 1, :], ALU.subtract)
                eng.tensor_tensor(pair[:, :, 1], turned[:, 2, :], turned[:, 3, :], ALU.add).then_inc(s_rope, 1)

        @block.tensor
        def _(eng):
            def turn_rows(src, t, bank):
                for k in range(HID_TILES):
                    mm = eng.transpose(ps[:, bank + k // 4, (k % 4) * P:(k % 4 + 1) * P],
                                       src[:, t, k * P:(k + 1) * P], core.ident[:, :])
                return mm

            for t in range(ROW_TILES):
                eng.wait_ge(s_ln, 7 + t)
                turn_rows(normed, t, 2 * t).then_inc(s_t, 1)
            eng.wait_ge(s_lo, ROW_TILES)
            for t in range(ROW_TILES):
                for k in range(HID_TILES):
                    for n, (s, m) in enumerate(PASSES):
                        for b in range(QKV // BANK):
                            mm = eng.matmul(ps[:, 3 * t + b, :], xT[s][:, k, t * P:(t + 1) * P],
                                            w_part[m][:, k, b * BANK:(b + 1) * BANK],
                                            start=(k == 0 and n == 0), stop=(k == HID_TILES - 1 and n == 2))
                mm.then_inc(s_mm, 1)
            eng.wait_ge(s_rope, 1)
            turn_rows(qk, 0, 6).then_inc(s_qt, 1)
            eng.wait_ge(s_kc, 1)
            eng.wait_ge(s_rp, 4)
            eng.wait_ge(s_v, 1)
            copies = k_copies[:, :, :, :, :].rearrange("p t j g d -> p t (j g d)")
            turn_rows(copies, 0, 0).then_inc(s_qt, 1)

            def turn_second(n):
                if n == 0:
                    eng.wait_ge(s_v, 2)
                    eng.wait_ge(s_rope, 2)
                elif n == 2:
                    eng.wait_ge(s_kc, 2)
                wait(eng, s_qta, (1, 2, 3, 3)[n])
                wait(eng, s_kta, (0, 0, 0, 2)[n])
                for k in range(GROUP):
                    src = (qk, copies)[n // 2]
                    at = (n % 2) * BANK + k * P
                    mm = eng.transpose(ps[:, 5, k * P:(k + 1) * P], src[:, 1, at:at + P], core.ident[:, :])
                mm.then_inc(s_qt, 1)

            def score(x):
                t, j = x // KV_HEADS, x % KV_HEADS
                wait(eng, s_masked, x)
                for r in range(GROUP):
                    at = slice(r * SELF_DIM, (r + 1) * SELF_DIM)
                    mm = eng.matmul(ps[:, r, 0:width(x)],
                                    qT[at, j, t * P:(t + 1) * P], kT[at, j, 0:width(x)], start=True, stop=True)
                mm.then_inc(s_s, 1)

            def turn_probs(x):
                eng.wait_ge(s_exp, x + 1)
                wait(eng, s_pa, x)
                for k in range(x // KV_HEADS + 1):
                    for r in range(GROUP):
                        mm = eng.transpose(ps[:, 4 + k, r * P:(r + 1) * P],
                                           scores[:, x % 3, r, k * P:(k + 1) * P], core.ident[:, :])
                mm.then_inc(s_pt, 1)

            def weigh(x):
                t, j = x // KV_HEADS, x % KV_HEADS
                eng.wait_ge(s_pa, x + 1)
                wait(eng, s_out, x - 1)
                for r in range(GROUP):
                    for k in range(t + 1):
                        mm = eng.matmul(ps[r * SELF_DIM:(r + 1) * SELF_DIM, 6 + x % 2, 0:P],
                                        v[:, k, j * SELF_DIM:(j + 1) * SELF_DIM],
                                        probsT[:, x % 2, k, r * P:(r + 1) * P], start=(k == 0), stop=(k == t))
                mm.then_inc(s_pv, 1)

            def turn_out(x):
                eng.wait_ge(s_oc, x + 1)
                eng.transpose(ps[:, 6 + x % 2, P:2 * P], own.stepT[:, x % 2, :], core.ident[:, :]).then_inc(s_ot, 1)

            def project(t, bank):
                eng.wait_ge(s_lo, ROW_TILES + t + 1)
                for k in range(HID_TILES):
                    eng.wait_ge(s_wlo, k + 1)
                    for n, (s, m) in enumerate(PASSES):
                        for half in range(2):
                            mm = eng.matmul(ps[:, bank + half, :], xT[s][:, k, t * P:(t + 1) * P],
                                            w_part[m][:, k, half * BANK:(half + 1) * BANK],
                                            start=(k == 0 and n == 0), stop=(k == HID_TILES - 1 and n == 2))
                mm.then_inc(s_mm, 1)

            eng.wait_ge(s_qta, 1)
            eng.wait_ge(s_kta, 1)
            eng.wait_ge(s_rp, 8)
            eng.wait_ge(s_v, ROW_TILES)
            score(0)
            score(1)
            for x in range(STEPS):
                if x in SECOND_AT:
                    turn_second(SECOND_AT.index(x))
                if x + 2 == KV_HEADS:
                    eng.wait_ge(s_qta, 3)
                    eng.wait_ge(s_kta, 3)
                if x + 2 < STEPS:
                    score(x + 2)
                turn_probs(x)
                if x > 0:
                    weigh(x - 1)
                if x > 1:
                    turn_out(x - 2)
            eng.wait_ge(s_out, KV_HEADS)
            eng.wait_ge(s_masked, STEPS)
            turn_rows(normed, 0, 0).then_inc(s_t, 1)
            weigh(STEPS - 1)
            turn_out(STEPS - 2)
            turn_out(STEPS - 1)
            project(0, 2)
            eng.wait_ge(s_out, STEPS)
            turn_rows(normed, 1, 4).then_inc(s_t, 1)
            project(1, 6)

        @block.scalar
        def _(eng):
            def split(k):
                eng.wait_ge(s_w[k % 2], 16 * (k // 2 + 1))
                eng.activation(w_part[0][:, k, 0:HID], w_raw[:, k % 2, 0:HID], ACT.Copy).then_inc(s_whi, 1)

            def high(t, count, bank):
                eng.wait_ge(s_t, count)
                eng.activation(xT[0][:, :, t * P:(t + 1) * P],
                               ps[:, bank:bank + 2, :].rearrange("p b (k n) -> p (b k) n", n=P),
                               ACT.Copy).then_inc(s_hi, 1)

            def copy_keys(t):
                eng.wait_ge(s_rope, t + 1)
                eng.activation(k_copies[:, t, :, :, :],
                               qk[:, t, HID:QK].rearrange("p (j d) -> p j d", d=SELF_DIM).unsqueeze(2)
                               .broadcast_to([P, KV_HEADS, GROUP, SELF_DIM]), ACT.Copy).then_inc(s_kc, 1)

            for t in range(ROW_TILES):
                high(t, t + 1, 2 * t)
            for t in range(ROW_TILES):
                eng.wait_ge(s_mm, t + 1)
                eng.activation(v[:, t, :], ps[:, 3 * t + 2, QK - 2 * BANK:BANK], ACT.Copy).then_inc(s_v, 1)
                if t == 0:
                    copy_keys(0)
            eng.wait_ge(s_qt, 1)
            eng.activation(qT[:, :, 0:P], ps[:, 6:8, :].rearrange("p b (k n) -> p (b k) n", n=P),
                           ACT.Copy).then_inc(s_qta, 1)
            def exponential(x):
                eng.wait_ge(s_nm, x + 1)
                for r in range(GROUP):
                    ins = eng.activation(scores[:, x % 3, r, 0:width(x)], scores[:, x % 3, r, 0:width(x)], ACT.Exp,
                                         scale=SCALE, bias=small[:, x, 1, r:r + 1],
                                         accum_out=small[:, x, 2, r:r + 1])
                ins.then_inc(s_exp, 1)

            def copy_out(x):
                eng.wait_ge(s_pv, x + 1)
                wait(eng, s_ot, x - 1)
                eng.activation(own.stepT[:, x % 2, :], ps[:, 6 + x % 2, 0:P], ACT.Copy).then_inc(s_oc, 1)

            exponential(0)
            for x in range(STEPS):
                if x + 1 < STEPS:
                    exponential(x + 1)
                eng.wait_ge(s_pt, x + 1)
                wait(eng, s_pv, x - 1)
                tiles = x // KV_HEADS + 1
                eng.activation(probsT[:, x % 2, 0:tiles, :], ps[:, 4:4 + tiles, :], ACT.Copy).then_inc(s_pa, 1)
                if x > 0:
                    copy_out(x - 1)
                if x == SECOND_AT[0]:
                    copy_keys(1)
                if x + 1 in SECOND_AT[:2]:
                    half = SECOND_AT.index(x + 1)
                    eng.wait_ge(s_qt, 3 + half)
                    eng.activation(qT[:, GROUP * half:GROUP * (half + 1), P:ROWS],
                                   ps[:, 5, :].rearrange("p (k n) -> p k n", n=P), ACT.Copy).then_inc(s_qta, 1)
                if x % 2:
                    split(x // 2)
            high(0, ROW_TILES + 1, 0)
            copy_out(STEPS - 1)
            high(1, ROW_TILES + 2, 4)

        @block.vector
        def _(eng):
            def split(k):
                eng.wait_ge(s_whi, k + 1)
                eng.tensor_tensor(w_part[1][:, k, 0:HID], w_raw[:, k % 2, 0:HID],
                                  w_part[0][:, k, 0:HID].bitcast(F32), ALU.subtract).then_inc(s_wlo, 1)

            def low(t, count, bank):
                eng.wait_ge(s_hi, count)
                eng.tensor_tensor(xT[1][:, :, t * P:(t + 1) * P],
                                  ps[:, bank:bank + 2, :].rearrange("p b (k n) -> p (b k) n", n=P),
                                  xT[0][:, :, t * P:(t + 1) * P].bitcast(F32), ALU.subtract).then_inc(s_lo, 1)

            layer_norm_vector(eng, core, core.x, normed, stats, mv, s_ln, s_var, s_rstd)
            for t in range(ROW_TILES):
                low(t, t + 1, 2 * t)
            eng.wait_ge(own.s_x, 32)
            for t in range(ROW_TILES):
                eng.wait_ge(s_mm, t + 1)
                rows = ps[:, 3 * t:3 * t + 3, :].rearrange("p b n -> p (b n)")[:, 0:QK]
                pair = rows.rearrange("p (h n two) -> p h n two", n=HALF, two=2)
                wait(eng, s_rope, t)
                eng.wait_ge(s_v, t + 1)
                for n, (odd, sine) in enumerate(((0, 0), (1, 1), (0, 1), (1, 0))):
                    table = tables[:, t, sine, :].unsqueeze(1).broadcast_to([P, QK // SELF_DIM, HALF])
                    eng.tensor_tensor(turned[:, n, :].rearrange("p (h n) -> p h n", n=HALF), pair[:, :, :, odd],
                                      table, ALU.mult).then_inc(s_rp, 1)
            eng.wait_ge(s_qt, 2)
            eng.tensor_copy(kT[:, :, 0:P], ps[:, 0:2, :].rearrange("p b (k n) -> p (b k) n", n=P)).then_inc(s_kta, 1)

            def maximum(x):
                w = width(x)
                eng.wait_ge(s_s, x + 1)
                wait(eng, s_pt, x - 2)
                if x >= KV_HEADS:
                    eng.tensor_copy(scores[:, x % 3, :, 0:P], ps[:, 0:GROUP, 0:P])
                eng.tensor_tensor(scores[:, x % 3, :, w - P:w], ps[:, 0:GROUP, w - P:w],
                                  mask[:, :].unsqueeze(1).broadcast_to([P, GROUP, P]), ALU.add).then_inc(s_masked, 1)
                eng.wait_ge(s_masked, x + 1)
                eng.tensor_reduce(small[:, x, 0, :], scores[:, x % 3, :, 0:w], AX.X, ALU.max).then_inc(s_mx, 1)
                eng.wait_ge(s_mx, x + 1)
                eng.tensor_scalar(small[:, x, 1, :], small[:, x, 0, :], -SCALE, None, ALU.mult).then_inc(s_nm, 1)

            def norm(x):
                t, j = x // KV_HEADS, x % KV_HEADS
                eng.wait_ge(s_exp, x + 1)
                eng.reciprocal(small[:, x, 3, :], small[:, x, 2, :]).then_inc(s_inv, 1)
                eng.wait_ge(s_inv, x + 1)
                eng.wait_ge(s_ot, x + 1)
                eng.tensor_tensor(normed[:, t, j * P:(j + 1) * P].rearrange("p (g d) -> p g d", d=SELF_DIM),
                                  ps[:, 6 + x % 2, P:2 * P].rearrange("p (g d) -> p g d", d=SELF_DIM),
                                  over_last(small[:, x, 3, :], (P, GROUP, SELF_DIM)), ALU.mult).then_inc(s_out, 1)

            maximum(0)
            maximum(1)
            for x in range(STEPS):
                if x in SECOND_AT[2:]:
                    half = SECOND_AT.index(x) - 2
                    eng.wait_ge(s_qt, 5 + half)
                    eng.tensor_copy(kT[:, GROUP * half:GROUP * (half + 1), P:ROWS],
                                    ps[:, 5, :].rearrange("p (k n) -> p k n", n=P)).then_inc(s_kta, 1)
                if x + 2 < STEPS:
                    maximum(x + 2)
                if x > 1:
                    norm(x - 2)
                if x % 2:
                    split(x // 2)
            low(0, ROW_TILES + 1, 0)
            norm(STEPS - 2)
            norm(STEPS - 1)
            low(1, ROW_TILES + 2, 4)
            for t in range(ROW_TILES):
                eng.wait_ge(s_mm, ROW_TILES + t + 1)
                eng.tensor_tensor(core.x[:, t, :].rearrange("p (b n) -> p b n", n=BANK),
                                  ps[:, 2 + 4 * t:4 + 4 * t, :],
                                  core.x[:, t, :].rearrange("p (b n) -> p b n", n=BANK), ALU.add)


def feed_forward(core, a, out):
    nc, ps = core.nc, core.psum
    NR = LORAS * RANK
    A_TILES = NR // P
    with ExitStack() as own:
        raw = [core.sbuf(f"f_raw{n}", [P, HID_TILES, BANK], stack=own) for n in range(2)]
        a_shared = core.sbuf("f_a_shared", [RANK, HID], stack=own)
        b_shared = core.sbuf("f_b_shared", [P, HID_TILES, RANK], stack=own)
        aT = [core.sbuf(f"f_aT_part{n}", [P, HID_TILES, NR], F32R, stack=own) for n in range(2)]
        asT = [core.sbuf(f"f_asT_part{n}", [P, HID_TILES, RANK], F32R, stack=own) for n in range(2)]
        bT = [core.sbuf(f"f_bT_part{n}", [P, A_TILES, HID], F32R, stack=own) for n in range(2)]
        bsT = [core.sbuf(f"f_bsT_part{n}", [RANK, HID], F32R, stack=own) for n in range(2)]
        w_part = [core.sbuf(f"f_w_part{n}", [P, HID_TILES, BANK], F32R, stack=own) for n in range(2)]
        normed = core.sbuf("f_xn", [P, ROW_TILES, HID], stack=own)
        stats = core.sbuf("f_ln_stats", [P, ROW_TILES, 2, 6], stack=own)
        mv = core.sbuf("f_ln_mv", [P, ROW_TILES, 4], stack=own)
        xT = [core.sbuf(f"f_xnT_part{n}", [P, HID_TILES, ROWS], F32R, stack=own) for n in range(2)]
        gates = core.sbuf("f_gates", [P, ROW_TILES, LORAS], stack=own)
        bias = core.sbuf("f_bias", [P, HID], stack=own)
        z = core.sbuf("f_z", [P, ROW_TILES, NR + RANK], stack=own)
        zT = [core.sbuf(f"f_zT_part{n}", [P, ROW_TILES, NR], F32R, stack=own) for n in range(2)]
        zsT = [core.sbuf(f"f_zsT_part{n}", [RANK, ROWS], F32R, stack=own) for n in range(2)]

        s_a = core.sem("f_a_loaded")
        s_b = core.sem("f_b_loaded")
        s_small = core.sem("f_gates_bias_loaded")
        s_w = [core.sem(f"f_w_loaded{n}") for n in range(2)]
        s_t = core.sem("f_adapters_turned")
        s_hi = core.sem("f_adapters_hi")
        s_lo = core.sem("f_adapters_lo")
        s_whi = core.sem("f_w_hi")
        s_wlo = core.sem("f_w_lo")
        s_ln = core.sem("f_ln_steps")
        s_var = core.sem("f_var_ready")
        s_rstd = core.sem("f_rstd_ready")
        s_xt = core.sem("f_xn_turned")
        s_xhi = core.sem("f_xn_hi")
        s_xlo = core.sem("f_xn_lo")
        s_ax = core.sem("f_ax_product")
        s_z = core.sem("f_z_rows")
        s_zt = core.sem("f_z_turned")
        s_zhi = core.sem("f_z_hi")
        s_zlo = core.sem("f_z_lo")
        s_xb = core.sem("f_x_plus_bias")
        s_mm = core.sem("f_products")
        s_done = core.sem("f_products_and_adapters")
        s_sum = core.sem("f_sums")
        s_out = core.sem("f_stored")

        fills = []
        for k in range(HID_TILES):
            fills.append(("a", [(raw[0][:, :, :].rearrange("p k n -> p (k n)")[:, t * HID + k * P:t * HID + (k + 1) * P], t * P, P)
                                for t in range(A_TILES)], P, NR, [part[:, k, :] for part in aT]))
        fills.append(("a", [(a_shared[:, k * P:(k + 1) * P], k * RANK, RANK) for k in range(HID_TILES)],
                      P, HID_TILES * RANK, [part[:, :, :].rearrange("p k n -> p (k n)") for part in asT]))
        for q in range(A_TILES):
            for h in range(2):
                fills.append(("b", [(raw[1][:, 4 * h + t, q * P:(q + 1) * P], t * P, P) for t in range(4)],
                              P, BANK, [part[:, q, h * BANK:(h + 1) * BANK] for part in bT]))
        for h in range(2):
            fills.append(("b", [(b_shared[:, 4 * h + t, :], t * P, P) for t in range(4)],
                          RANK, BANK, [part[:, h * BANK:(h + 1) * BANK] for part in bsT]))
        A_FILLS = HID_TILES + 1
        FILL_BANKS = (0, 1, 6, 7)
        EARLY_FILLS = len(FILL_BANKS)

        def fill_bank(n):
            return FILL_BANKS[n % len(FILL_BANKS)]

        def halves(t):
            return slice(t * P, (t + 1) * P)

        with nc.Block() as block:
            @block.sync
            def _(eng):
                eng.dma_start(raw[0][:, :, :].rearrange("p k n -> p (k n)").rearrange("p (t i) -> p t i", i=HID),
                              a["lora_A"].rearrange("n r i -> (n r) i").rearrange("(t p) i -> p t i", p=P)).then_inc(s_a, 16)
                eng.dma_start(a_shared[:, :], a["lora_A_shared"]).then_inc(s_a, 16)
                for t in range(HID_TILES):
                    eng.dma_start(raw[1][:, t, :].rearrange("p (n r) -> p n r", r=RANK),
                                  a["lora_B"][:, t * P:(t + 1) * P, :].rearrange("n p r -> p n r")).then_inc(s_b, 16)
                eng.dma_start(b_shared[:, :, :], a["lora_B_shared"].rearrange("(t p) r -> p t r", p=P)).then_inc(s_b, 16)
                for b in range(LORA_BATCH):
                    t, at = b * ROWS_PER_GATE // P, b * ROWS_PER_GATE % P
                    eng.dma_start(gates[at:at + ROWS_PER_GATE, t, :],
                                  a["gate"][b:b + 1, :].broadcast_to([ROWS_PER_GATE, LORAS])).then_inc(s_small, 16)
                eng.dma_start(bias[:, :], a["bias"].rearrange("(o n) -> o n", o=1).broadcast_to([P, HID])).then_inc(s_small, 16)
                for h in range(2):
                    eng.wait_ge(s_t, (A_FILLS, len(fills))[h])
                    eng.dma_start(raw[h][:, :, :], a["kernel"].rearrange("(k p) n -> p k n", p=P)[:, :, h * BANK:(h + 1) * BANK]).then_inc(s_w[h], 16)
                for h in range(2):
                    for t in range(ROW_TILES):
                        eng.wait_ge(s_sum, ROW_TILES * h + t + 1)
                        eng.dma_start(out[0, t * P:(t + 1) * P, h * BANK:(h + 1) * BANK],
                                      normed[:, t, h * BANK:(h + 1) * BANK]).then_inc(s_out, 16)
                eng.wait_ge(s_out, 32 * ROW_TILES)

            @block.gpsimd
            def _(eng):
                layer_norm_pool(eng, core, mv, s_var, s_rstd)
                eng.wait_ge(s_small, 16 * (LORA_BATCH + 1))
                eng.wait_ge(s_ln, 8)
                for t in range(ROW_TILES):
                    eng.tensor_tensor(core.x[:, t, :], core.x[:, t, :], bias[:, :], ALU.add).then_inc(s_xb, 1)

            @block.tensor
            def _(eng):
                def turn_adapter(n):
                    which, moves, parts, width, dest = fills[n]
                    if n == 0:
                        eng.wait_ge(s_a, 32)
                    if n == A_FILLS:
                        eng.wait_ge(s_b, 16 * (HID_TILES + 1))
                    wait(eng, s_lo, n - len(FILL_BANKS) + 1)
                    for src, at, cols in moves:
                        rows = RANK if src.shape[0] == RANK else P
                        mm = eng.transpose(ps[0:parts, fill_bank(n), at:at + (cols if parts == P else P)], src,
                                           core.ident[0:rows, 0:rows])
                    mm.then_inc(s_t, 1)

                for n in range(EARLY_FILLS):
                    turn_adapter(n)
                for t in range(ROW_TILES):
                    eng.wait_ge(s_ln, 7 + t)
                    for k in range(HID_TILES):
                        mm = eng.transpose(ps[:, 2 + 2 * t + k // 4, (k % 4) * P:(k % 4 + 1) * P],
                                           normed[:, t, halves(k)], core.ident[:, :])
                    mm.then_inc(s_xt, 1)
                for n in range(EARLY_FILLS, len(fills)):
                    turn_adapter(n)
                eng.wait_ge(s_lo, len(fills))
                eng.wait_ge(s_xlo, ROW_TILES)
                for t in range(ROW_TILES):
                    for bank, w, cols, at in ((6 + t, aT, NR, 0), (t, asT, RANK, 0)):
                        for k in range(HID_TILES):
                            for n, (s, m) in enumerate(PASSES):
                                mm = eng.matmul(ps[:, bank, at:at + cols], xT[s][:, k, halves(t)], w[m][:, k, :],
                                                start=(k == 0 and n == 0), stop=(k == HID_TILES - 1 and n == 2))
                mm.then_inc(s_ax, 1)

                def base(h):
                    eng.wait_ge(s_wlo, h + 1)
                    for t in range(ROW_TILES):
                        for k in range(HID_TILES):
                            for n, (s, m) in enumerate(PASSES):
                                mm = eng.matmul(ps[:, 2 + 2 * t + h, :], xT[s][:, k, halves(t)], w_part[m][:, k, :],
                                                start=(k == 0 and n == 0), stop=False)
                    return mm

                def delta(h):
                    for t in range(ROW_TILES):
                        for k in range(A_TILES):
                            for s, m in PASSES:
                                eng.matmul(ps[:, 2 + 2 * t + h, :], zT[s][:, t, halves(k)],
                                           bT[m][:, k, h * BANK:(h + 1) * BANK], start=False, stop=False)
                        for n, (s, m) in enumerate(PASSES):
                            mm = eng.matmul(ps[:, 2 + 2 * t + h, :], zsT[s][:, halves(t)],
                                            bsT[m][:, h * BANK:(h + 1) * BANK], start=False, stop=(n == 2))
                        mm.then_inc(s_done, 1)

                base(0).then_inc(s_mm, 1)
                eng.wait_ge(s_z, 4)
                for t in range(ROW_TILES):
                    for k in range(A_TILES):
                        eng.transpose(ps[:, 6 + t, halves(k)], z[:, t, halves(k)], core.ident[:, :])
                for t in range(ROW_TILES):
                    mm = eng.transpose(ps[0:RANK, 0, halves(t)], z[:, t, NR:NR + RANK], core.ident[:, :])
                mm.then_inc(s_zt, 1)
                eng.wait_ge(s_zlo, 2)
                delta(0)
                base(1).then_inc(s_mm, 1)
                delta(1)

            @block.scalar
            def _(eng):
                def high_adapter(n):
                    which, moves, parts, width, dest = fills[n]
                    eng.wait_ge(s_t, n + 1)
                    eng.activation(dest[0], ps[0:parts, fill_bank(n), 0:width], ACT.Copy).then_inc(s_hi, 1)

                for n in range(EARLY_FILLS):
                    high_adapter(n)
                for t in range(ROW_TILES):
                    eng.wait_ge(s_xt, t + 1)
                    eng.activation(xT[0][:, :, halves(t)],
                                   ps[:, 2 + 2 * t:4 + 2 * t, :].rearrange("p b (k n) -> p (b k) n", n=P),
                                   ACT.Copy).then_inc(s_xhi, 1)
                for n in range(EARLY_FILLS, len(fills)):
                    high_adapter(n)
                eng.wait_ge(s_w[0], 16)
                eng.activation(w_part[0][:, :, :], raw[0][:, :, :], ACT.Copy).then_inc(s_whi, 1)
                eng.wait_ge(s_zt, 1)
                eng.activation(zT[0][:, :, :], ps[:, 6:8, :], ACT.Copy).then_inc(s_zhi, 1)
                eng.activation(zsT[0][:, :], ps[0:RANK, 0, 0:ROWS], ACT.Copy).then_inc(s_zhi, 1)
                eng.wait_ge(s_w[1], 16)
                eng.wait_ge(s_mm, 1)
                eng.activation(w_part[0][:, :, :], raw[1][:, :, :], ACT.Copy).then_inc(s_whi, 1)

            @block.vector
            def _(eng):
                def low_adapter(n):
                    which, moves, parts, width, dest = fills[n]
                    eng.wait_ge(s_hi, n + 1)
                    eng.tensor_tensor(dest[1], ps[0:parts, fill_bank(n), 0:width], dest[0].bitcast(F32),
                                      ALU.subtract).then_inc(s_lo, 1)

                layer_norm_vector(eng, core, core.x, normed, stats, mv, s_ln, s_var, s_rstd)
                for n in range(EARLY_FILLS):
                    low_adapter(n)
                for t in range(ROW_TILES):
                    eng.wait_ge(s_xhi, t + 1)
                    eng.tensor_tensor(xT[1][:, :, halves(t)],
                                      ps[:, 2 + 2 * t:4 + 2 * t, :].rearrange("p b (k n) -> p (b k) n", n=P),
                                      xT[0][:, :, halves(t)].bitcast(F32), ALU.subtract).then_inc(s_xlo, 1)
                for n in range(EARLY_FILLS, len(fills)):
                    low_adapter(n)
                eng.wait_ge(s_whi, 1)
                eng.tensor_tensor(w_part[1][:, :, :], raw[0][:, :, :], w_part[0][:, :, :].bitcast(F32),
                                  ALU.subtract).then_inc(s_wlo, 1)
                eng.wait_ge(s_ax, 1)
                eng.wait_ge(s_small, 16 * (LORA_BATCH + 1))
                for t in range(ROW_TILES):
                    eng.tensor_tensor(z[:, t, 0:NR].rearrange("p (n r) -> p n r", r=RANK),
                                      ps[:, 6 + t, :].rearrange("p (n r) -> p n r", r=RANK),
                                      over_last(gates[:, t, :], (P, LORAS, RANK)), ALU.mult).then_inc(s_z, 1)
                    eng.tensor_copy(z[:, t, NR:NR + RANK], ps[:, t, 0:RANK]).then_inc(s_z, 1)
                eng.wait_ge(s_zhi, 2)
                eng.tensor_tensor(zT[1][:, :, :], ps[:, 6:8, :], zT[0][:, :, :].bitcast(F32), ALU.subtract).then_inc(s_zlo, 1)
                eng.tensor_tensor(zsT[1][:, :], ps[0:RANK, 0, 0:ROWS], zsT[0][:, :].bitcast(F32),
                                  ALU.subtract).then_inc(s_zlo, 1)
                eng.wait_ge(s_whi, 2)
                eng.tensor_tensor(w_part[1][:, :, :], raw[1][:, :, :], w_part[0][:, :, :].bitcast(F32),
                                  ALU.subtract).then_inc(s_wlo, 1)
                eng.wait_ge(s_xb, ROW_TILES)
                for h in range(2):
                    for t in range(ROW_TILES):
                        eng.wait_ge(s_done, ROW_TILES * h + t + 1)
                        eng.tensor_tensor(normed[:, t, h * BANK:(h + 1) * BANK], ps[:, 2 + 2 * t + h, :],
                                          core.x[:, t, h * BANK:(h + 1) * BANK], ALU.add).then_inc(s_sum, 1)


def perceiver_layer(nc, a, out):
    with ExitStack() as stack:
        core = Core(nc, stack)

        def scratch(name, shape):
            return nc.dram_tensor(name, shape, F32, kind="Internal").ap()

        q_scratch = scratch("q_scratch", (KV_HEADS, P, 2, GROUP, ROWS))
        k_scratch = scratch("k_scratch", (KV_HEADS, P, KEY_TILES, DIM))
        v_scratch = scratch("v_scratch", (KV_HEADS, P, KEY_TILES, DIM))
        o_scratch = scratch("o_scratch", (P, HEADS, 2, ROWS))
        with ExitStack() as place:
            shared = Shared(core, place)
        with ExitStack() as place:
            projection = Projection(core, a["Wo"], o_scratch, place)
        with ExitStack() as own:
            project_inputs(core, a, own, shared, q_scratch, k_scratch, v_scratch)
        with ExitStack() as own:
            core.sbuf("place_of_shared", [P, SHARED_WORDS], stack=own)
            cross_attention(core, shared, projection, own, q_scratch, k_scratch, v_scratch, o_scratch)
        with ExitStack() as stack_of_self:
            buffers = SelfBuffers(core, stack_of_self)
            project_attention(core, a, shared, projection, buffers)
            self_attention(core, a, buffers)
        feed_forward(core, a, out)


_NAMES = {
    "x": "x", "ctx": "ctx_4096", "Wq": "L0_xattn_Wq", "Wk": "L0_xattn_Wk", "Wv": "L0_xattn_Wv",
    "Wo": "L0_xattn_Wo", "q_norm_w": "L0_xattn_q_norm_w", "k_norm_w": "L0_xattn_k_norm_w",
    "wq": "L0_attn_wq", "wk": "L0_attn_wk", "wv": "L0_attn_wv", "wo": "L0_attn_wo",
    "gate": "L0_ffn_gate", "kernel": "L0_ffn_kernel", "bias": "L0_ffn_bias", "lora_A": "L0_ffn_lora_A",
    "lora_B": "L0_ffn_lora_B", "lora_A_shared": "L0_ffn_lora_A_shared", "lora_B_shared": "L0_ffn_lora_B_shared",
}


def shape_constants():
    half = SELF_DIM // 2
    freqs = (1.0 / np.float32(10000.0) ** (np.arange(0, SELF_DIM, 2, dtype=np.float32) / np.float32(SELF_DIM))).astype(np.float32)
    angle = np.outer(np.arange(ROWS, dtype=np.float32), freqs).astype(np.float32)
    rope = np.stack([np.cos(angle), np.sin(angle)], axis=1).astype(np.float32)
    assert rope.shape == (ROWS, 2, half)
    return {
        "ident": np.eye(P, dtype=np.float32),
        "rope": rope,
        "mask": np.triu(np.full((P, P), NEGATIVE, np.float32), 1),
    }


def kernel(**inputs):
    import concourse.bacc as bacc
    from concourse.bass_utils import run_bass_kernel_spmd

    nc = bacc.Bacc("TRN2", target_bir_lowering=False, num_devices=1)
    given = {short: np.ascontiguousarray(inputs[name]) for short, name in _NAMES.items()} | shape_constants()
    arrays, aps = {}, {}
    for short, array in given.items():
        arrays[f"in_{short}"] = array
        aps[short] = nc.dram_tensor(f"in_{short}", array.shape, mybir.dt.from_np(array.dtype), kind="ExternalInput").ap()
    out = nc.dram_tensor("out_x", (1, ROWS, HID), F32, kind="ExternalOutput").ap()
    perceiver_layer(nc, aps, out)
    result = run_bass_kernel_spmd(nc, [arrays], core_ids=[0])
    return result.results[0]["out_x"]
```

```python
from contextlib import ExitStack

import numpy as np

import concourse.bass as bass
from concourse import mybir

F32 = mybir.dt.float32
F32R = mybir.dt.float32r
ALU = mybir.AluOpType
ACT = mybir.ActivationFunctionType
AX = mybir.AxisListType

P = 128
BANK = 512
ROWS = 256
ROW_TILES = ROWS // P
HID = 1024
HID_TILES = HID // P
CTX = 4096
CTX_TILES = CTX // P
KEYS = CTX + ROWS
KEY_TILES = KEYS // P
HEADS = 32
KV_HEADS = 8
GROUP = HEADS // KV_HEADS
DIM = 128
LN_EPS = 1e-5
RMS_EPS = 1e-6
SELF_DIM = HID // HEADS
LORAS = 16
RANK = 32
LORA_BATCH = 8
ROWS_PER_GATE = ROWS // LORA_BATCH
NEGATIVE = -1e30

PASSES = ((0, 0), (0, 1), (1, 0))


def wait(engine, semaphore, value):
    if not isinstance(value, int) or value > 0:
        engine.wait_ge(semaphore, value)


def over_last(ap, shape):
    return ap.unsqueeze(len(shape) - 1).broadcast_to(list(shape))


class Core:

    def __init__(self, nc, stack):
        self.nc, self.stack = nc, stack
        self.psum = stack.enter_context(nc.psum_tensor("psum", [P, 8, BANK], F32))
        self.ident = self.sbuf("ident", [P, P])
        self.ones = self.sbuf("ones", [P, P])
        self.minus_half = self.sbuf("minus_half", [P, KV_HEADS])
        self.x = self.sbuf("x_rows", [P, ROW_TILES, HID])

    def sbuf(self, name, shape, dtype=F32, stack=None):
        return (stack or self.stack).enter_context(self.nc.sbuf_tensor(name, shape, dtype))

    def sem(self, name):
        return self.stack.enter_context(self.nc.semaphore(name))


def layer_norm_statistics(eng, rows, stats, mv, done, to_pool):
    for t in range(ROW_TILES):
        for half in range(2):
            eng.bn_stats(stats[:, t, half, :], rows[:, t, half * BANK:(half + 1) * BANK]).then_inc(done, 1)
        eng.wait_ge(done, 3 * t + 2)
        eng.bn_aggr(mv[:, t, 0:2], stats[:, t, :, :]).then_inc(done, 1)
        eng.wait_ge(done, 3 * t + 3)
        eng.tensor_scalar(mv[:, t, 2:3], mv[:, t, 1:2], LN_EPS, None, ALU.add).then_inc(to_pool, 1)


def layer_norm_tile(eng, rows, normed, stats, mv, t, done, to_pool, from_pool):
    for half in range(2):
        eng.bn_stats(stats[:, t, half, :], rows[:, t, half * BANK:(half + 1) * BANK]).then_inc(done, 1)
    eng.wait_ge(done, 4 * t + 2)
    eng.bn_aggr(mv[:, t, 0:2], stats[:, t, :, :]).then_inc(done, 1)
    eng.wait_ge(done, 4 * t + 3)
    eng.tensor_scalar(mv[:, t, 2:3], mv[:, t, 1:2], LN_EPS, None, ALU.add).then_inc(to_pool, 1)
    eng.wait_ge(from_pool, t + 1)
    eng.tensor_scalar(normed[:, t, :], rows[:, t, :], mv[:, t, 0:1], mv[:, t, 3:4],
                      ALU.subtract, ALU.mult).then_inc(done, 1)


def layer_norm_pool(eng, core, mv, to_pool, from_pool, tiles=range(ROW_TILES)):
    for t in tiles:
        eng.wait_ge(to_pool, t + 1)
        eng.tensor_tensor(mv[:, t, 3:4], mv[:, t, 2:3], core.minus_half[:, 0:1], ALU.pow).then_inc(from_pool, 1)


SHARED_WORDS = 2 * KEYS + KEY_TILES * DIM + GROUP * 2 * ROWS


class Shared:

    def __init__(self, core, stack):
        self.keysT = [core.sbuf(f"keysT_part{n}", [P, KEYS], F32R, stack=stack) for n in range(2)]
        self.k_raw = core.sbuf("k_raw", [P, KEY_TILES, DIM], stack=stack)
        self.queries = core.sbuf("queries", [P, GROUP, 2, ROWS], F32R, stack=stack)
        self.s_kraw = core.sem("x_k_loaded")
        self.s_q = [core.sem(f"x_q_loaded{m}") for m in range(GROUP)]
        self.s_turn = core.sem("x_keys_turned")
        self.s_khi = core.sem("x_keys_hi")
        self.s_klo = core.sem("x_keys_lo")
        self.s_qst = [core.sem(f"i_q_stored{n}") for n in range(2)]
        self.s_ost = [core.sem(f"x_o_stored{n}") for n in range(2)]


class Projection:
    HEADS = 2

    def __init__(self, core, wo, o_scratch, stack):
        self.wo, self.o_scratch = wo.rearrange("(h p) n -> p h n", p=P), o_scratch
        self.w_raw = core.sbuf("wo_raw", [P, 2, self.HEADS, HID], stack=stack)
        self.w_part = [core.sbuf(f"wo_part{n}", [P, 2, self.HEADS, HID], F32R, stack=stack) for n in range(2)]
        self.outT = core.sbuf("oT_parts", [P, 2, self.HEADS, 2, ROWS], F32R, stack=stack)
        self.s_w = [core.sem(f"p_w_loaded{n}") for n in range(2)]
        self.s_o = [core.sem(f"p_o_loaded{n}") for n in range(2)]
        self.s_whi = core.sem("p_w_hi")
        self.s_wlo = core.sem("p_w_lo")
        self.s_mm = core.sem("p_products")

    def banks(self, t):
        return slice(0, 2) if t == 0 else slice(2, 6, 3)

    def product(self, eng, ps, par, t, g, start, stop):
        for n, (s, m) in enumerate(PASSES):
            for half, bank in enumerate(((0, 1), (2, 5))[t]):
                mm = eng.matmul(ps[:, bank, :], self.outT[:, par, g, s, t * P:(t + 1) * P],
                                self.w_part[m][:, par, g, half * BANK:(half + 1) * BANK],
                                start=(start and n == 0), stop=(stop and n == 2))
        return mm

    def load_weights(self, eng, i, par):
        eng.dma_start(self.w_raw[:, par, :, :],
                      self.wo[:, bass.ds((2 * i + par) * self.HEADS, self.HEADS), :]).then_inc(self.s_w[par], 16)

    def load_outputs(self, eng, i, par):
        eng.dma_start(self.outT[:, par, :, :, :].bitcast(F32),
                      self.o_scratch[:, bass.ds((2 * i + par) * self.HEADS, self.HEADS), :, :]).then_inc(self.s_o[par], 16)

    def high(self, eng, i, par, g):
        eng.wait_ge(self.s_w[par], 16 * (i + 1))
        eng.activation(self.w_part[0][:, par, g, :], self.w_raw[:, par, g, :], ACT.Copy).then_inc(self.s_whi, 1)

    def low(self, eng, i, par, g):
        eng.wait_ge(self.s_whi, (2 * i + par) * self.HEADS + g + 1)
        eng.tensor_tensor(self.w_part[1][:, par, g, :], self.w_raw[:, par, g, :],
                          self.w_part[0][:, par, g, :].bitcast(F32), ALU.subtract).then_inc(self.s_wlo, 1)


CHUNKS = -(-KEYS // BANK)


def chunk_columns(c):
    return c * BANK, min(BANK, KEYS - c * BANK)


def project_inputs(core, a, own, shared, q_scratch, k_scratch, v_scratch):
    nc, ps = core.nc, core.psum
    KV = KV_HEADS * DIM
    T_BANK, K_BANK, V_BANK, KEYS_BANK = 0, 2, 4, 6
    LAST = CTX_TILES // 2 - 1
    LATENT = KEY_TILES // 2 - 1
    PIECES = 2 * HID_TILES
    Q_PAIRS = KV_HEADS // 2

    wv_part = [core.sbuf(f"wv_part{n}", [P, HID_TILES, KV], F32R, stack=own) for n in range(2)]
    wk_part = [core.sbuf("wk_part0", [P, HID_TILES, KV], F32R, stack=own)]
    q_part = [core.sbuf(f"q_part{n}", [P, 2, GROUP, ROWS], F32R, stack=own) for n in range(2)]
    wk_part.append(core.sbuf("wk_part1", [P, HID_TILES, KV], F32R, stack=own))
    w_raw = core.sbuf("w_raw", [P, 2, KV], stack=own)
    rows = core.sbuf("key_rows", [P, 2, HID], stack=own)
    rowsT = [core.sbuf(f"key_rowsT_part{n}", [P, 2, HID_TILES, P], F32R, stack=own) for n in range(2)]
    square = core.sbuf("squares", [P, KV], stack=own)
    small = core.sbuf("rms_small", [P, 3, KV_HEADS], stack=own)
    k_out = core.sbuf("k_out", [P, 2, KV], stack=own)
    v_out = core.sbuf("v_out", [P, 2, KV], stack=own)
    stats = core.sbuf("ln_stats", [P, ROW_TILES, 2, 6], stack=own)
    mv = core.sbuf("ln_mv", [P, ROW_TILES, 4], stack=own)
    weights = core.sbuf("norm_weights", [P, 4], stack=own)

    s_const = core.sem("i_ident_loaded")
    s_small = core.sem("i_x_weights_loaded")
    s_fill = core.sem("i_constants_set")
    s_nw = core.sem("i_norm_weights")
    s_ln = core.sem("i_ln_steps")
    s_var = core.sem("i_var_ready")
    s_rstd = core.sem("i_rstd_ready")
    s_w = [core.sem(f"i_w_loaded{n}") for n in range(4)]
    s_whi = core.sem("i_w_hi")
    s_wlo = core.sem("i_w_lo")
    s_rows = [core.sem(f"i_rows_loaded{n}") for n in range(2)]
    s_t = core.sem("i_rows_transposed")
    s_hi = core.sem("i_rows_hi")
    s_lo = core.sem("i_rows_lo")
    s_k = core.sem("i_k_product")
    s_v = core.sem("i_v_product")
    s_q = core.sem("i_q_product")
    s_sq = core.sem("i_squared")
    s_sum = core.sem("i_summed")
    s_ms = core.sem("i_mean_square")
    s_rms = core.sem("i_rms_scale")
    s_krow = core.sem("i_k_rows")
    s_vrow = core.sem("i_v_rows")
    s_qrow = core.sem("i_q_rows")
    s_qt = core.sem("i_q_transposed")
    s_qhi = core.sem("i_q_hi")
    s_qlo = core.sem("i_q_lo")
    s_kst = [core.sem(f"i_k_stored{n}") for n in range(2)]
    s_vst = [core.sem(f"i_v_stored{n}") for n in range(2)]
    s_qst = shared.s_qst
    s_wq = [core.sem(f"i_wq_loaded{h}") for h in range(4)]

    def w_buffer(n):
        return (w_raw, v_out)[n % 4 // 2][:, n % 2, :]

    def q_raw(c, h):
        buffer = w_raw[:, h % 2, :] if c < 2 or h < 2 else k_out[:, h % 2, :]
        return buffer.rearrange("p (k n) -> p k n", n=BANK)

    def q_piece(part, par, h):
        return part[:, 2 * h:2 * h + 2, par * BANK:(par + 1) * BANK]

    with nc.Block() as block:
        @block.sync
        def _(eng):
            ctx = a["ctx"].rearrange("b (t p) n -> p (b t) n", p=P)
            wq = a["Wq"].rearrange("(k p) n -> p k n", p=P)

            def load(i, par):
                wait(eng, s_t, 2 * i + par - 1)
                eng.dma_start(rows[:, par, :], ctx[:, bass.ds(2 * i + par, 1), :].rearrange("p o n -> p (o n)")).then_inc(s_rows[par], 16)

            def load_weights(n):
                wait(eng, s_wlo, n - 3)
                w = a["Wk"] if n < HID_TILES else a["Wv"]
                k = n % HID_TILES
                eng.dma_start(w_buffer(n), w[k * P:(k + 1) * P, :]).then_inc(s_w[n % 4], 16)

            def load_q_weights(i, par):
                c = 2 * i + par
                for h in range(4):
                    if isinstance(i, int) and i == 0:
                        eng.wait_ge(s_wlo, PIECES + 4 * c + h - 1)
                        loaded = s_w[h % 2]
                    else:
                        if isinstance(i, int) and c == 2 and h < 2:
                            eng.wait_ge(s_wlo, PIECES + 6 + h + 1)
                        elif not (isinstance(i, int) and c == 2):
                            eng.wait_ge(s_wlo, PIECES + 4 * (c - 1) + h + 1)
                        loaded = s_wq[h]
                    eng.dma_start(q_raw(2 if loaded is s_wq[h] else 0, h),
                                  wq[:, 2 * h:2 * h + 2, bass.ds(c * BANK, BANK)]).then_inc(loaded, 16)

            def store(i, par):
                t = 2 * i + par
                for done, out, scratch, stored in ((s_krow, k_out, k_scratch, s_kst), (s_vrow, v_out, v_scratch, s_vst)):
                    wait(eng, done, t + 1)
                    eng.dma_start(scratch[:, :, bass.ds(t, 1), :].rearrange("h p o d -> p (h o) d"),
                                  out[:, par, :].rearrange("p (h d) -> p h d", d=DIM)).then_inc(stored[par], 16)

            def store_q(i, par):
                c = 2 * i + par
                eng.wait_ge(s_qlo, c + 1)
                for n in range(2):
                    eng.dma_start(q_scratch[bass.ds(c, 1), :, n, :, :].rearrange("o p g r -> (o p) g r"),
                                  q_part[n][:, par, :, :].bitcast(F32)).then_inc(s_qst[par], 16)

            load(0, 0)
            eng.dma_start(core.ident[:, :], a["ident"]).then_inc(s_const, 16)
            load_weights(0)
            load_weights(1)
            load(0, 1)
            for n in range(2, PIECES):
                load_weights(n)
            eng.dma_start(core.x[:, :, :], a["x"].rearrange("b (t p) n -> p (b t) n", p=P)).then_inc(s_small, 16)
            eng.dma_start(weights[:, 0:1], a["q_norm_w"].rearrange("(p o) -> p o", o=1)).then_inc(s_small, 16)
            eng.dma_start(weights[:, 1:2], a["k_norm_w"].rearrange("(p o) -> p o", o=1)).then_inc(s_small, 16)
            with eng.Fori(0, LAST) as i:
                load(i + 1, 0)
                store(i, 0)
                load(i + 1, 1)
                store(i, 1)
            store(LAST, 0)
            store(LAST, 1)
            store(LATENT, 0)
            load_q_weights(0, 0)
            store(LATENT, 1)
            load_q_weights(0, 1)
            for par in range(2):
                eng.wait_ge(s_kst[par], 16 * KEY_TILES // 2)
                eng.wait_ge(s_vst[par], 16 * KEY_TILES // 2)
            eng.dma_start(shared.k_raw[:, :, :], k_scratch[0, :, :, :]).then_inc(shared.s_kraw, 16)
            load_q_weights(1, 0)
            load_q_weights(1, 1)
            with eng.Fori(2, Q_PAIRS) as i:
                store_q(i - 2, 0)
                load_q_weights(i, 0)
                store_q(i - 2, 1)
                load_q_weights(i, 1)
            eng.wait_ge(s_qst[0], 32)
            for m in range(GROUP):
                eng.dma_start(shared.queries[:, m, :, :].bitcast(F32), q_scratch[0, :, :, m, :]).then_inc(shared.s_q[m], 16)
            for i in (Q_PAIRS - 2, Q_PAIRS - 1):
                store_q(i, 0)
                store_q(i, 1)

        @block.gpsimd
        def _(eng):
            eng.memset(core.minus_half[:, :], -0.5).then_inc(s_fill, 1)
            eng.memset(core.ones[:, :], 1.0).then_inc(s_fill, 1)
            eng.wait_ge(s_fill, 2)

            def scale(n):
                eng.wait_ge(s_ms, n + 1)
                eng.tensor_tensor(small[:, 2, :], small[:, 1, :], core.minus_half[:, :], ALU.pow).then_inc(s_rms, 1)

            scale(0)
            scale(1)
            layer_norm_pool(eng, core, mv, s_var, s_rstd)
            with eng.Fori(2, KEY_TILES + KV_HEADS) as n:
                scale(n)

        @block.tensor
        def _(eng):
            def transposes(i, par, latent=False):
                t = 2 * i + par
                if latent:
                    eng.wait_ge(s_ln, 7 + par)
                else:
                    wait(eng, s_rows[par], 16 * (i + 1))
                wait(eng, s_lo, t)
                for k in range(HID_TILES):
                    mm = eng.transpose(ps[:, T_BANK + k // 4, (k % 4) * P:(k % 4 + 1) * P],
                                       rows[:, par, k * P:(k + 1) * P], core.ident[:, :])
                mm.then_inc(s_t, 1)

            def product(bank, par, w_part, ready):
                for k in range(HID_TILES):
                    if ready is not None:
                        eng.wait_ge(s_wlo, ready + k + 1)
                    for n, (s, m) in enumerate(PASSES):
                        for half in range(2):
                            mm = eng.matmul(ps[:, bank + half, :], rowsT[s][:, par, k, :],
                                            w_part[m][:, k, half * BANK:(half + 1) * BANK],
                                            start=(k == 0 and n == 0), stop=(k == HID_TILES - 1 and n == 2))
                return mm

            def products(i, par, first=False):
                t = 2 * i + par
                wait(eng, s_lo, t + 1)
                wait(eng, s_krow, t)
                product(K_BANK, par, wk_part, 0 if first else None).then_inc(s_k, 1)
                wait(eng, s_vrow, t)
                product(V_BANK, par, wv_part, HID_TILES if first else None).then_inc(s_v, 1)

            eng.wait_ge(s_const, 16)
            transposes(0, 0)
            transposes(0, 1)
            products(0, 0, first=True)
            transposes(1, 0)
            products(0, 1)
            with eng.Fori(1, LAST) as i:
                transposes(i, 1)
                products(i, 0)
                transposes(i + 1, 0)
                products(i, 1)
            transposes(LAST, 1)
            products(LAST, 0)
            transposes(LATENT, 0, latent=True)
            products(LAST, 1)
            transposes(LATENT, 1, latent=True)
            products(LATENT, 0)
            products(LATENT, 1)

            def q_products(i, par, between=()):
                c = 2 * i + par
                bank = (K_BANK, T_BANK)[par]
                if isinstance(i, int) and i == 0:
                    eng.wait_ge((s_krow, s_lo)[par], KEY_TILES)
                else:
                    eng.wait_ge(s_qrow, c - 1)
                for h in range(4):
                    if between and h >= 2:
                        turn_keys(between[2 * h - 4])
                        turn_keys(between[2 * h - 3])
                    if between and h == 3:
                        q_transposes(i, 0)
                    eng.wait_ge(s_wlo, PIECES + 4 * c + h + 1)
                    for k in (2 * h, 2 * h + 1):
                        for t in range(ROW_TILES):
                            for n, (s, m) in enumerate(PASSES):
                                mm = eng.matmul(ps[:, bank + t, :], rowsT[s][:, t, k, :],
                                                wk_part[m][:, k, par * BANK:(par + 1) * BANK],
                                                start=(k == 0 and n == 0), stop=(k == HID_TILES - 1 and n == 2))
                mm.then_inc(s_q, 1)

            def q_transposes(i, par):
                c = 2 * i + par
                if isinstance(i, int) and c == 0:
                    eng.wait_ge(s_vrow, KEY_TILES)
                wait(eng, s_qrow, c + 1)
                wait(eng, s_qlo, c)
                for t in range(ROW_TILES):
                    for g in range(GROUP):
                        mm = eng.transpose(ps[:, V_BANK + t, g * P:(g + 1) * P],
                                           rows[:, par, t * BANK + g * P:t * BANK + (g + 1) * P], core.ident[:, :])
                mm.then_inc(s_qt, 1)

            def turn_keys(c):
                at, width = chunk_columns(c)
                eng.wait_ge(shared.s_kraw, 16)
                wait(eng, shared.s_klo, c - 1)
                for k in range(width // P):
                    mm = eng.transpose(ps[:, KEYS_BANK + c % 2, k * P:(k + 1) * P],
                                       shared.k_raw[:, at // P + k, :], core.ident[:, :])
                mm.then_inc(shared.s_turn, 1)

            q_products(0, 0)
            q_products(0, 1)
            q_transposes(0, 0)
            with eng.Fori(1, Q_PAIRS - 1) as i:
                q_products(i, 0)
                q_transposes(i - 1, 1)
                q_products(i, 1)
                q_transposes(i, 0)
            i = Q_PAIRS - 1
            turn_keys(0)
            turn_keys(1)
            q_products(i, 0)
            turn_keys(2)
            turn_keys(3)
            q_transposes(i - 1, 1)
            q_products(i, 1, between=(4, 5, 6, 7))
            turn_keys(CHUNKS - 1)
            q_transposes(i, 1)

        @block.scalar
        def _(eng):
            def split_weights(n):
                eng.wait_ge(s_w[n % 4], 16 * (n // 4 + 1))
                part = (wk_part, wv_part)[n // HID_TILES][0]
                eng.activation(part[:, n % HID_TILES, :], w_buffer(n), ACT.Copy).then_inc(s_whi, 1)

            def high(i, par):
                t = 2 * i + par
                wait(eng, s_t, t + 1)
                wait(eng, s_v, t - 1)
                eng.activation(rowsT[0][:, par, :, :],
                               ps[:, T_BANK:T_BANK + 2, :].rearrange("p b (k n) -> p (b k) n", n=P),
                               ACT.Copy).then_inc(s_hi, 1)

            def squares(product, count, bank, number):
                eng.wait_ge(product, count)
                wait(eng, s_sum, number)
                eng.activation(square[:, :].rearrange("p (b n) -> p b n", n=BANK), ps[:, bank:bank + 2, :],
                               ACT.Square).then_inc(s_sq, 1)

            def copy_v(i, par):
                wait(eng, s_v, 2 * i + par + 1)
                wait(eng, s_vst[par], 16 * i)
                eng.activation(v_out[:, par, :].rearrange("p (b n) -> p b n", n=BANK), ps[:, V_BANK:V_BANK + 2, :],
                               ACT.Copy).then_inc(s_vrow, 1)

            def drain(i, par):
                squares(s_k, 2 * i + par + 1, K_BANK, 2 * i + par)
                copy_v(i, par)

            high(0, 0)
            split_weights(0)
            split_weights(1)
            high(0, 1)
            for n in range(2, PIECES):
                split_weights(n)
            with eng.Fori(0, LAST) as i:
                drain(i, 0)
                high(i + 1, 0)
                drain(i, 1)
                high(i + 1, 1)
            drain(LAST, 0)
            high(LATENT, 0)
            drain(LAST, 1)
            high(LATENT, 1)
            drain(LATENT, 0)
            squares(s_k, KEY_TILES, K_BANK, KEY_TILES - 1)

            def q_split(i, par):
                c = 2 * i + par
                wait(eng, s_q, c - 1)
                for h in range(4):
                    first = isinstance(i, int) and i == 0
                    if first:
                        eng.wait_ge(s_w[h % 2], 4 * PIECES + 16 * (2 * c + h // 2 + 1))
                    else:
                        eng.wait_ge(s_wq[h], 16 * (c - 1))
                    eng.activation(q_piece(wk_part[0], par, h), q_raw(0 if first else 2, h), ACT.Copy).then_inc(s_whi, 1)

            def q_squares(i, par):
                c = 2 * i + par
                squares(s_q, c + 1, (K_BANK, T_BANK)[par], KEY_TILES + c)

            def q_high(i, par):
                eng.wait_ge(s_qt, 2 * i + par + 1)
                wait(eng, s_qst[par], 32 * i)
                eng.activation(q_part[0][:, par, :, :].rearrange("p g (t n) -> p t g n", n=P),
                               ps[:, V_BANK:V_BANK + 2, :].rearrange("p t (g n) -> p t g n", n=P),
                               ACT.Identity, scale=weights[:, 3:4]).then_inc(s_qhi, 1)

            def high_keys(c):
                at, width = chunk_columns(c)
                eng.wait_ge(shared.s_turn, c + 1)
                eng.activation(shared.keysT[0][:, at:at + width], ps[:, KEYS_BANK + c % 2, 0:width],
                               ACT.Copy).then_inc(shared.s_khi, 1)

            eng.wait_ge(s_k, KEY_TILES)
            q_split(0, 0)
            copy_v(LATENT, 1)
            eng.wait_ge(s_nw, 2)
            q_split(0, 1)
            q_squares(0, 0)
            with eng.Fori(1, Q_PAIRS - 1) as i:
                q_split(i, 0)
                q_squares(i - 1, 1)
                q_high(i - 1, 0)
                q_split(i, 1)
                q_squares(i, 0)
                q_high(i - 1, 1)
            i = Q_PAIRS - 1
            q_split(i, 0)
            high_keys(0)
            high_keys(1)
            q_squares(i - 1, 1)
            q_high(i - 1, 0)
            q_split(i, 1)
            q_squares(i, 0)
            high_keys(2)
            high_keys(3)
            q_high(i - 1, 1)
            for c in range(4, CHUNKS - 1):
                high_keys(c)
            q_high(i, 0)
            q_squares(i, 1)
            high_keys(CHUNKS - 1)
            q_high(i, 1)

        @block.vector
        def _(eng):
            def split_weights(n):
                eng.wait_ge(s_whi, n + 1)
                part = (wk_part, wv_part)[n // HID_TILES]
                eng.tensor_tensor(part[1][:, n % HID_TILES, :], w_buffer(n),
                                  part[0][:, n % HID_TILES, :].bitcast(F32), ALU.subtract).then_inc(s_wlo, 1)

            def low(i, par):
                wait(eng, s_hi, 2 * i + par + 1)
                eng.tensor_tensor(rowsT[1][:, par, :, :],
                                  ps[:, T_BANK:T_BANK + 2, :].rearrange("p b (k n) -> p (b k) n", n=P),
                                  rowsT[0][:, par, :, :].bitcast(F32), ALU.subtract).then_inc(s_lo, 1)

            def scales(number):
                wait(eng, s_sq, number + 1)
                eng.tensor_reduce(small[:, 0, :], square[:, :].rearrange("p (h d) -> p h d", d=DIM),
                                  AX.X, ALU.add).then_inc(s_sum, 1)
                wait(eng, s_sum, number + 1)
                eng.tensor_scalar(small[:, 1, :], small[:, 0, :], 1.0 / DIM, RMS_EPS,
                                  ALU.mult, ALU.add).then_inc(s_ms, 1)
                wait(eng, s_rms, number + 1)

            def norm(i, par):
                scales(2 * i + par)
                wait(eng, s_kst[par], 16 * i)
                eng.tensor_tensor(k_out[:, par, :].rearrange("p (h d) -> p h d", d=DIM),
                                  ps[:, K_BANK:K_BANK + 2, :].rearrange("p b (h d) -> p (b h) d", d=DIM),
                                  over_last(small[:, 2, :], (P, KV_HEADS, DIM)), ALU.mult).then_inc(s_krow, 1)

            low(0, 0)
            split_weights(0)
            split_weights(1)
            low(0, 1)
            for n in range(2, PIECES):
                split_weights(n)
            norm(0, 0)
            low(1, 0)
            norm(0, 1)
            low(1, 1)
            eng.wait_ge(s_small, 48)
            eng.tensor_tensor(weights[:, 2:3], weights[:, 0:1], weights[:, 1:2], ALU.mult).then_inc(s_nw, 1)
            eng.wait_ge(s_nw, 1)
            eng.tensor_scalar(weights[:, 3:4], weights[:, 2:3], float(1.0 / np.sqrt(DIM)), None,
                              ALU.mult).then_inc(s_nw, 1)
            layer_norm_statistics(eng, core.x, stats, mv, s_ln, s_var)
            with eng.Fori(1, LAST) as i:
                norm(i, 0)
                low(i + 1, 0)
                norm(i, 1)
                low(i + 1, 1)
            norm(LAST, 0)
            eng.wait_ge(s_rstd, ROW_TILES)
            eng.wait_ge(s_t, CTX_TILES)
            for t in range(ROW_TILES):
                eng.tensor_scalar(rows[:, t, :], core.x[:, t, :], mv[:, t, 0:1], mv[:, t, 3:4],
                                  ALU.subtract, ALU.mult).then_inc(s_ln, 1)
            low(LATENT, 0)
            norm(LAST, 1)
            low(LATENT, 1)
            norm(LATENT, 0)
            norm(LATENT, 1)

            def q_split(i, par):
                for h in range(4):
                    eng.wait_ge(s_whi, PIECES + 4 * (2 * i + par) + h + 1)
                    eng.tensor_tensor(q_piece(wk_part[1], par, h),
                                      q_raw(0 if isinstance(i, int) and i == 0 else 2, h),
                                      q_piece(wk_part[0], par, h).bitcast(F32), ALU.subtract).then_inc(s_wlo, 1)

            def q_norm(i, par):
                c = 2 * i + par
                bank = (K_BANK, T_BANK)[par]
                scales(KEY_TILES + c)
                wait(eng, s_qt, c - 1)
                eng.tensor_tensor(rows[:, par, :].rearrange("p (h d) -> p h d", d=DIM),
                                  ps[:, bank:bank + 2, :].rearrange("p b (h d) -> p (b h) d", d=DIM),
                                  over_last(small[:, 2, :], (P, KV_HEADS, DIM)), ALU.mult).then_inc(s_qrow, 1)

            def q_low(i, par):
                eng.wait_ge(s_qhi, 2 * i + par + 1)
                for t in range(ROW_TILES):
                    ins = eng.scalar_tensor_tensor(
                        out=q_part[1][:, par, :, t * P:(t + 1) * P],
                        in0=ps[:, V_BANK + t, :].rearrange("p (g n) -> p g n", n=P), scalar=weights[:, 3:4],
                        in1=q_part[0][:, par, :, t * P:(t + 1) * P].bitcast(F32),
                        op0=ALU.mult, op1=ALU.subtract)
                ins.then_inc(s_qlo, 1)

            def low_keys(c):
                at, width = chunk_columns(c)
                eng.wait_ge(shared.s_khi, c + 1)
                eng.tensor_tensor(shared.keysT[1][:, at:at + width], ps[:, KEYS_BANK + c % 2, 0:width],
                                  shared.keysT[0][:, at:at + width].bitcast(F32), ALU.subtract).then_inc(shared.s_klo, 1)

            q_split(0, 0)
            q_split(0, 1)
            q_norm(0, 0)
            with eng.Fori(1, Q_PAIRS - 1) as i:
                q_split(i, 0)
                q_norm(i - 1, 1)
                q_low(i - 1, 0)
                q_split(i, 1)
                q_norm(i, 0)
                q_low(i - 1, 1)
            i = Q_PAIRS - 1
            q_split(i, 0)
            low_keys(0)
            low_keys(1)
            q_norm(i - 1, 1)
            q_low(i - 1, 0)
            q_split(i, 1)
            q_norm(i, 0)
            low_keys(2)
            low_keys(3)
            q_low(i - 1, 1)
            for c in range(4, CHUNKS - 1):
                low_keys(c)
            q_low(i, 0)
            q_norm(i, 1)
            low_keys(CHUNKS - 1)
            q_low(i, 1)


def cross_attention(core, shared, out, own, q_scratch, k_scratch, v_scratch, o_scratch):
    nc, ps = core.nc, core.psum
    STEPS = KEY_TILES // 2
    UNITS = 2 * CHUNKS
    S_BANK, T_BANK, O_BANK, AUX = 0, 3, 5, 7
    QK_AT = [(2 * s, 2 * s + 1) if s < 4 else (s + 4,) if s < 12 else (16, 17) if s == 12 else () for s in range(STEPS)]
    TURN_AT = {1: 0, 2: 1, 3: 2, 4: 3, 6: 4, 8: 5, 10: 6, 12: 7, 13: 8}
    SPLIT_AT = {5: (0, 0), 6: (0, 1), 7: (1, 0), 8: (1, 1), 11: (2, 0), 12: (2, 1), 14: (3, 0), 15: (3, 1)}
    PRODUCT_AT = {7: (0, 0), 9: (0, 1), 11: (1, 0), 13: (1, 1)}
    EARLY_EXP = {13: (0,), 14: (1,), 15: (2, 3), 16: (4,)}
    LATE_EXP = {s: (s + 5,) for s in range(UNITS - 5)}
    SUM_AT, SPREAD_AT = 13, 15

    keysT, k_raw, queries = shared.keysT, shared.k_raw, shared.queries
    scores = core.sbuf("scores", [P, 2, ROW_TILES, KEYS], stack=own)
    values = [core.sbuf(f"values_part{n}", [P, KEY_TILES, DIM], F32R, stack=own) for n in range(2)]
    v_raw = core.sbuf("v_raw", [P, KEY_TILES, DIM], stack=own)
    probsT = [core.sbuf(f"probsT_part{n}", [P, 2, 2, ROWS], F32R, stack=own) for n in range(2)]
    o_full = core.sbuf("o_full", [P, 2, ROWS], stack=own)
    o_part = core.sbuf("o_part", [P, 2, 2, ROWS], F32R, stack=own)
    spread = core.sbuf("inverse_sums_spread", [P, ROWS], stack=own)
    diag = core.sbuf("inverse_sums_diagonal", [P, ROW_TILES, P], stack=own)
    unit_max = core.sbuf("unit_max", [P, 2, ROW_TILES, CHUNKS], stack=own)
    minus_max = core.sbuf("minus_max", [P, 2, ROW_TILES], stack=own)
    unit_sum = core.sbuf("unit_sum", [P, 2, ROW_TILES, CHUNKS], stack=own)
    row_sum = core.sbuf("row_sum", [P, 2, ROW_TILES], stack=own)

    s_kraw, s_q, s_turn, s_khi, s_klo = shared.s_kraw, shared.s_q, shared.s_turn, shared.s_khi, shared.s_klo
    s_vraw = core.sem("x_v_loaded")
    s_vhi = core.sem("x_values_hi")
    s_vlo = core.sem("x_values_lo")
    s_qk = core.sem("x_unit_products")
    s_se = core.sem("x_unit_drained")
    s_max = core.sem("x_max")
    s_exp = core.sem("x_exp")
    s_pt = core.sem("x_probs_turned")
    s_phi = core.sem("x_probs_hi")
    s_plo = core.sem("x_probs_lo")
    s_pv = core.sem("x_pv")
    s_sum = core.sem("x_row_sums")
    s_inv = core.sem("x_inverse_sums")
    s_diag = core.sem("x_diagonal")
    s_bc = core.sem("x_spread_product")
    s_spread = core.sem("x_spread")
    s_on = core.sem("x_o_normed")
    s_ohi = core.sem("x_o_hi")
    s_olo = core.sem("x_o_lo")
    s_ost = shared.s_ost

    def heads(eng, body):
        body(0)
        with eng.Fori(1, KV_HEADS - 1) as j:
            body(j)
        body(KV_HEADS - 1)

    def final(j):
        return isinstance(j, int) and j == KV_HEADS - 1

    ones = core.ones[:, :].unsqueeze(1).broadcast_to([P, 2, P])

    def norm_output(eng, j, m):
        G = 4 * j + m
        eng.wait_ge(s_pv, STEPS * (G + 1))
        eng.wait_ge(s_spread, G + 1)
        wait(eng, s_olo, G - 1)
        eng.tensor_tensor(o_full[:, m % 2, :], ps[:, O_BANK + m % 2, 0:ROWS], spread[:, :],
                          ALU.mult).then_inc(s_on, 1)

    def split_output(eng, j, m):
        G = 4 * j + m
        eng.wait_ge(s_on, G + 1)
        wait(eng, s_ost[m % 2], 16 * (2 * j + m // 2))
        eng.tensor_tensor(o_part[:, m % 2, 0, :].rearrange("p (t n) -> p t n", n=P),
                          o_full[:, m % 2, :].rearrange("p (t n) -> p t n", n=P), ones, ALU.mult).then_inc(s_ohi, 1)
        eng.wait_ge(s_ohi, G + 1)
        eng.tensor_tensor(o_part[:, m % 2, 1, :], o_full[:, m % 2, :],
                          o_part[:, m % 2, 0, :].bitcast(F32), ALU.subtract).then_inc(s_olo, 1)

    def store(eng, j, m):
        eng.wait_ge(s_olo, 4 * j + m + 1)
        eng.dma_start(o_scratch[:, bass.ds(4 * j + m, 1), :, :].rearrange("p o n r -> p (o n) r"),
                      o_part[:, m % 2, :, :].bitcast(F32)).then_inc(s_ost[m % 2], 16)

    with nc.Block() as block:
        @block.sync
        def _(eng):
            def load_k(j):
                wait(eng, s_turn, CHUNKS * j)
                eng.dma_start(k_raw[:, :, :], k_scratch[bass.ds(j, 1), :, :, :].rearrange("o p t d -> (o p) t d")).then_inc(s_kraw, 16)

            def load_v(j):
                wait(eng, s_vlo, STEPS * j)
                eng.dma_start(v_raw[:, :, :], v_scratch[bass.ds(j, 1), :, :, :].rearrange("o p t d -> (o p) t d")).then_inc(s_vraw, 16)

            def load_q(j, m):
                wait(eng, s_qk, UNITS * (4 * j + m - 3))
                eng.dma_start(queries[:, m, :, :].bitcast(F32),
                              q_scratch[bass.ds(j, 1), :, :, m, :].rearrange("o p n r -> (o p) n r")).then_inc(s_q[m], 16)

            load_v(0)

            for par in range(2):
                eng.wait_ge(shared.s_qst[par], 16 * KV_HEADS)

            def body(j):
                if not final(j):
                    load_k(j + 1)
                    load_q(j + 1, 0)
                    load_v(j + 1)
                for m in range(GROUP):
                    ending = m == GROUP - 1 and final(j)
                    if ending:
                        project_weights(0)
                        project_weights(1)
                    if m > 0:
                        if not final(j):
                            load_q(j + 1, m)
                        store(eng, j, m - 1)
                    if ending:
                        project_outputs(0)
                        project_outputs(1)
                        project_weights(2)
                        project_weights(3)
                        project_outputs(2)
                        project_outputs(3)
                if not final(j):
                    store(eng, j, GROUP - 1)
            def project_weights(c):
                if c < 2:
                    eng.wait_ge(s_qk, UNITS * HEADS)
                else:
                    eng.wait_ge(out.s_wlo, out.HEADS * (c - 1))
                out.load_weights(eng, c // 2, c % 2)

            def project_outputs(c):
                wait(eng, out.s_mm, c - 1)
                for n in range(2):
                    eng.wait_ge(s_ost[n], 16 * (c + 1))
                out.load_outputs(eng, c // 2, c % 2)

            heads(eng, body)

        @block.gpsimd
        def _(eng):

            def split_values(j, p):
                at = slice(2 * p, 2 * p + 2)
                wait(eng, s_pv, STEPS * (4 * j - 1) + p + 1)
                if p == 0:
                    wait(eng, s_vraw, 16 * (j + 1))
                eng.tensor_tensor(values[0][:, at, :], v_raw[:, at, :], ones, ALU.mult).then_inc(s_vhi, 1)
                low_values(j, p)

            def low_values(j, p):
                at = slice(2 * p, 2 * p + 2)
                eng.wait_ge(s_vhi, STEPS * j + p + 1)
                eng.tensor_tensor(values[1][:, at, :], v_raw[:, at, :], values[0][:, at, :].bitcast(F32),
                                  ALU.subtract).then_inc(s_vlo, 1)

            for p in range(STEPS):
                low_values(0, p)

            def body(j):
                for m in range(GROUP - 1):
                    split_output(eng, j, m)
                if not final(j):
                    for p in range(STEPS):
                        split_values(j + 1, p)
                    split_output(eng, j, GROUP - 1)
            heads(eng, body)

        @block.tensor
        def _(eng):
            def turn_keys(j, c):
                at, width = chunk_columns(c)
                if c == 0:
                    eng.wait_ge(s_kraw, 16 * (j + 1))
                    wait(eng, s_spread, 4 * j - 2)
                else:
                    eng.wait_ge(s_klo, CHUNKS * j + c)
                for k in range(width // P):
                    mm = eng.transpose(ps[:, AUX, k * P:(k + 1) * P], k_raw[:, at // P + k, :], core.ident[:, :])
                mm.then_inc(s_turn, 1)

            def unit(j, m, n):
                at, width = chunk_columns(n // 2)
                if n == 0:
                    eng.wait_ge(s_q[m], 16 * (j + 1))
                if m == 0 and n % 2 == 0:
                    eng.wait_ge(s_klo, CHUNKS * j + n // 2 + 1)
                wait(eng, s_se, UNITS * (4 * j + m) + n - 2)
                for i, (s, k) in enumerate(PASSES):
                    mm = eng.matmul(ps[:, S_BANK + n % 3, 0:width], queries[:, m, s, (n % 2) * P:(n % 2 + 1) * P],
                                    keysT[k][:, at:at + width], start=(i == 0), stop=(i == 2))
                mm.then_inc(s_qk, 1)

            def turn_probs(j, m, p):
                index = STEPS * (4 * j + m) + p
                bank = T_BANK + (m + p) % 2
                if p % 2 == 0:
                    eng.wait_ge(s_exp, UNITS * (4 * j + m) + p + 2)
                wait(eng, s_plo, index - 1)
                for k in range(2):
                    for r in range(ROW_TILES):
                        mm = eng.transpose(ps[:, bank, k * ROWS + r * P:k * ROWS + (r + 1) * P],
                                           scores[:, m % 2, r, (2 * p + k) * P:(2 * p + k + 1) * P], core.ident[:, :])
                mm.then_inc(s_pt, 1)

            def weigh_values(j, m, p):
                index = STEPS * (4 * j + m) + p
                eng.wait_ge(s_plo, index + 1)
                if m == 0:
                    eng.wait_ge(s_vlo, STEPS * j + p + 1)
                if p == 0:
                    wait(eng, s_on, 4 * j + m - 1)
                for k in range(2):
                    for i, (s, v) in enumerate(PASSES):
                        mm = eng.matmul(ps[:, O_BANK + m % 2, 0:ROWS], values[s][:, 2 * p + k, :],
                                        probsT[v][:, (m + p) % 2, k, :],
                                        start=(p == 0 and k == 0 and i == 0),
                                        stop=(p == STEPS - 1 and k == 1 and i == 2))
                mm.then_inc(s_pv, 1)

            def spread_sums(j, m):
                G = 4 * j + m
                eng.wait_ge(s_diag, G + 1)
                wait(eng, s_spread, G)
                if m == 2 and not final(j):
                    eng.wait_ge(s_klo, CHUNKS * (j + 2))
                eng.matmul(ps[:, AUX, 0:ROWS], core.ones[:, :], diag[:, :, :].rearrange("p t n -> p (t n)"),
                           start=True, stop=True).then_inc(s_bc, 1)

            def project(c, g):
                if (c, g) == (0, 0):
                    eng.wait_ge(s_se, UNITS * HEADS)
                    eng.wait_ge(s_on, HEADS - 1)
                eng.wait_ge(out.s_o[c], 16)
                eng.wait_ge(out.s_wlo, out.HEADS * c + g + 1)
                for t in range(ROW_TILES):
                    mm = out.product(eng, ps, c, t, g, (c, g) == (0, 0), False)
                if g == out.HEADS - 1:
                    mm.then_inc(out.s_mm, 1)

            for n in range(UNITS):
                unit(0, 0, n)
            turn_probs(0, 0, 0)

            def body(j):
                for m in range(GROUP):
                    more = not (final(j) and m == GROUP - 1)
                    j1, m1 = (j, m + 1) if m < GROUP - 1 else (j + 1, 0)
                    for p in range(STEPS):
                        if p < STEPS - 1:
                            turn_probs(j, m, p + 1)
                        elif more:
                            turn_probs(j1, m1, 0)
                        if more:
                            for n in QK_AT[p]:
                                unit(j1, m1, n)
                        if m == 2 and not final(j) and p in TURN_AT:
                            turn_keys(j + 1, TURN_AT[p])
                        if p == SPREAD_AT:
                            spread_sums(j, m)
                        if m == GROUP - 1 and final(j) and p in PRODUCT_AT:
                            project(*PRODUCT_AT[p])
                        weigh_values(j, m, p)
            heads(eng, body)

        @block.scalar
        def _(eng):
            def high_keys(j, c):
                at, width = chunk_columns(c)
                eng.wait_ge(s_turn, CHUNKS * j + c + 1)
                eng.activation(keysT[0][:, at:at + width], ps[:, AUX, 0:width], ACT.Copy).then_inc(s_khi, 1)

            def exponential(j, m, n):
                at, width = chunk_columns(n // 2)
                r, c = n % 2, n // 2
                if n == 0:
                    eng.wait_ge(s_max, 4 * j + m + 1)
                    wait(eng, s_sum, 4 * j + m - 1)
                eng.activation(scores[:, m % 2, r, at:at + width], scores[:, m % 2, r, at:at + width], ACT.Exp,
                               bias=minus_max[:, m % 2, r:r + 1],
                               accum_out=unit_sum[:, m % 2, r, c:c + 1]).then_inc(s_exp, 1)

            def high_probs(j, m, p):
                index = STEPS * (4 * j + m) + p
                eng.wait_ge(s_pt, index + 1)
                wait(eng, s_pv, index - 1)
                eng.activation(probsT[0][:, (m + p) % 2, :, :],
                               ps[:, T_BANK + (m + p) % 2, :].rearrange("p (k r) -> p k r", r=ROWS),
                               ACT.Copy).then_inc(s_phi, 1)

            def copy_spread(j, m):
                eng.wait_ge(s_bc, 4 * j + m + 1)
                wait(eng, s_on, 4 * j + m)
                eng.activation(spread[:, :], ps[:, AUX, 0:ROWS], ACT.Copy).then_inc(s_spread, 1)

            eng.wait_ge(s_vraw, 16)
            for p in range(STEPS):
                eng.activation(values[0][:, 2 * p:2 * p + 2, :], v_raw[:, 2 * p:2 * p + 2, :], ACT.Copy).then_inc(s_vhi, 1)
            for n in range(5):
                exponential(0, 0, n)
            high_probs(0, 0, 0)

            def body(j):
                for m in range(GROUP):
                    more = not (final(j) and m == GROUP - 1)
                    j1, m1 = (j, m + 1) if m < GROUP - 1 else (j + 1, 0)
                    for p in range(STEPS):
                        if p < STEPS - 1:
                            high_probs(j, m, p + 1)
                        elif more:
                            high_probs(j1, m1, 0)
                        for n in LATE_EXP.get(p, ()):
                            exponential(j, m, n)
                        if more:
                            for n in EARLY_EXP.get(p, ()):
                                exponential(j1, m1, n)
                        if m == 2 and not final(j) and p in TURN_AT:
                            high_keys(j + 1, TURN_AT[p])
                        if m == GROUP - 1 and final(j) and p in SPLIT_AT:
                            c, g = SPLIT_AT[p]
                            wait(eng, out.s_mm, c - 1)
                            out.high(eng, c // 2, c % 2, g)
                        if p == SPREAD_AT:
                            copy_spread(j, m)
            heads(eng, body)

        @block.vector
        def _(eng):
            def low_keys(j, c):
                at, width = chunk_columns(c)
                eng.wait_ge(s_khi, CHUNKS * j + c + 1)
                eng.tensor_tensor(keysT[1][:, at:at + width], ps[:, AUX, 0:width],
                                  keysT[0][:, at:at + width].bitcast(F32), ALU.subtract).then_inc(s_klo, 1)

            def drain_unit(j, m, n):
                at, width = chunk_columns(n // 2)
                r, c = n % 2, n // 2
                G = 4 * j + m
                eng.wait_ge(s_qk, UNITS * G + n + 1)
                if n == 0:
                    wait(eng, s_pt, STEPS * (G - 1))
                if isinstance(j, int) and (G, n) == (1, 0):
                    for par in range(2):
                        eng.wait_ge(shared.s_qst[par], 16 * KV_HEADS)
                eng.tensor_scalar(scores[:, m % 2, r, at:at + width], ps[:, S_BANK + n % 3, 0:width], 1.0, None,
                                  ALU.mult, ALU.max, accum_out=unit_max[:, m % 2, r, c:c + 1]).then_inc(s_se, 1)

            def maximum(j, m):
                G = 4 * j + m
                eng.wait_ge(s_se, UNITS * (G + 1))
                wait(eng, s_exp, UNITS * (G - 1))
                eng.tensor_reduce(minus_max[:, m % 2, :], unit_max[:, m % 2, :, :], AX.X, ALU.max,
                                  negate=True).then_inc(s_max, 1)

            def low_probs(j, m, p):
                index = STEPS * (4 * j + m) + p
                eng.wait_ge(s_phi, index + 1)
                eng.tensor_tensor(probsT[1][:, (m + p) % 2, :, :],
                                  ps[:, T_BANK + (m + p) % 2, :].rearrange("p (k r) -> p k r", r=ROWS),
                                  probsT[0][:, (m + p) % 2, :, :].bitcast(F32), ALU.subtract).then_inc(s_plo, 1)

            def invert_sums(j, m):
                G = 4 * j + m
                eng.wait_ge(s_exp, UNITS * (G + 1))
                eng.tensor_reduce(row_sum[:, 0, :], unit_sum[:, m % 2, :, :], AX.X, ALU.add).then_inc(s_sum, 1)
                eng.wait_ge(s_sum, G + 1)
                eng.reciprocal(row_sum[:, 1, :], row_sum[:, 0, :]).then_inc(s_inv, 1)
                eng.wait_ge(s_inv, G + 1)
                wait(eng, s_bc, G)
                for r in range(ROW_TILES):
                    ins = eng.tensor_scalar(diag[:, r, :], core.ident[:, :], row_sum[:, 1, r:r + 1], None, ALU.mult)
                ins.then_inc(s_diag, 1)

            for n in range(UNITS):
                drain_unit(0, 0, n)
            maximum(0, 0)
            low_probs(0, 0, 0)

            def body(j):
                for m in range(GROUP):
                    more = not (final(j) and m == GROUP - 1)
                    j1, m1 = (j, m + 1) if m < GROUP - 1 else (j + 1, 0)
                    for p in range(STEPS):
                        if p < STEPS - 1:
                            low_probs(j, m, p + 1)
                        elif more:
                            low_probs(j1, m1, 0)
                        if p == 0 and m > 0:
                            norm_output(eng, j, m - 1)
                        if more:
                            for n in QK_AT[p]:
                                drain_unit(j1, m1, n)
                            if p == 12:
                                maximum(j1, m1)
                        if m == 2 and not final(j) and p in TURN_AT:
                            low_keys(j + 1, TURN_AT[p])
                        if m == GROUP - 1 and final(j) and p in SPLIT_AT:
                            c, g = SPLIT_AT[p]
                            out.low(eng, c // 2, c % 2, g)
                        if p == SUM_AT:
                            invert_sums(j, m)
                if not final(j):
                    norm_output(eng, j, GROUP - 1)
            heads(eng, body)

    return norm_output, split_output, store


ADAPTER_WORDS = ROW_TILES * (HID + 2 * 6 + 4) + HID + HID_TILES * RANK + 2 * HID_TILES * BANK


class Adapters:

    def __init__(self, core, stack):
        self.normed = core.sbuf("f_xn", [P, ROW_TILES, HID], stack=stack)
        self.stats = core.sbuf("f_ln_stats", [P, ROW_TILES, 2, 6], stack=stack)
        self.mv = core.sbuf("f_ln_mv", [P, ROW_TILES, 4], stack=stack)
        self.a_shared = core.sbuf("f_a_shared", [RANK, HID], stack=stack)
        self.b_shared = core.sbuf("f_b_shared", [P, HID_TILES, RANK], stack=stack)
        self.raw = [core.sbuf(f"f_raw{n}", [P, HID_TILES, BANK], stack=stack) for n in range(2)]
        self.s_a = core.sem("f_a_loaded")
        self.s_b = core.sem("f_b_loaded")
        self.s_ln = core.sem("f_ln_steps")
        self.s_var = core.sem("f_var_ready")
        self.s_rstd = core.sem("f_rstd_ready")

    def load_a(self, eng, a):
        eng.dma_start(self.raw[0][:, :, :].rearrange("p k n -> p (k n)").rearrange("p (t i) -> p t i", i=HID),
                      a["lora_A"].rearrange("n r i -> (n r) i").rearrange("(t p) i -> p t i", p=P)).then_inc(self.s_a, 16)
        eng.dma_start(self.a_shared[:, :], a["lora_A_shared"]).then_inc(self.s_a, 16)

    def load_b(self, eng, a):
        for t in range(HID_TILES):
            eng.dma_start(self.raw[1][:, t, :].rearrange("p (n r) -> p n r", r=RANK),
                          a["lora_B"][:, t * P:(t + 1) * P, :].rearrange("n p r -> p n r")).then_inc(self.s_b, 16)
        eng.dma_start(self.b_shared[:, :, :], a["lora_B_shared"].rearrange("(t p) r -> p t r", p=P)).then_inc(self.s_b, 16)


class SelfBuffers:
    QKV = HID + 2 * KV_HEADS * SELF_DIM
    QK = HID + KV_HEADS * SELF_DIM
    TURNED = HID // (GROUP * SELF_DIM)

    def __init__(self, core, stack):
        QK, QKV, TURNED = self.QK, self.QKV, self.TURNED
        self.normed = core.sbuf("a_xn", [P, ROW_TILES, HID], stack=stack)
        self.stats = core.sbuf("a_ln_stats", [P, ROW_TILES, 2, 6], stack=stack)
        self.mv = core.sbuf("a_ln_mv", [P, ROW_TILES, 4], stack=stack)
        self.turned = core.sbuf("a_rope_products", [P, 4, QK // 2], stack=stack)
        self.qk = core.sbuf("a_qk_rows", [P, ROW_TILES, QK], stack=stack)
        self.k_copies = core.sbuf("a_k_copies", [P, ROW_TILES, KV_HEADS, GROUP, SELF_DIM], stack=stack)
        self.qT = core.sbuf("a_qT", [P, TURNED, ROWS], stack=stack)
        self.kT = core.sbuf("a_kT", [P, TURNED, ROWS], stack=stack)
        self.xT = [core.sbuf(f"a_xnT_part{n}", [P, HID_TILES, ROWS], F32R, stack=stack) for n in range(2)]
        self.w_raw = core.sbuf("a_w_raw", [P, 2, HID], stack=stack)
        self.w_part = [core.sbuf(f"a_w_part{n}", [P, HID_TILES, QKV], F32R, stack=stack) for n in range(2)]
        self.tables = core.sbuf("a_rope_tables", [P, ROW_TILES, 2, SELF_DIM // 2], stack=stack)
        self.mask = core.sbuf("a_mask", [P, P], stack=stack)
        self.v = core.sbuf("a_v_rows", [P, ROW_TILES, KV_HEADS * SELF_DIM], stack=stack)
        self.scores = core.sbuf("a_scores", [P, 3, GROUP, ROWS], stack=stack)
        self.probsT = core.sbuf("a_probsT", [P, 2, 2, BANK], stack=stack)
        self.stepT = core.sbuf("a_step_outT", [P, 2, P], stack=stack)
        self.small = core.sbuf("a_small", [P, ROW_TILES * KV_HEADS, 4, GROUP], stack=stack)
        self.s_w = core.sem("a_qkv_weights_loaded")
        self.s_whi = core.sem("a_qkv_weights_hi")
        self.s_wlo = core.sem("a_qkv_weights_lo")
        self.piece = self.w_raw[:, :, :].rearrange("p two n -> p (two n)")[:, 0:QKV].unsqueeze(1)
        self.s_x = core.sem("a_tables_loaded")
        self.s_ln = core.sem("a_ln_steps")
        self.s_var = core.sem("a_var_ready")
        self.s_rstd = core.sem("a_rstd_ready")

    BESIDE = HID_TILES - 2

    def load_piece(self, eng, a, k):
        wait(eng, self.s_wlo, k)
        KV = KV_HEADS * SELF_DIM
        for w, at, n in (("wq", 0, HID), ("wk", HID, KV), ("wv", HID + KV, KV)):
            eng.dma_start(self.piece[:, 0, at:at + n],
                          a[w].rearrange("(k p) n -> p k n", p=P)[:, bass.ds(k, 1), :]
                          .rearrange("p o n -> p (o n)")).then_inc(self.s_w, 16)

    def high_piece(self, eng, k):
        eng.wait_ge(self.s_w, 48 * (k + 1))
        eng.activation(self.w_part[0][:, bass.ds(k, 1), :], self.piece, ACT.Copy).then_inc(self.s_whi, 1)

    def low_piece(self, eng, k):
        eng.wait_ge(self.s_whi, k + 1)
        eng.tensor_tensor(self.w_part[1][:, bass.ds(k, 1), :], self.piece,
                          self.w_part[0][:, bass.ds(k, 1), :].bitcast(F32), ALU.subtract).then_inc(self.s_wlo, 1)


def project_attention(core, a, shared, out, own, norm_output, split_output, store):
    nc, ps = core.nc, core.psum
    LAST_HEAD = KV_HEADS - 1, GROUP - 1
    PAIRS = HEADS // out.HEADS // 2
    s_mm = out.s_mm
    s_xd = core.sem("p_x_sums")

    with nc.Block() as block:
        @block.sync
        def _(eng):
            def load(i, par):
                c = 2 * i + par
                eng.wait_ge(out.s_wlo, out.HEADS * (c - 1))
                out.load_weights(eng, i, par)
                eng.wait_ge(s_mm, c - 1)
                for n in range(2):
                    eng.wait_ge(shared.s_ost[n], 16 * (c + 1))
                out.load_outputs(eng, i, par)

            store(eng, *LAST_HEAD)
            load(2, 0)
            load(2, 1)
            for n in range(2):
                eng.wait_ge(shared.s_ost[n], 16 * HEADS // 2)
            eng.dma_start(own.tables[:, :, :, :], a["rope"].rearrange("(t p) c n -> p t c n", p=P)).then_inc(own.s_x, 16)
            eng.dma_start(own.mask[:, :], a["mask"]).then_inc(own.s_x, 16)
            own.load_piece(eng, a, 0)
            with eng.Fori(3, PAIRS) as i:
                load(i, 0)
                load(i, 1)
                own.load_piece(eng, a, i - 2)
            own.load_piece(eng, a, own.BESIDE)

        @block.tensor
        def _(eng):
            def products(i, par):
                c = 2 * i + par
                eng.wait_ge(out.s_o[par], 16 * (i + 1))
                for g in range(out.HEADS):
                    eng.wait_ge(out.s_wlo, out.HEADS * c + g + 1)
                    for t in range(ROW_TILES):
                        mm = out.product(eng, ps, par, t, g, False, False)
                mm.then_inc(s_mm, 1)
            with eng.Fori(1, PAIRS - 1) as i:
                products(i, 0)
                products(i, 1)
            first = [(0, 0, 0), (0, 0, 1), (1, 0, 0), (0, 1, 0), (0, 1, 1)]
            then = [(1, 0, 1), (1, 1, 0), (1, 1, 1)]
            for part in (first, then):
                for t, par, g in part:
                    eng.wait_ge(out.s_o[par], 16 * PAIRS)
                    eng.wait_ge(out.s_wlo, out.HEADS * (2 * PAIRS - 2 + par) + g + 1)
                    mm = out.product(eng, ps, par, t, g, False, (par, g) == (1, out.HEADS - 1))
                mm.then_inc(s_mm, 1)

        @block.gpsimd
        def _(eng):
            split_output(eng, *LAST_HEAD)
            layer_norm_pool(eng, core, own.mv, own.s_var, own.s_rstd, (0,))

        @block.scalar
        def _(eng):
            def split(i, par):
                eng.wait_ge(s_mm, 2 * i + par - 1)
                for g in range(out.HEADS):
                    out.high(eng, i, par, g)

            split(2, 0)
            split(2, 1)
            own.high_piece(eng, 0)
            with eng.Fori(3, PAIRS) as i:
                split(i, 0)
                split(i, 1)
                own.high_piece(eng, i - 2)

        @block.vector
        def _(eng):
            def split(i, par):
                for g in range(out.HEADS):
                    out.low(eng, i, par, g)

            norm_output(eng, *LAST_HEAD)
            split(2, 0)
            split(2, 1)
            own.low_piece(eng, 0)
            with eng.Fori(3, PAIRS) as i:
                split(i, 0)
                split(i, 1)
                own.low_piece(eng, i - 2)
            for t in range(ROW_TILES):
                eng.wait_ge(s_mm, 2 * PAIRS - 1 + t)
                eng.tensor_tensor(core.x[:, t, :].rearrange("p (b n) -> p b n", n=BANK),
                                  ps[:, out.banks(t), :],
                                  core.x[:, t, :].rearrange("p (b n) -> p b n", n=BANK), ALU.add).then_inc(s_xd, 1)
                if t == 0:
                    eng.wait_ge(s_xd, 1)
                    layer_norm_tile(eng, core.x, own.normed, own.stats, own.mv, 0, own.s_ln, own.s_var, own.s_rstd)


def self_attention(core, a, own, adapters):
    nc, ps = core.nc, core.psum
    QKV, QK = own.QKV, own.QK
    STEPS = ROW_TILES * KV_HEADS
    SCALE = float(1.0 / np.sqrt(SELF_DIM))
    HALF = SELF_DIM // 2
    normed, xT, w_raw, w_part, turned, qk, v = own.normed, own.xT, own.w_raw, own.w_part, own.turned, own.qk, own.v
    k_copies, qT, kT, scores, probsT, small = own.k_copies, own.qT, own.kT, own.scores, own.probsT, own.small
    tables, mask, stats, mv = own.tables, own.mask, own.stats, own.mv

    s_w = [core.sem(f"a_w_loaded{n}") for n in range(2)]
    s_whi = core.sem("a_w_hi")
    s_wlo = core.sem("a_w_lo")
    s_ln, s_var, s_rstd = own.s_ln, own.s_var, own.s_rstd
    s_t = core.sem("a_transposed")
    s_hi = core.sem("a_hi")
    s_lo = core.sem("a_lo")
    s_mm = core.sem("a_products")
    s_v = core.sem("a_v_rows_ready")
    s_rp = core.sem("a_rope_products_ready")
    s_rope = core.sem("a_rope_ready")
    s_kc = core.sem("a_k_copied")
    s_qt = core.sem("a_qk_turned")
    s_qta = core.sem("a_qT_ready")
    s_kta = core.sem("a_kT_ready")
    s_s = core.sem("a_scores_product")
    s_masked = core.sem("a_masked")
    s_mx = core.sem("a_max")
    s_nm = core.sem("a_minus_max")
    s_exp = core.sem("a_exp")
    s_pt = core.sem("a_probs_turned")
    s_pa = core.sem("a_probsT")
    s_pv = core.sem("a_pv")
    s_oc = core.sem("a_out_copied")
    s_ot = core.sem("a_out_turned")
    s_inv = core.sem("a_inverse")
    s_out = core.sem("a_out_rows")
    s_xd = core.sem("a_x_sums")

    def width(x):
        return P * (x // KV_HEADS + 1)

    SECOND_AT = (2, 3, 4, 5)

    with nc.Block() as block:
        @block.sync
        def _(eng):
            own.load_piece(eng, a, HID_TILES - 1)
            eng.wait_ge(own.s_wlo, HID_TILES)
            for k in range(HID_TILES):
                if k == HID_TILES // 2:
                    eng.wait_ge(s_qt, 6)
                    adapters.load_a(eng, a)
                wait(eng, s_wlo, k - 1)
                eng.dma_start(w_raw[:, k % 2, 0:HID], a["wo"][k * P:(k + 1) * P, :]).then_inc(s_w[k % 2], 16)
            eng.wait_ge(s_s, STEPS)
            adapters.load_b(eng, a)

        @block.gpsimd
        def _(eng):
            layer_norm_pool(eng, core, mv, s_var, s_rstd, (1,))
            for t in range(ROW_TILES):
                pair = qk[:, t, :].rearrange("p (n two) -> p n two", two=2)
                eng.wait_ge(s_rp, 4 * t + 4)
                eng.tensor_tensor(pair[:, :, 0], turned[:, 0, :], turned[:, 1, :], ALU.subtract)
                eng.tensor_tensor(pair[:, :, 1], turned[:, 2, :], turned[:, 3, :], ALU.add).then_inc(s_rope, 1)
            layer_norm_pool(eng, core, adapters.mv, adapters.s_var, adapters.s_rstd, (0,))

        @block.tensor
        def _(eng):
            def turn_rows(src, t, bank, step=1):
                for k in range(HID_TILES):
                    mm = eng.transpose(ps[:, bank + step * (k // 4), (k % 4) * P:(k % 4 + 1) * P],
                                       src[:, t, k * P:(k + 1) * P], core.ident[:, :])
                return mm

            def turn_normed(t):
                eng.wait_ge(s_ln, 4 * (t + 1))
                wait(eng, s_lo, t)
                turn_rows(normed, t, 6).then_inc(s_t, 1)

            copies = k_copies[:, :, :, :, :].rearrange("p t j g d -> p t (j g d)")

            def turn_first(n):
                if n == 0:
                    eng.wait_ge(s_rope, 1)
                    turn_rows(qk, 0, 3, 4).then_inc(s_qt, 1)
                else:
                    eng.wait_ge(s_kc, 1)
                    eng.wait_ge(s_rp, 4)
                    eng.wait_ge(s_v, 1)
                    turn_rows(copies, 0, 0).then_inc(s_qt, 1)

            turn_normed(0)
            for t in range(ROW_TILES):
                eng.wait_ge(s_lo, t + 1)
                for k in range(HID_TILES):
                    if (t, k) == (0, HID_TILES // 2):
                        turn_normed(1)
                    if t == 1 and k >= HID_TILES - 2:
                        turn_first(k - (HID_TILES - 2))
                    if t == 0:
                        eng.wait_ge(own.s_wlo, k + 1)
                    for n, (s, m) in enumerate(PASSES):
                        for b in range(QKV // BANK):
                            mm = eng.matmul(ps[:, 4 * t + b, :], xT[s][:, k, t * P:(t + 1) * P],
                                            w_part[m][:, k, b * BANK:(b + 1) * BANK],
                                            start=(k == 0 and n == 0), stop=(k == HID_TILES - 1 and n == 2))
                mm.then_inc(s_mm, 1)
            def turn_second(n):
                if n == 0:
                    eng.wait_ge(s_v, 2)
                    eng.wait_ge(s_rope, 2)
                elif n == 2:
                    eng.wait_ge(s_kc, 2)
                wait(eng, s_qta, (1, 2, 3, 3)[n])
                wait(eng, s_kta, (0, 0, 0, 2)[n])
                for k in range(GROUP):
                    src = (qk, copies)[n // 2]
                    at = (n % 2) * BANK + k * P
                    mm = eng.transpose(ps[:, 5, k * P:(k + 1) * P], src[:, 1, at:at + P], core.ident[:, :])
                mm.then_inc(s_qt, 1)

            def score(x):
                t, j = x // KV_HEADS, x % KV_HEADS
                wait(eng, s_masked, x)
                for r in range(GROUP):
                    at = slice(r * SELF_DIM, (r + 1) * SELF_DIM)
                    mm = eng.matmul(ps[:, r, 0:width(x)],
                                    qT[at, j, t * P:(t + 1) * P], kT[at, j, 0:width(x)], start=True, stop=True)
                mm.then_inc(s_s, 1)

            def turn_probs(x):
                eng.wait_ge(s_exp, x + 1)
                wait(eng, s_pa, x)
                for k in range(x // KV_HEADS + 1):
                    for r in range(GROUP):
                        mm = eng.transpose(ps[:, 4 + k, r * P:(r + 1) * P],
                                           scores[:, x % 3, r, k * P:(k + 1) * P], core.ident[:, :])
                mm.then_inc(s_pt, 1)

            def weigh(x):
                t, j = x // KV_HEADS, x % KV_HEADS
                eng.wait_ge(s_pa, x + 1)
                wait(eng, s_out, x - 1)
                for r in range(GROUP):
                    for k in range(t + 1):
                        mm = eng.matmul(ps[r * SELF_DIM:(r + 1) * SELF_DIM, 6 + x % 2, 0:P],
                                        v[:, k, j * SELF_DIM:(j + 1) * SELF_DIM],
                                        probsT[:, x % 2, k, r * P:(r + 1) * P], start=(k == 0), stop=(k == t))
                mm.then_inc(s_pv, 1)

            def turn_out(x):
                eng.wait_ge(s_oc, x + 1)
                eng.transpose(ps[:, 6 + x % 2, P:2 * P], own.stepT[:, x % 2, :], core.ident[:, :]).then_inc(s_ot, 1)

            def project(t, bank, pieces):
                eng.wait_ge(s_lo, ROW_TILES + t + 1)
                for k in pieces:
                    eng.wait_ge(s_wlo, k + 1)
                    for n, (s, m) in enumerate(PASSES):
                        for half in range(2):
                            mm = eng.matmul(ps[:, bank + half, :], xT[s][:, k, t * P:(t + 1) * P],
                                            w_part[m][:, k, half * BANK:(half + 1) * BANK],
                                            start=(k == 0 and n == 0), stop=(k == HID_TILES - 1 and n == 2))
                return mm

            eng.wait_ge(s_qta, 1)
            eng.wait_ge(s_kta, 1)
            score(0)
            score(1)
            eng.wait_ge(s_rp, 8)
            eng.wait_ge(s_v, ROW_TILES)
            for x in range(STEPS):
                if x in SECOND_AT:
                    turn_second(SECOND_AT.index(x))
                if x + 2 == KV_HEADS:
                    eng.wait_ge(s_qta, 3)
                    eng.wait_ge(s_kta, 3)
                if x + 2 < STEPS:
                    score(x + 2)
                if x == STEPS - 2:
                    eng.wait_ge(s_out, KV_HEADS)
                    eng.wait_ge(s_masked, STEPS)
                    turn_rows(normed, 0, 0).then_inc(s_t, 1)
                turn_probs(x)
                if x > 0:
                    weigh(x - 1)
                if x > 1:
                    turn_out(x - 2)
            project(0, 2, range(0, 2))
            weigh(STEPS - 1)
            turn_out(STEPS - 2)
            project(0, 2, range(2, 3))
            turn_out(STEPS - 1)
            project(0, 2, range(3, 5))
            eng.wait_ge(s_out, STEPS)
            turn_rows(normed, 1, 4).then_inc(s_t, 1)
            project(0, 2, range(5, HID_TILES)).then_inc(s_mm, 1)
            project(1, 6, range(HID_TILES)).then_inc(s_mm, 1)

        @block.scalar
        def _(eng):
            def split(k):
                eng.wait_ge(s_w[k % 2], 16 * (k // 2 + 1))
                eng.activation(w_part[0][:, k, 0:HID], w_raw[:, k % 2, 0:HID], ACT.Copy).then_inc(s_whi, 1)

            def high(t, count, bank):
                eng.wait_ge(s_t, count)
                eng.activation(xT[0][:, :, t * P:(t + 1) * P],
                               ps[:, bank:bank + 2, :].rearrange("p b (k n) -> p (b k) n", n=P),
                               ACT.Copy).then_inc(s_hi, 1)

            def copy_keys(t):
                eng.wait_ge(s_rope, t + 1)
                eng.activation(k_copies[:, t, :, :, :],
                               qk[:, t, HID:QK].rearrange("p (j d) -> p j d", d=SELF_DIM).unsqueeze(2)
                               .broadcast_to([P, KV_HEADS, GROUP, SELF_DIM]), ACT.Copy).then_inc(s_kc, 1)

            for t in range(ROW_TILES):
                high(t, t + 1, 6)
                own.high_piece(eng, own.BESIDE + t)
            for t in range(ROW_TILES):
                eng.wait_ge(s_mm, t + 1)
                eng.activation(v[:, t, :], ps[:, 4 * t + 2, QK - 2 * BANK:BANK], ACT.Copy).then_inc(s_v, 1)
                if t == 0:
                    copy_keys(0)
                    eng.wait_ge(s_qt, 1)
                    for half, bank in enumerate((3, 7)):
                        ins = eng.activation(qT[:, GROUP * half:GROUP * (half + 1), 0:P],
                                             ps[:, bank, :].rearrange("p (k n) -> p k n", n=P), ACT.Copy)
                    ins.then_inc(s_qta, 1)
            def exponential(x):
                eng.wait_ge(s_nm, x + 1)
                for r in range(GROUP):
                    ins = eng.activation(scores[:, x % 3, r, 0:width(x)], scores[:, x % 3, r, 0:width(x)], ACT.Exp,
                                         scale=SCALE, bias=small[:, x, 1, r:r + 1],
                                         accum_out=small[:, x, 2, r:r + 1])
                ins.then_inc(s_exp, 1)

            def copy_out(x):
                eng.wait_ge(s_pv, x + 1)
                wait(eng, s_ot, x - 1)
                eng.activation(own.stepT[:, x % 2, :], ps[:, 6 + x % 2, 0:P], ACT.Copy).then_inc(s_oc, 1)

            exponential(0)
            for x in range(STEPS):
                if x + 1 < STEPS:
                    exponential(x + 1)
                eng.wait_ge(s_pt, x + 1)
                wait(eng, s_pv, x - 1)
                tiles = x // KV_HEADS + 1
                eng.activation(probsT[:, x % 2, 0:tiles, :], ps[:, 4:4 + tiles, :], ACT.Copy).then_inc(s_pa, 1)
                if x > 0:
                    copy_out(x - 1)
                if x == STEPS - 2:
                    high(0, ROW_TILES + 1, 0)
                if x == SECOND_AT[0]:
                    copy_keys(1)
                if x + 1 in SECOND_AT[:2]:
                    half = SECOND_AT.index(x + 1)
                    eng.wait_ge(s_qt, 3 + half)
                    eng.activation(qT[:, GROUP * half:GROUP * (half + 1), P:ROWS],
                                   ps[:, 5, :].rearrange("p (k n) -> p k n", n=P), ACT.Copy).then_inc(s_qta, 1)
                if x % 2:
                    split(x // 2)
            copy_out(STEPS - 1)
            high(1, ROW_TILES + 2, 4)

        @block.vector
        def _(eng):
            def split(k):
                eng.wait_ge(s_whi, k + 1)
                eng.tensor_tensor(w_part[1][:, k, 0:HID], w_raw[:, k % 2, 0:HID],
                                  w_part[0][:, k, 0:HID].bitcast(F32), ALU.subtract).then_inc(s_wlo, 1)

            def low(t, count, bank):
                eng.wait_ge(s_hi, count)
                eng.tensor_tensor(xT[1][:, :, t * P:(t + 1) * P],
                                  ps[:, bank:bank + 2, :].rearrange("p b (k n) -> p (b k) n", n=P),
                                  xT[0][:, :, t * P:(t + 1) * P].bitcast(F32), ALU.subtract).then_inc(s_lo, 1)

            for t in range(ROW_TILES):
                low(t, t + 1, 6)
                if t == 0:
                    layer_norm_tile(eng, core.x, normed, stats, mv, 1, s_ln, s_var, s_rstd)
                own.low_piece(eng, own.BESIDE + t)
            eng.wait_ge(own.s_x, 32)
            for t in range(ROW_TILES):
                eng.wait_ge(s_mm, t + 1)
                rows = ps[:, 4 * t:4 * t + 3, :].rearrange("p b n -> p (b n)")[:, 0:QK]
                pair = rows.rearrange("p (h n two) -> p h n two", n=HALF, two=2)
                wait(eng, s_rope, t)
                eng.wait_ge(s_v, t + 1)
                for n, (odd, sine) in enumerate(((0, 0), (1, 1), (0, 1), (1, 0))):
                    table = tables[:, t, sine, :].unsqueeze(1).broadcast_to([P, QK // SELF_DIM, HALF])
                    eng.tensor_tensor(turned[:, n, :].rearrange("p (h n) -> p h n", n=HALF), pair[:, :, :, odd],
                                      table, ALU.mult).then_inc(s_rp, 1)
                if t == 0:
                    eng.wait_ge(s_qt, 2)
                    eng.tensor_copy(kT[:, :, 0:P], ps[:, 0:2, :].rearrange("p b (k n) -> p (b k) n", n=P)).then_inc(s_kta, 1)

            def maximum(x):
                w = width(x)
                eng.wait_ge(s_s, x + 1)
                wait(eng, s_pt, x - 2)
                if x >= KV_HEADS:
                    eng.tensor_copy(scores[:, x % 3, :, 0:P], ps[:, 0:GROUP, 0:P])
                eng.tensor_tensor(scores[:, x % 3, :, w - P:w], ps[:, 0:GROUP, w - P:w],
                                  mask[:, :].unsqueeze(1).broadcast_to([P, GROUP, P]), ALU.add).then_inc(s_masked, 1)
                eng.wait_ge(s_masked, x + 1)
                eng.tensor_reduce(small[:, x, 0, :], scores[:, x % 3, :, 0:w], AX.X, ALU.max).then_inc(s_mx, 1)
                eng.wait_ge(s_mx, x + 1)
                eng.tensor_scalar(small[:, x, 1, :], small[:, x, 0, :], -SCALE, None, ALU.mult).then_inc(s_nm, 1)

            def norm(x):
                t, j = x // KV_HEADS, x % KV_HEADS
                eng.wait_ge(s_exp, x + 1)
                eng.reciprocal(small[:, x, 3, :], small[:, x, 2, :]).then_inc(s_inv, 1)
                eng.wait_ge(s_inv, x + 1)
                eng.wait_ge(s_ot, x + 1)
                eng.tensor_tensor(normed[:, t, j * P:(j + 1) * P].rearrange("p (g d) -> p g d", d=SELF_DIM),
                                  ps[:, 6 + x % 2, P:2 * P].rearrange("p (g d) -> p g d", d=SELF_DIM),
                                  over_last(small[:, x, 3, :], (P, GROUP, SELF_DIM)), ALU.mult).then_inc(s_out, 1)

            maximum(0)
            maximum(1)
            for x in range(STEPS):
                if x in SECOND_AT[2:]:
                    half = SECOND_AT.index(x) - 2
                    eng.wait_ge(s_qt, 5 + half)
                    eng.tensor_copy(kT[:, GROUP * half:GROUP * (half + 1), P:ROWS],
                                    ps[:, 5, :].rearrange("p (k n) -> p k n", n=P)).then_inc(s_kta, 1)
                if x + 2 < STEPS:
                    maximum(x + 2)
                if x > 1:
                    norm(x - 2)
                if x == STEPS - 2:
                    low(0, ROW_TILES + 1, 0)
                if x % 2:
                    split(x // 2)
            norm(STEPS - 2)
            norm(STEPS - 1)
            low(1, ROW_TILES + 2, 4)
            for t in range(ROW_TILES):
                eng.wait_ge(s_mm, ROW_TILES + t + 1)
                eng.tensor_tensor(core.x[:, t, :].rearrange("p (b n) -> p b n", n=BANK),
                                  ps[:, 2 + 4 * t:4 + 4 * t, :],
                                  core.x[:, t, :].rearrange("p (b n) -> p b n", n=BANK), ALU.add).then_inc(s_xd, 1)
                if t == 0:
                    eng.wait_ge(s_xd, 1)
                    layer_norm_tile(eng, core.x, adapters.normed, adapters.stats, adapters.mv, 0,
                                    adapters.s_ln, adapters.s_var, adapters.s_rstd)


def feed_forward(core, a, adapters, own, out):
    nc, ps = core.nc, core.psum
    NR = LORAS * RANK
    A_TILES = NR // P
    raw, a_shared, b_shared, s_a, s_b = adapters.raw, adapters.a_shared, adapters.b_shared, adapters.s_a, adapters.s_b
    normed, stats, mv = adapters.normed, adapters.stats, adapters.mv
    s_ln, s_var, s_rstd = adapters.s_ln, adapters.s_var, adapters.s_rstd
    aT = [core.sbuf(f"f_aT_part{n}", [P, HID_TILES, NR + RANK], F32R, stack=own) for n in range(2)]
    bT = [core.sbuf(f"f_bT_part{n}", [P, A_TILES, HID], F32R, stack=own) for n in range(2)]
    bsT = [core.sbuf(f"f_bsT_part{n}", [RANK, HID], F32R, stack=own) for n in range(2)]
    w_part = [core.sbuf(f"f_w_part{n}", [P, HID_TILES, BANK], F32R, stack=own) for n in range(2)]
    xT = [core.sbuf(f"f_xnT_part{n}", [P, HID_TILES, ROWS], F32R, stack=own) for n in range(2)]
    gates = core.sbuf("f_gates", [P, ROW_TILES, LORAS], stack=own)
    bias = core.sbuf("f_bias", [P, HID], stack=own)
    z = core.sbuf("f_z", [P, ROW_TILES, NR + RANK], stack=own)
    zT = [core.sbuf(f"f_zT_part{n}", [P, ROW_TILES, NR], F32R, stack=own) for n in range(2)]
    zsT = [core.sbuf(f"f_zsT_part{n}", [RANK, ROWS], F32R, stack=own) for n in range(2)]

    s_small = core.sem("f_gates_bias_loaded")
    s_w = [core.sem(f"f_w_loaded{n}") for n in range(2)]
    s_t = core.sem("f_adapters_turned")
    s_hi = core.sem("f_adapters_hi")
    s_lo = core.sem("f_adapters_lo")
    s_whi = core.sem("f_w_hi")
    s_wlo = core.sem("f_w_lo")
    s_xt = core.sem("f_xn_turned")
    s_xhi = core.sem("f_xn_hi")
    s_xlo = core.sem("f_xn_lo")
    s_ax = core.sem("f_ax_product")
    s_z = core.sem("f_z_rows")
    s_zt = core.sem("f_z_turned")
    s_zhi = core.sem("f_z_hi")
    s_zlo = core.sem("f_z_lo")
    s_xb = core.sem("f_x_plus_bias")
    s_mm = core.sem("f_products")
    s_done = core.sem("f_products_and_adapters")
    s_sum = core.sem("f_sums")
    s_out = core.sem("f_stored")

    fills = []
    fills.append(("a", [(a_shared[:, k * P:(k + 1) * P], k * RANK, RANK) for k in range(HID_TILES)],
                  P, HID_TILES * RANK, [part[:, :, NR:NR + RANK] for part in aT]))
    for k in range(HID_TILES):
        fills.append(("a", [(raw[0][:, :, :].rearrange("p k n -> p (k n)")[:, t * HID + k * P:t * HID + (k + 1) * P], t * P, P)
                            for t in range(A_TILES)], P, NR, [part[:, k, 0:NR] for part in aT]))
    for q in range(A_TILES):
        for h in range(2):
            fills.append(("b", [(raw[1][:, 4 * h + t, q * P:(q + 1) * P], t * P, P) for t in range(4)],
                          P, BANK, [part[:, q, h * BANK:(h + 1) * BANK] for part in bT]))
    for h in range(2):
        fills.append(("b", [(b_shared[:, 4 * h + t, :], t * P, P) for t in range(4)],
                      RANK, BANK, [part[:, h * BANK:(h + 1) * BANK] for part in bsT]))
    A_FILLS = HID_TILES + 1
    AX = [[(bank, 0, NR // 2), (bank + 1, NR // 2, NR // 2 + RANK)] for bank in (6, 0)]
    FILL_BANKS = (2, 3, 4, 5)
    EARLY_FILLS = len(FILL_BANKS)
    LATE_SPLITS = ([("adapter", n) for n in range(EARLY_FILLS, len(fills) - HID_TILES // 2)]
                   + [step for n in range(HID_TILES // 2)
                      for step in (("adapter", len(fills) - HID_TILES // 2 + n), ("kernel", n))]
                   + [("kernel", n) for n in range(HID_TILES // 2, HID_TILES)])

    def fill_bank(n):
        return FILL_BANKS[n % len(FILL_BANKS)]

    def halves(t):
        return slice(t * P, (t + 1) * P)

    with nc.Block() as block:
        @block.sync
        def _(eng):
            for b in range(LORA_BATCH):
                t, at = b * ROWS_PER_GATE // P, b * ROWS_PER_GATE % P
                eng.dma_start(gates[at:at + ROWS_PER_GATE, t, :],
                              a["gate"][b:b + 1, :].broadcast_to([ROWS_PER_GATE, LORAS])).then_inc(s_small, 16)
            eng.dma_start(bias[:, :], a["bias"].rearrange("(o n) -> o n", o=1).broadcast_to([P, HID])).then_inc(s_small, 16)
            for h in range(2):
                eng.wait_ge(s_t, (A_FILLS, len(fills))[h])
                eng.dma_start(raw[h][:, :, :], a["kernel"].rearrange("(k p) n -> p k n", p=P)[:, :, h * BANK:(h + 1) * BANK]).then_inc(s_w[h], 16)
            for h in range(2):
                for t in range(ROW_TILES):
                    eng.wait_ge(s_sum, ROW_TILES * h + t + 1)
                    eng.dma_start(out[0, t * P:(t + 1) * P, h * BANK:(h + 1) * BANK],
                                  normed[:, t, h * BANK:(h + 1) * BANK]).then_inc(s_out, 16)
            eng.wait_ge(s_out, 32 * ROW_TILES)

        @block.gpsimd
        def _(eng):
            layer_norm_pool(eng, core, mv, s_var, s_rstd, (1,))
            eng.wait_ge(s_small, 16 * (LORA_BATCH + 1))
            eng.wait_ge(s_ln, 8)
            for t in range(ROW_TILES):
                eng.tensor_tensor(core.x[:, t, :], core.x[:, t, :], bias[:, :], ALU.add).then_inc(s_xb, 1)

        @block.tensor
        def _(eng):
            def turn_adapter(n):
                which, moves, parts, width, dest = fills[n]
                if n == 0:
                    eng.wait_ge(s_a, 32)
                if n == A_FILLS:
                    eng.wait_ge(s_b, 16 * (HID_TILES + 1))
                wait(eng, s_lo, n - len(FILL_BANKS) + 1)
                for src, at, cols in moves:
                    rows = RANK if src.shape[0] == RANK else P
                    mm = eng.transpose(ps[0:parts, fill_bank(n), at:at + (cols if parts == P else P)], src,
                                       core.ident[0:rows, 0:rows])
                mm.then_inc(s_t, 1)

            def turn_rows(t):
                eng.wait_ge(s_ln, 4 * (t + 1))
                wait(eng, s_xlo, t)
                for k in range(HID_TILES):
                    mm = eng.transpose(ps[:, k // 4, (k % 4) * P:(k % 4 + 1) * P],
                                       normed[:, t, halves(k)], core.ident[:, :])
                mm.then_inc(s_xt, 1)

            turn_rows(0)
            for n in range(EARLY_FILLS):
                turn_adapter(n)
            turn_rows(1)
            for t in range(ROW_TILES):
                eng.wait_ge(s_xlo, t + 1)
                for k in range(HID_TILES):
                    if EARLY_FILLS + HID_TILES * t + k < len(fills):
                        turn_adapter(EARLY_FILLS + HID_TILES * t + k)
                    if t == 0:
                        eng.wait_ge(s_lo, k + 2)
                    for n, (s, m) in enumerate(PASSES):
                        for bank, at, cols in AX[t]:
                            mm = eng.matmul(ps[:, bank, 0:cols], xT[s][:, k, halves(t)], aT[m][:, k, at:at + cols],
                                            start=(k == 0 and n == 0), stop=(k == HID_TILES - 1 and n == 2))
                mm.then_inc(s_ax, 1)
            eng.wait_ge(s_lo, len(fills))

            def base(h):
                for k in range(HID_TILES):
                    eng.wait_ge(s_wlo, HID_TILES * h + k + 1)
                    for t in range(ROW_TILES):
                        for n, (s, m) in enumerate(PASSES):
                            mm = eng.matmul(ps[:, 2 + 2 * t + h, :], xT[s][:, k, halves(t)], w_part[m][:, k, :],
                                            start=(k == 0 and n == 0), stop=False)
                    mm.then_inc(s_mm, 1)

            def delta(h):
                for t in range(ROW_TILES):
                    for k in range(A_TILES):
                        for s, m in PASSES:
                            eng.matmul(ps[:, 2 + 2 * t + h, :], zT[s][:, t, halves(k)],
                                       bT[m][:, k, h * BANK:(h + 1) * BANK], start=False, stop=False)
                    for n, (s, m) in enumerate(PASSES):
                        mm = eng.matmul(ps[:, 2 + 2 * t + h, :], zsT[s][:, halves(t)],
                                        bsT[m][:, h * BANK:(h + 1) * BANK], start=False, stop=(n == 2))
                    mm.then_inc(s_done, 1)

            base(0)
            eng.wait_ge(s_z, 3 * ROW_TILES)
            for t in range(ROW_TILES):
                for k in range(A_TILES):
                    eng.transpose(ps[:, 6 + t, halves(k)], z[:, t, halves(k)], core.ident[:, :])
            for t in range(ROW_TILES):
                mm = eng.transpose(ps[0:RANK, 0, halves(t)], z[:, t, NR:NR + RANK], core.ident[:, :])
            mm.then_inc(s_zt, 1)
            base(1)
            eng.wait_ge(s_zlo, 2)
            delta(0)
            delta(1)

        @block.scalar
        def _(eng):
            def high_adapter(n):
                which, moves, parts, width, dest = fills[n]
                eng.wait_ge(s_t, n + 1)
                eng.activation(dest[0], ps[0:parts, fill_bank(n), 0:width], ACT.Copy).then_inc(s_hi, 1)

            def high_rows(t):
                eng.wait_ge(s_xt, t + 1)
                eng.activation(xT[0][:, :, halves(t)],
                               ps[:, 0:2, :].rearrange("p b (k n) -> p (b k) n", n=P),
                               ACT.Copy).then_inc(s_xhi, 1)

            def high_kernel(h, k):
                if k == 0:
                    eng.wait_ge(s_w[h], 16)
                if h == 1:
                    eng.wait_ge(s_mm, k + 1)
                eng.activation(w_part[0][:, k, :], raw[h][:, k, :], ACT.Copy).then_inc(s_whi, 1)

            high_rows(0)
            for n in range(EARLY_FILLS):
                high_adapter(n)
            high_rows(1)
            for what, n in LATE_SPLITS:
                if what == "adapter":
                    high_adapter(n)
                else:
                    high_kernel(0, n)
            for k in range(HID_TILES):
                high_kernel(1, k)
            eng.wait_ge(s_zt, 1)
            eng.activation(zT[0][:, :, :], ps[:, 6:8, :], ACT.Copy).then_inc(s_zhi, 1)
            eng.activation(zsT[0][:, :], ps[0:RANK, 0, 0:ROWS], ACT.Copy).then_inc(s_zhi, 1)

        @block.vector
        def _(eng):
            def low_adapter(n):
                which, moves, parts, width, dest = fills[n]
                eng.wait_ge(s_hi, n + 1)
                eng.tensor_tensor(dest[1], ps[0:parts, fill_bank(n), 0:width], dest[0].bitcast(F32),
                                  ALU.subtract).then_inc(s_lo, 1)

            def low_rows(t):
                eng.wait_ge(s_xhi, t + 1)
                eng.tensor_tensor(xT[1][:, :, halves(t)],
                                  ps[:, 0:2, :].rearrange("p b (k n) -> p (b k) n", n=P),
                                  xT[0][:, :, halves(t)].bitcast(F32), ALU.subtract).then_inc(s_xlo, 1)

            def low_kernel(h, k):
                eng.wait_ge(s_whi, HID_TILES * h + k + 1)
                eng.tensor_tensor(w_part[1][:, k, :], raw[h][:, k, :], w_part[0][:, k, :].bitcast(F32),
                                  ALU.subtract).then_inc(s_wlo, 1)

            layer_norm_tile(eng, core.x, normed, stats, mv, 1, s_ln, s_var, s_rstd)
            low_rows(0)
            for n in range(EARLY_FILLS):
                low_adapter(n)
            low_rows(1)
            for what, n in LATE_SPLITS:
                if what == "adapter":
                    low_adapter(n)
                else:
                    low_kernel(0, n)
            eng.wait_ge(s_small, 16 * (LORA_BATCH + 1))
            for t in range(ROW_TILES):
                eng.wait_ge(s_ax, t + 1)
                for n, (bank, at, cols) in enumerate(AX[t]):
                    eng.tensor_tensor(z[:, t, at:at + NR // 2].rearrange("p (n r) -> p n r", r=RANK),
                                      ps[:, bank, 0:NR // 2].rearrange("p (n r) -> p n r", r=RANK),
                                      over_last(gates[:, t, n * LORAS // 2:(n + 1) * LORAS // 2], (P, LORAS // 2, RANK)),
                                      ALU.mult).then_inc(s_z, 1)
                eng.tensor_copy(z[:, t, NR:NR + RANK], ps[:, AX[t][1][0], NR // 2:NR // 2 + RANK]).then_inc(s_z, 1)
            for k in range(HID_TILES):
                low_kernel(1, k)
            eng.wait_ge(s_zhi, 2)
            eng.tensor_tensor(zT[1][:, :, :], ps[:, 6:8, :], zT[0][:, :, :].bitcast(F32), ALU.subtract).then_inc(s_zlo, 1)
            eng.tensor_tensor(zsT[1][:, :], ps[0:RANK, 0, 0:ROWS], zsT[0][:, :].bitcast(F32),
                              ALU.subtract).then_inc(s_zlo, 1)
            eng.wait_ge(s_xb, ROW_TILES)
            for h in range(2):
                for t in range(ROW_TILES):
                    eng.wait_ge(s_done, ROW_TILES * h + t + 1)
                    eng.tensor_tensor(normed[:, t, h * BANK:(h + 1) * BANK], ps[:, 2 + 2 * t + h, :],
                                      core.x[:, t, h * BANK:(h + 1) * BANK], ALU.add).then_inc(s_sum, 1)


def perceiver_layer(nc, a, out):
    with ExitStack() as stack:
        core = Core(nc, stack)

        def scratch(name, shape):
            return nc.dram_tensor(name, shape, F32, kind="Internal").ap()

        q_scratch = scratch("q_scratch", (KV_HEADS, P, 2, GROUP, ROWS))
        k_scratch = scratch("k_scratch", (KV_HEADS, P, KEY_TILES, DIM))
        v_scratch = scratch("v_scratch", (KV_HEADS, P, KEY_TILES, DIM))
        o_scratch = scratch("o_scratch", (P, HEADS, 2, ROWS))
        with ExitStack() as place:
            shared = Shared(core, place)
        with ExitStack() as place:
            projection = Projection(core, a["Wo"], o_scratch, place)
        with ExitStack() as place:
            adapters = Adapters(core, place)
        with ExitStack() as own:
            project_inputs(core, a, own, shared, q_scratch, k_scratch, v_scratch)
        with ExitStack() as own:
            core.sbuf("place_of_shared", [P, SHARED_WORDS], stack=own)
            last_output = cross_attention(core, shared, projection, own, q_scratch, k_scratch, v_scratch, o_scratch)
        with ExitStack() as stack_of_self:
            buffers = SelfBuffers(core, stack_of_self)
            project_attention(core, a, shared, projection, buffers, *last_output)
            self_attention(core, a, buffers, adapters)
        with ExitStack() as own:
            core.sbuf("place_of_adapters", [P, ADAPTER_WORDS], stack=own)
            feed_forward(core, a, adapters, own, out)


_NAMES = {
    "x": "x", "ctx": "ctx_4096", "Wq": "L0_xattn_Wq", "Wk": "L0_xattn_Wk", "Wv": "L0_xattn_Wv",
    "Wo": "L0_xattn_Wo", "q_norm_w": "L0_xattn_q_norm_w", "k_norm_w": "L0_xattn_k_norm_w",
    "wq": "L0_attn_wq", "wk": "L0_attn_wk", "wv": "L0_attn_wv", "wo": "L0_attn_wo",
    "gate": "L0_ffn_gate", "kernel": "L0_ffn_kernel", "bias": "L0_ffn_bias", "lora_A": "L0_ffn_lora_A",
    "lora_B": "L0_ffn_lora_B", "lora_A_shared": "L0_ffn_lora_A_shared", "lora_B_shared": "L0_ffn_lora_B_shared",
}


def shape_constants():
    half = SELF_DIM // 2
    freqs = (1.0 / np.float32(10000.0) ** (np.arange(0, SELF_DIM, 2, dtype=np.float32) / np.float32(SELF_DIM))).astype(np.float32)
    angle = np.outer(np.arange(ROWS, dtype=np.float32), freqs).astype(np.float32)
    rope = np.stack([np.cos(angle), np.sin(angle)], axis=1).astype(np.float32)
    assert rope.shape == (ROWS, 2, half)
    return {
        "ident": np.eye(P, dtype=np.float32),
        "rope": rope,
        "mask": np.triu(np.full((P, P), NEGATIVE, np.float32), 1),
    }


def kernel(**inputs):
    import concourse.bacc as bacc
    from concourse.bass_utils import run_bass_kernel_spmd

    nc = bacc.Bacc("TRN2", target_bir_lowering=False, num_devices=1)
    given = {short: np.ascontiguousarray(inputs[name]) for short, name in _NAMES.items()} | shape_constants()
    arrays, aps = {}, {}
    for short, array in given.items():
        arrays[f"in_{short}"] = array
        aps[short] = nc.dram_tensor(f"in_{short}", array.shape, mybir.dt.from_np(array.dtype), kind="ExternalInput").ap()
    out = nc.dram_tensor("out_x", (1, ROWS, HID), F32, kind="ExternalOutput").ap()
    perceiver_layer(nc, aps, out)
    result = run_bass_kernel_spmd(nc, [arrays], core_ids=[0])
    return result.results[0]["out_x"]
```
